# Optimizing a Trainium2 kernel written in Bass

```python
import numpy as np
import jax
import jax.numpy as jnp

def _softmax(x, axis=-1):
    return jax.nn.softmax(x, axis=axis)

def _gelu(x):
    return jax.nn.gelu(x, approximate=True)

def _silu(x):
    return jax.nn.silu(x)

def _sigmoid(x):
    return jax.nn.sigmoid(x)

def _layernorm(x, axis=-1, eps=1e-05):
    m = jnp.mean(x, axis=axis, keepdims=True)
    v = jnp.var(x, axis=axis, keepdims=True)
    return (x - m) / jnp.sqrt(v + eps)

def _scatter_add(tgt, idx, src, axis=0):
    return tgt.at[idx].add(src)

def _segment_sum(src, seg, n):
    return jax.ops.segment_sum(src, seg, n)
kernel_name = 'mk_gps_d1_gnn_r8_51a154'

def setup_inputs(seed: int=0):
    np.random.seed(seed)
    _w = jnp.asarray

    def _rec_inputs():
        import jax
        import jax.numpy as jnp
        _gk = jax.random.key(seed)
        x = -7.329e-05 + 0.9999 * jax.random.normal(jax.random.fold_in(_gk, 1), (1250, 512), jnp.float32)
        src = jax.random.randint(jax.random.fold_in(_gk, 2), (20000,), 0, 1250, jnp.int32)
        dst = jnp.minimum((1250 * jax.random.uniform(jax.random.fold_in(_gk, 3), (20000,)) ** 2.0).astype(jnp.int32), 9999)
        _o = jnp.argsort(dst, stable=True)
        src = src[_o]
        dst = dst[_o]
        edge_weight = jax.random.uniform(jax.random.fold_in(_gk, 12), (20000,), jnp.float32, 0.0, 0.999999)
        return (x, src, dst, edge_weight)
    x, src, dst, edge_weight = _rec_inputs()

    def _L0_gnn_setup():
        import jax, jax.numpy as jnp
        import numpy as np
        N_NODES = 12500
        N_EDGES = 400000
        IN_F = 512
        OUT_F = 512
        RANK = 64
        key = jax.random.key(seed)
        ks = jax.random.split(key, 8)
        inp = jax.random.normal(ks[0], (N_NODES, IN_F), dtype=jnp.float32)
        U = jax.random.normal(ks[1], (IN_F, RANK), dtype=jnp.float32) / np.sqrt(IN_F)
        s = jax.random.uniform(ks[2], (RANK,), dtype=jnp.float32)
        Vt = jax.random.normal(ks[3], (RANK, OUT_F), dtype=jnp.float32) / np.sqrt(RANK)
        bias = jax.random.normal(ks[4], (OUT_F,), dtype=jnp.float32) * 0.01
        edge_row = jax.random.randint(ks[5], (N_EDGES,), 0, N_NODES, dtype=jnp.int64 if jax.config.jax_enable_x64 else jnp.int32)
        edge_col = jax.random.randint(ks[6], (N_EDGES,), 0, N_NODES, dtype=jnp.int64 if jax.config.jax_enable_x64 else jnp.int32)
        edge_val = jax.random.uniform(ks[7], (N_EDGES,), dtype=jnp.float32)
        return {'input': inp, 'U': U, 's': s, 'Vt': Vt, 'bias': bias, 'edge_row': edge_row, 'edge_col': edge_col, 'edge_val': edge_val}
    _L0_gnn_all = _L0_gnn_setup()
    _L0_gnn_in = {k: v for k, v in _L0_gnn_all.items() if k in ('U', 's', 'Vt', 'bias')}
    del _L0_gnn_all

    def _L0_mix_setup():
        import jax, jax.numpy as jnp
        import numpy as np
        HEADS = 8
        DIM_HEAD = 64
        key = jax.random.key(seed)
        k1, k2, k3 = jax.random.split(key, 3)
        B, L, D = (8, 512, 512)
        hidden = HEADS * DIM_HEAD
        x = jax.random.normal(k1, (B, L, D), dtype=jnp.float32)
        Wqkv = jax.random.normal(k2, (3 * hidden, D), dtype=jnp.float32) * (1.0 / np.sqrt(D))
        Wout = jax.random.normal(k3, (D, hidden), dtype=jnp.float32) * (1.0 / np.sqrt(hidden))
        bout = jnp.zeros((D,), dtype=jnp.float32)
        return {'x': x, 'Wqkv': Wqkv, 'Wout': Wout, 'bout': bout}
    _L0_mix_all = _L0_mix_setup()
    _L0_mix_in = {k: v for k, v in _L0_mix_all.items() if k in ('Wqkv', 'Wout', 'bout')}
    del _L0_mix_all

    def _L0_ffn_setup():
        import jax, jax.numpy as jnp
        import numpy as np
        D, E, DR, K, DFF, DSH = (512, 64, 64, 2, 256, 1024)
        TEMP = 0.7
        SHARED_SCALE = 0.25
        EPS = 1e-05

        def _ln(x, g, b):
            m = jnp.mean(x, axis=-1, keepdims=True)
            v = jnp.mean(jnp.square(x - m), axis=-1, keepdims=True)
            return (x - m) * jax.lax.rsqrt(v + EPS) * g + b
        key = jax.random.key(seed)
        ks = jax.random.split(key, 16)
        s = 0.02
        return {'x': jax.random.normal(ks[0], (1, 512, D), dtype=jnp.float32), 'ln1_g': jnp.ones((D,), jnp.float32), 'ln1_b': jnp.zeros((D,), jnp.float32), 'Wr': jax.random.normal(ks[1], (D, DR), jnp.float32) * s, 'codebook': jax.random.normal(ks[2], (E, DR), jnp.float32), 'W1': jax.random.normal(ks[3], (E, D, DFF), jnp.float32) * s, 'b1': jnp.zeros((E, DFF), jnp.float32), 'W2': jax.random.normal(ks[4], (E, DFF, D), jnp.float32) * s, 'b2': jnp.zeros((E, D), jnp.float32), 'Ws1': jax.random.normal(ks[5], (D, DSH), jnp.float32) * s, 'bs1': jnp.zeros((DSH,), jnp.float32), 'Ws2': jax.random.normal(ks[6], (DSH, D), jnp.float32) * s, 'bs2': jnp.zeros((D,), jnp.float32), 'ffln_g': jnp.ones((D,), jnp.float32), 'ffln_b': jnp.zeros((D,), jnp.float32), 'Wf1': jax.random.normal(ks[7], (D, DFF), jnp.float32) * s, 'bf1': jnp.zeros((DFF,), jnp.float32), 'Wf2': jax.random.normal(ks[8], (DFF, D), jnp.float32) * s, 'bf2': jnp.zeros((D,), jnp.float32)}
    _L0_ffn_all = _L0_ffn_setup()
    _L0_ffn_in = {k: v for k, v in _L0_ffn_all.items() if k in ('ln1_g', 'ln1_b', 'Wr', 'codebook', 'W1', 'b1', 'W2', 'b2', 'Ws1', 'bs1', 'Ws2', 'bs2', 'ffln_g', 'ffln_b', 'Wf1', 'bf1', 'Wf2', 'bf2')}
    del _L0_ffn_all
    return {'x': x, 'src': src, 'dst': dst, 'edge_weight': edge_weight, 'L0_gnn_U': _L0_gnn_in['U'], 'L0_gnn_s': _L0_gnn_in['s'], 'L0_gnn_Vt': _L0_gnn_in['Vt'], 'L0_gnn_bias': _L0_gnn_in['bias'], 'L0_mix_Wqkv': _L0_mix_in['Wqkv'], 'L0_mix_Wout': _L0_mix_in['Wout'], 'L0_mix_bout': _L0_mix_in['bout'], 'L0_ffn_ln1_g': _L0_ffn_in['ln1_g'], 'L0_ffn_ln1_b': _L0_ffn_in['ln1_b'], 'L0_ffn_Wr': _L0_ffn_in['Wr'], 'L0_ffn_codebook': _L0_ffn_in['codebook'], 'L0_ffn_W1': _L0_ffn_in['W1'], 'L0_ffn_b1': _L0_ffn_in['b1'], 'L0_ffn_W2': _L0_ffn_in['W2'], 'L0_ffn_b2': _L0_ffn_in['b2'], 'L0_ffn_Ws1': _L0_ffn_in['Ws1'], 'L0_ffn_bs1': _L0_ffn_in['bs1'], 'L0_ffn_Ws2': _L0_ffn_in['Ws2'], 'L0_ffn_bs2': _L0_ffn_in['bs2'], 'L0_ffn_ffln_g': _L0_ffn_in['ffln_g'], 'L0_ffn_ffln_b': _L0_ffn_in['ffln_b'], 'L0_ffn_Wf1': _L0_ffn_in['Wf1'], 'L0_ffn_bf1': _L0_ffn_in['bf1'], 'L0_ffn_Wf2': _L0_ffn_in['Wf2'], 'L0_ffn_bf2': _L0_ffn_in['bf2']}

def reference(x, src, dst, edge_weight, L0_gnn_U, L0_gnn_s, L0_gnn_Vt, L0_gnn_bias, L0_mix_Wqkv, L0_mix_Wout, L0_mix_bout, L0_ffn_ln1_g, L0_ffn_ln1_b, L0_ffn_Wr, L0_ffn_codebook, L0_ffn_W1, L0_ffn_b1, L0_ffn_W2, L0_ffn_b2, L0_ffn_Ws1, L0_ffn_bs1, L0_ffn_Ws2, L0_ffn_bs2, L0_ffn_ffln_g, L0_ffn_ffln_b, L0_ffn_Wf1, L0_ffn_bf1, L0_ffn_Wf2, L0_ffn_bf2):
    import jax
    import jax.numpy as jnp

    def _L0_gnn_ref(input, U, s, Vt, bias, edge_row, edge_col, edge_val):
        import jax, jax.numpy as jnp
        import numpy as np
        N_NODES = 12500
        N_EDGES = 400000
        IN_F = 512
        OUT_F = 512
        RANK = 64
        support = input @ U * s
        support = support @ Vt
        gathered = support[edge_col] * edge_val[:, None]
        output = jax.ops.segment_sum(gathered, edge_row, num_segments=input.shape[0])
        output = output + bias
        return jax.nn.relu(output)

    def _L0_mix_ref(x, Wqkv, Wout, bout):
        import jax, jax.numpy as jnp
        import numpy as np
        HEADS = 8
        DIM_HEAD = 64
        B, L, D = x.shape
        H, C = (HEADS, DIM_HEAD)
        qkv = jnp.einsum('bld,od->bol', x, Wqkv)
        qkv = qkv.reshape(B, 3, H, C, L)
        q, k, v = (qkv[:, 0], qkv[:, 1], qkv[:, 2])
        k = jax.nn.softmax(k, axis=-1)
        q = jax.nn.softmax(q, axis=-2)
        context = jnp.einsum('bhdn,bhen->bhde', k, v)
        out = jnp.einsum('bhde,bhdn->bhen', context, q)
        out = out.reshape(B, H * C, L)
        y = jnp.einsum('bcl,dc->bld', out, Wout) + bout
        return y

    def _L0_ffn_ref(x, ln1_g, ln1_b, Wr, codebook, W1, b1, W2, b2, Ws1, bs1, Ws2, bs2, ffln_g, ffln_b, Wf1, bf1, Wf2, bf2):
        import jax, jax.numpy as jnp
        import numpy as np
        D, E, DR, K, DFF, DSH = (512, 64, 64, 2, 256, 1024)
        TEMP = 0.7
        SHARED_SCALE = 0.25
        EPS = 1e-05

        def _ln(x, g, b):
            m = jnp.mean(x, axis=-1, keepdims=True)
            v = jnp.mean(jnp.square(x - m), axis=-1, keepdims=True)
            return (x - m) * jax.lax.rsqrt(v + EPS) * g + b
        B, S, _ = x.shape
        T = B * S
        h = _ln(x, ln1_g, ln1_b).reshape(T, D)
        r = h @ Wr
        logits = r @ codebook.T / TEMP
        probs = jax.nn.softmax(logits, axis=-1)
        vals, idx = jax.lax.top_k(probs, K)
        w = vals / jnp.sum(vals, axis=-1, keepdims=True)
        combine = jnp.zeros((T, E), x.dtype).at[jnp.arange(T)[:, None], idx].set(w)
        eh = jax.nn.silu(jnp.einsum('td,edf->tef', h, W1) + b1)
        eo = jnp.einsum('tef,efd->ted', eh, W2) + b2
        moe = jnp.einsum('te,ted->td', combine, eo)
        shared = (jax.nn.silu(h @ Ws1 + bs1) @ Ws2 + bs2) * SHARED_SCALE
        hmoe = (moe + shared).reshape(B, S, D)
        f = _ln(hmoe, ffln_g, ffln_b)
        f = jax.nn.silu(f @ Wf1 + bf1) @ Wf2 + bf2
        return x + hmoe + f
    xn = _layernorm(x, axis=-1)
    x = x + _L0_gnn_ref(xn, L0_gnn_U, L0_gnn_s, L0_gnn_Vt, L0_gnn_bias, src, dst, edge_weight) + _L0_mix_ref(xn[None], L0_mix_Wqkv, L0_mix_Wout, L0_mix_bout)[0]
    x = x + _L0_ffn_ref(_layernorm(x, axis=-1)[None], L0_ffn_ln1_g, L0_ffn_ln1_b, L0_ffn_Wr, L0_ffn_codebook, L0_ffn_W1, L0_ffn_b1, L0_ffn_W2, L0_ffn_b2, L0_ffn_Ws1, L0_ffn_bs1, L0_ffn_Ws2, L0_ffn_bs2, L0_ffn_ffln_g, L0_ffn_ffln_b, L0_ffn_Wf1, L0_ffn_bf1, L0_ffn_Wf2, L0_ffn_bf2)[0]
    return x

_drawn_inputs = setup_inputs


def setup_inputs(seed=0):
    import zlib

    import numpy as np

    out = dict(_drawn_inputs(seed))
    spreads = {'L0_mix_bout': (0.0, 0.1),
     'L0_ffn_ln1_g': (1.0, 0.559),
     'L0_ffn_ln1_b': (0.0, 0.449),
     'L0_ffn_b1': (0.0, 0.8),
     'L0_ffn_b2': (0.0, 0.1),
     'L0_ffn_bs1': (0.0, 0.8),
     'L0_ffn_bs2': (0.0, 0.601),
     'L0_ffn_ffln_g': (1.0, 0.6),
     'L0_ffn_ffln_b': (0.0, 0.8),
     'L0_ffn_bf1': (0.0, 0.8),
     'L0_ffn_bf2': (0.0, 0.1)}
    factors = {'L0_gnn_bias': 8.0, 'L0_ffn_Ws1': 2.825, 'L0_ffn_Ws2': 2.713}
    for name, (base, spread) in spreads.items():
        noise = np.random.default_rng([zlib.crc32(name.encode()), seed]).standard_normal(out[name].shape)
        drawn = base * np.exp(spread * noise) if base else spread * noise
        out[name] = jnp.asarray(drawn.astype(out[name].dtype))
    for name, factor in factors.items():
        out[name] = (out[name] * factor).astype(out[name].dtype)
    return out
```

```python
from contextlib import contextmanager

import concourse.bass as bass
from concourse import mybir

F32 = mybir.dt.float32
F16 = mybir.dt.float16
BF16 = mybir.dt.bfloat16
F32R = mybir.dt.float32r
I32 = mybir.dt.int32
U32 = mybir.dt.uint32
ALU = mybir.AluOpType
ACT = mybir.ActivationFunctionType
AX = mybir.AxisListType

N = 1250
D = 512
E_EDGES = 20000
P = 125
NT = N // P
PW = P + 1
KD = D // 128
RANK = 64
HEADS = 8
PAIRS = HEADS // 2
EC = E_EDGES // P
BC = 8
OH_RING = 4
BANK = 512
EPS = 1e-5

NE = 64
DR = 64
DFF = 256
DSH = 1024
SB = DSH // 128
TEMP = 0.7
SHARED_SCALE = 0.25
SLOTS = 64
TILES = (2 * N + (SLOTS - 1) * NE) // SLOTS
GROUPS = [(0, 4), (4, 7), (7, 10)]

PAIR_TILES = TILES // 2
W_RING = 6
STEPS = TILES // W_RING

SPLIT = {"u": 1, "wqkv": 1 + KD, "wout": 2 + KD, "vt": 3 + KD, "wr": 4 + KD, "ws1": 5 + KD, "ws2": 6 + KD, "wf1": 7 + KD,
         "wf2": 8 + KD}
MADE_NODES, MADE_FILLS, MADE_IDENT, MADE_BEFORE, MADE_IDS, MADE_ZEROS = 1, 6, 7, 8, 12, 13
MADE_NODE_COLS, MADE_EXPERT_IDS, MADE_EDGES = 1, 3, 6

AHEAD = 2
CHUNK_AHEAD = 32


def done(n):
    return n + 1 + AHEAD


def freed(n, ring=2):
    return n + 1 + AHEAD - ring


def tile_done(j):
    return j + 1 + W_RING


def tile_freed(j, ring):
    return j + 1 + W_RING - ring


class Steps:

    def __init__(self):
        self.n, self.turns = 0, 0

    def one(self):
        self.n += 1
        return 1

    def now(self):
        return self.n + self.turns

    @contextmanager
    def loop(self, it, count, each):
        start, self.turns = self.n, it * each
        yield
        assert self.n == start + each, self.n - start
        self.n, self.turns = start + each * count, 0


class Region:

    def __init__(self, nc, start, end):
        self.nc, self.at, self.end = nc, start, end

    def place(self, name, shape, dtype=F32):
        size = mybir.dt.size(dtype)
        for n in shape[1:]:
            size *= n
        tensor = self.nc.alloc_sbuf_tensor_at(name, shape, dtype, offset=self.at)
        self.at += (size + 31) // 32 * 32
        assert self.at <= self.end, (name, self.at, self.end)
        return tensor


def gps_layer(nc, x, src, dst, edge_weight, u, s, vt, gnn_bias, wqkv_t, wout_t, bout, ln1_g, ln1_b, wr, codebook_t,
              experts, b2, ws1, bs1_cols, ws2, bs2, ffln_g_cols, ffln_b_cols, wf1, bf1_cols, wf2, bf2, out):
    base = (nc.sbuf_base + 31) // 32 * 32
    top = nc.sbuf_usable_end // 32 * 32

    keep = Region(nc, base, top)
    x_sb = keep.place("x_sb", [P, NT, D])
    ident = keep.place("ident", [128, 128])
    before = keep.place("before", [P, P], BF16)
    ones = keep.place("ones", [P, P], BF16)
    zero_w = keep.place("zero_w", [P, 128], F32R)
    eps_col = keep.place("eps_col", [P, 1])
    stats = keep.place("stats", [P, NT, 6])
    moments = keep.place("moments", [P, NT, 2])
    std = keep.place("std", [P, NT])
    rstd = keep.place("rstd", [P, NT])
    logits = keep.place("logits", [P, NT, NE])
    top_logit = keep.place("top_logit", [P, NT, 8])
    top_expert = keep.place("top_expert", [P, NT, 8], U32)
    expert_id = keep.place("expert_id", [P, NE])
    expert_i32 = keep.place("expert_i32", [P, NE], I32)
    tile_start_i32 = keep.place("tile_start_i32", [P, 1], I32)
    tile_start = keep.place("tile_start", [P, 1])
    token_id = keep.place("token_id", [P, NT], I32)
    picks = keep.place("picks", [P, NT, 2])
    gap = keep.place("gap", [P, NT])
    gate1 = keep.place("gate1", [P, NT])
    gate2 = keep.place("gate2", [P, NT])
    slots_f = keep.place("slots_f", [P, 2, NT])
    slots = keep.place("slots", [P, 2, NT], I32)
    slot_low = keep.place("slot_low", [P, 2, NT], I32)
    slot_high = keep.place("slot_high", [P, 2, NT], I32)
    table_at = keep.place("table_at", [P, 2, NT], I32)
    padded_i32 = keep.place("padded_i32", [P, NE], I32)
    padded = keep.place("padded", [P, NE])
    scan = [keep.place(f"scan{i}", [P, NE]) for i in range(2)]
    starts = keep.place("starts", [P, NE])
    tile_expert_f = keep.place("tile_expert_f", [P, 1])
    tile_expert = keep.place("tile_expert", [P, 1], I32)
    tile_expert_row = keep.place("tile_expert_row", [1, P], I32)
    slot_token = keep.place("slot_token", [128, PAIR_TILES], I32)
    no_token = keep.place("no_token", [128, PAIR_TILES], I32)
    bs1_sb = keep.place("bs1_sb", [128, SB])
    mid = Region(nc, keep.at, top)
    q_sb = mid.place("q_sb", [P, NT, D])
    agg_sb = mid.place("agg_sb", [128, NT, PW])
    kv = Region(nc, mid.at, top)
    k_sb = kv.place("k_sb", [P, NT, D])
    v_sb = kv.place("v_sb", [P, NT, PAIRS, 130])
    kv_start, kv_end = mid.at, kv.at
    wqkv_raw = Region(nc, kv_start, kv_end).place("wqkv_raw", [128, KD, 3 * D])
    pe_ = Region(nc, kv_end, top)
    wqkv_hi = pe_.place("wqkv_hi", [128, KD, 3 * D], F32R)
    wqkv_lo = pe_.place("wqkv_lo", [128, KD, 3 * D], F32R)
    u_raw = pe_.place("u_raw", [128, KD, RANK])
    u_hl = pe_.place("u_hl", [128, KD, 2 * RANK], F32R)
    s_row = pe_.place("s_row", [P, RANK])
    t_sb = pe_.place("t_sb", [P, NT, RANK])
    xn = [pe_.place(f"xn{i}", [P, D]) for i in range(2)]
    xnt_hi = [pe_.place(f"xnt_hi{i}", [128, KD, PW], F32R) for i in range(2)]
    xnt_lo = [pe_.place(f"xnt_lo{i}", [128, KD, PW], F32R) for i in range(2)]
    node_of_col = pe_.place("node_of_col", [P, NT, PW], F16)
    node_i32 = nc.alloc_sbuf_tensor_at("node_i32", [P, NT, PW], I32, offset=pe_.at)
    onehot = [pe_.place(f"onehot{i}", [P, NT * PW], F32R) for i in range(OH_RING)]
    rows = [pe_.place(f"rows{i}", [P, BC, RANK]) for i in range(2)]
    rows_hl = [pe_.place(f"rows_hl{i}", [P, BC, 2 * RANK], F32R) for i in range(2)]
    q_exp = [pe_.place(f"q_exp{i}", [P, D]) for i in range(2)]
    q_top = pe_.place("q_top", [P, HEADS])
    q_sum = pe_.place("q_sum", [P, HEADS])
    q_inv = pe_.place("q_inv", [P, HEADS])
    k_top = pe_.place("k_top", [P, D])
    dst_sb = pe_.place("dst_sb", [P, EC], I32)
    src_sb = pe_.place("src_sb", [P, EC], I32)
    src_f = pe_.place("src_f", [P, EC])
    weight_sb = pe_.place("weight_sb", [P, EC])
    batch_dst = [pe_.place(f"batch_dst{i}", [P, BC], I32) for i in range(2)]
    late = Region(nc, kv_end, top)
    hT_hi = late.place("hT_hi", [128, KD, NT, PW], F32R)
    hT_lo = late.place("hT_lo", [128, KD, NT, PW], F32R)
    after_hT = late.at
    vt2_raw = late.place("vt2_raw", [128, D])
    vt2_hi = late.place("vt2_hi", [128, D], F32R)
    vt2_lo = late.place("vt2_lo", [128, D], F32R)
    bias_row = late.place("bias_row", [P, D])
    bout_row = late.place("bout_row", [P, D])
    g_row = late.place("g_row", [P, D])
    b_row = late.place("b_row", [P, D])
    wr_raw = late.place("wr_raw", [128, KD, DR])
    wr_hl = late.place("wr_hl", [128, KD, 2 * DR], F32R)
    codebook2 = late.place("codebook2", [128, NE])
    wout_raw = late.place("wout_raw", [128, PAIRS, D])
    wout_hi = late.place("wout_hi", [128, PAIRS, D], F32R)
    wout_lo = late.place("wout_lo", [128, PAIRS, D], F32R)
    m_hi = late.place("m_hi", [128, PAIRS, D], F32R)
    m_lo = late.place("m_lo", [128, PAIRS, D], F32R)
    ctx = late.place("ctx", [128, PAIRS, 128])
    ctxT_hi = late.place("ctxT_hi", [128, PAIRS, 128], F32R)
    ctxT_lo = late.place("ctxT_lo", [128, PAIRS, 128], F32R)
    k_inv = late.place("k_inv", [128, PAIRS])
    k_top_col = late.place("k_top_col", [128, PAIRS])
    k_top_wide = late.place("k_top_wide", [128, PAIRS, P])
    upd = Region(nc, kv_start, kv_end)
    q_tile = [upd.place(f"q_tile{i}", [P, D]) for i in range(2)]
    qT_hi = [upd.place(f"qT_hi{i}", [128, PAIRS, PW], F32R) for i in range(2)]
    qT_lo = [upd.place(f"qT_lo{i}", [128, PAIRS, PW], F32R) for i in range(2)]
    agg_hi = [upd.place(f"agg_hi{i}", [128, PW], F32R) for i in range(2)]
    agg_lo = [upd.place(f"agg_lo{i}", [128, PW], F32R) for i in range(2)]
    mixed = [upd.place(f"mixed{i}", [P, D]) for i in range(2)]
    x1 = [upd.place(f"x1_{i}", [P, D]) for i in range(2)]
    z = [upd.place(f"z{i}", [P, D]) for i in range(2)]
    h_tile = [upd.place(f"h_tile{i}", [P, D]) for i in range(2)]
    rT = [upd.place(f"rT{i}", [128, PW]) for i in range(2)]
    x1_parts = [upd.place(f"x1_parts{i}", [P, 6]) for i in range(2)]
    x1_moments = [upd.place(f"x1_moments{i}", [P, 2]) for i in range(2)]
    x1_std = [upd.place(f"x1_std{i}", [P, 1]) for i in range(2)]
    x1_rstd = [upd.place(f"x1_rstd{i}", [P, 1]) for i in range(2)]
    z_var = [upd.place(f"z_var{i}", [P, 1]) for i in range(2)]
    z_std = [upd.place(f"z_std{i}", [P, 1]) for i in range(2)]
    z_rstd = [upd.place(f"z_rstd{i}", [P, 1]) for i in range(2)]

    zone1 = Region(nc, keep.at, kv_end)
    shared = zone1.place("shared", [P, NT, D])
    after_shared = zone1.at
    ws1_hi = zone1.place("ws1_hi", [128, KD, DSH], F32R)
    ws1_lo = zone1.place("ws1_lo", [128, KD, DSH], F32R)
    shared_h = [zone1.place(f"shared_h{i}", [128, 4 * PW]) for i in range(2)]
    bs2_row = zone1.place("bs2_row", [P, D])
    work = zone1.place("work", [P, NT, NE])
    zone2 = Region(nc, after_hT, top)
    ws2_hi = zone2.place("ws2_hi", [128, SB, D], F32R)
    ws2_lo = zone2.place("ws2_lo", [128, SB, D], F32R)
    ws1_raw = nc.alloc_sbuf_tensor_at("ws1_raw", [128, KD, DSH], F32, offset=zone2.at)
    ws2_raw = nc.alloc_sbuf_tensor_at("ws2_raw", [128, SB, D], F32, offset=zone2.at + 4 * KD * DSH)
    shared_hT_hi = zone2.place("shared_hT_hi", [128, SB, 4 * PW], F32R)
    shared_hT_lo = zone2.place("shared_hT_lo", [128, SB, 4 * PW], F32R)
    zone2.at += 512
    first_pick = zone2.place("first_pick", [P, NT, NE], BF16)
    second_pick = zone2.place("second_pick", [P, NT, NE], BF16)
    picked_any = zone2.place("picked_any", [P, NT, NE], BF16)
    earlier = zone2.place("earlier", [P, NT + 1, NE], BF16)
    slot_all = zone2.place("slot_all", [P, NT, NE])
    moe = Region(nc, after_shared, top)
    combineT = moe.place("combineT", [NE, NT, 128])
    b2_sb = moe.place("b2_sb", [NE, D])
    w_ring = [moe.place(f"w_ring{i}", [128, KD * DFF + 2 * D + 2]) for i in range(W_RING)]
    pair_idx = [moe.place(f"pair_idx{i}", [128, 1], I32) for i in range(3)]
    pair_rows = [moe.place(f"pair_rows{i}", [128, D]) for i in range(3)]
    pair_rowsT = [moe.place(f"pair_rowsT{i}", [128, KD, 128]) for i in range(3)]
    up = [moe.place(f"up{i}", [128, 128]) for i in range(2)]
    upT = [moe.place(f"upT{i}", [128, 2, SLOTS]) for i in range(2)]
    down = [moe.place(f"down{i}", [128, D // 2]) for i in range(2)]
    wf1_raw = moe.place("wf1_raw", [128, KD, DFF])
    wf1_hi = moe.place("wf1_hi", [128, KD, DFF], F32R)
    wf1_lo = moe.place("wf1_lo", [128, KD, DFF], F32R)
    wf1_g = moe.place("wf1_g", [128, KD, DFF])
    wf2_raw = moe.place("wf2_raw", [128, 2, D])
    wf2_hi = moe.place("wf2_hi", [128, 2, D], F32R)
    wf2_lo = moe.place("wf2_lo", [128, 2, D], F32R)
    g_col = moe.place("g_col", [128, KD])
    b_col = moe.place("b_col", [128, KD])
    bf1_raw = moe.place("bf1_raw", [128, 2])
    bf1_sb = moe.place("bf1_sb", [128, 2])
    bf2_row = moe.place("bf2_row", [P, D])
    last_ = Region(nc, moe.at, top)
    eo_first = [last_.place(f"eo_first{i}", [P, D]) for i in range(2)]
    eo_second = [last_.place(f"eo_second{i}", [P, D]) for i in range(2)]
    hmoe = [last_.place(f"hmoe{i}", [P, D]) for i in range(2)]
    ff_in = [last_.place(f"ff_in{i}", [P, D]) for i in range(2)]
    hm_parts = [last_.place(f"hm_parts{i}", [P, 6]) for i in range(2)]
    hm_moments = [last_.place(f"hm_moments{i}", [P, 2]) for i in range(2)]
    hm_std = [last_.place(f"hm_std{i}", [P, 1]) for i in range(2)]
    hm_rstd = [last_.place(f"hm_rstd{i}", [P, 1]) for i in range(2)]
    ffT_hi = last_.place("ffT_hi", [128, KD, 4, PW], F32R)
    ffT_lo = last_.place("ffT_lo", [128, KD, 4, PW], F32R)
    ff_h = [last_.place(f"ff_h{i}", [128, 4 * PW]) for i in range(2)]
    ff_hT_hi = last_.place("ff_hT_hi", [128, 2, 4 * PW], F32R)
    ff_hT_lo = last_.place("ff_hT_lo", [128, 2, 4 * PW], F32R)
    result = [last_.place(f"result{i}", [P, D]) for i in range(2)]

    bank = [nc.alloc_psum_tensor(f"bank{i}", [128, BANK], F32) for i in range(8)]

    t_rows = nc.dram_tensor("t_rows", (N, RANK), F32, kind="Internal").ap()
    h_rows = nc.dram_tensor("h_rows", (N, D), F32, kind="Internal").ap()

    slot_table = nc.dram_tensor("slot_table", (128 * PAIR_TILES, 1), I32, kind="Internal").ap()
    tile_expert_d = nc.dram_tensor("tile_expert_d", (P, 1), I32, kind="Internal").ap()
    expert_rows = nc.dram_tensor("expert_rows", (TILES * SLOTS, D), F32, kind="Internal").ap()

    def sem(name):
        return nc.alloc_semaphore(name)

    def sems(names):
        return [sem(n) for n in names.split()]

    x_loaded = [sem(f"x_loaded{i}") for i in range(NT // 2)]
    wqkv_loaded, edges_loaded = sems(
        "wqkv_loaded edges_loaded")
    moments_done, std_done = sems(
        "moments_done std_done")
    xn_done, xn_turned, xnt_hi_done, xnt_lo_done, t_mm, t_done = sems(
        "xn_done xn_turned xnt_hi_done xnt_lo_done t_mm t_done")
    t_stored, agg_opened, indices_done, chunk_mm, onehot_done = sems(
        "t_stored agg_opened indices_done chunk_mm onehot_done")
    gathered = [sem(f"gathered{i}") for i in range(2)]
    rows_scaled, rows_hi_done, rows_lo_done = sems("rows_scaled rows_hi_done rows_lo_done")
    q_mm, k_mm, v_mm, q_sub_done, q_exp_done = sems(
        "q_mm k_mm v_mm q_sub_done q_exp_done")
    k_top_done, k_copied, v_copied, agg_closed, agg_copied = sems("k_top_done k_copied v_copied agg_closed agg_copied")
    wout_loaded, = sems(
        "wout_loaded")
    k_top_turned, k_top_wide_done, k_top_back, k_sub_done, k_exp_done = sems(
        "k_top_turned k_top_wide_done k_top_back k_sub_done k_exp_done")
    ctx_mm, ctx_zeroed, ctx_done, ctx_turned, ctxT_hi_done, ctxT_lo_done = sems(
        "ctx_mm ctx_zeroed ctx_done ctx_turned ctxT_hi_done ctxT_lo_done")
    m_mm, m_hi_done, m_lo_done = sems(
        "m_mm m_hi_done m_lo_done")
    xb_done, q_tile_done, q_turned, qT_hi_done, qT_lo_done, agg_hi_done, agg_lo_done, g_mm, y_mm = sems(
        "xb_done q_tile_done q_turned qT_hi_done qT_lo_done agg_hi_done agg_lo_done g_mm y_mm")
    g_sum_done, y_sum_done, x1_done, x1_moments_done, x1_std_done, x1_rstd_done, z_var_done = sems(
        "g_sum_done y_sum_done x1_done x1_moments_done x1_std_done x1_rstd_done z_var_done")
    z_done, z_std_done, z_rstd_done = sems("z_done z_std_done z_rstd_done")
    res_done, h_done, h_turned, hT_hi_done, hT_lo_done, r_mm, rT_done, l_mm, logits_done, picked = sems(
        "res_done h_done h_turned hT_hi_done hT_lo_done r_mm rT_done l_mm logits_done picked")
    pads_zeroed = sem("pads_zeroed")
    gnn_loaded, update_loaded = sems("gnn_loaded update_loaded")
    pair_index_done, x1_parts_done = sems("pair_index_done x1_parts_done")
    made, made_dve, dve_step, halves_hi, halves_lo = sems("made made_dve dve_step halves_hi halves_lo")
    h_stored = [sem(f"h_stored{i}") for i in range(2)]
    ws1_loaded, ws2_loaded, table_cleared = sems(
        "ws1_loaded ws2_loaded table_cleared")
    earlier_done, gap_done = sems(
        "earlier_done gap_done")
    gap_exp, rank_mm, count_mm = sems(
        "gap_exp rank_mm count_mm")
    table_at_done, = sems(
        "table_at_done")
    tile_expert_done, tile_expert_stored, tile_expert_loaded, table_written, table_loaded = sems(
        "tile_expert_done tile_expert_stored tile_expert_loaded table_written table_loaded")
    shared_up, shared_act, shared_lo_done, shared_down, shared_done = sems(
        "shared_up shared_act shared_lo_done shared_down shared_done")
    combine_done, combine_turned, combineT_done, b2_mm, b2_added = sems(
        "combine_done combine_turned combineT_done b2_mm b2_added")
    ffw_loaded, wf1_g_done, bf1_mm, bf1_done = sems(
        "ffw_loaded wf1_g_done bf1_mm bf1_done")
    w_loaded = [sem(f"w_loaded{i}") for i in range(W_RING)]
    pair_fetched = [sem(f"pair_fetched{i}") for i in range(3)]
    pair_turned, pairT_done, up_mm, up_copied, up_turned, up_act, down_mm, down_copied = sems(
        "pair_turned pairT_done up_mm up_copied up_turned up_act down_mm down_copied")
    down_stored = [sem(f"down_stored{i}") for i in range(2)]
    eo_fetched = [sem(f"eo_fetched{i}") for i in range(2)]
    hm_done, hm_moments_done, hm_std_done, hm_rstd_done, ff_in_done, hm_kept, bf2_added = sems(
        "hm_done hm_moments_done hm_std_done hm_rstd_done ff_in_done hm_kept bf2_added")
    ff_turned, ffT_hi_done, ffT_lo_done, ff_up, ff_act, ff_h_lo_done, ff_down, result_done = sems(
        "ff_turned ffT_hi_done ffT_lo_done ff_up ff_act ff_h_lo_done ff_down result_done")
    result_stored = [sem(f"result_stored{i}") for i in range(2)]

    x_v = x.rearrange("(p t) d -> p t d", t=NT)
    out_v = out.rearrange("(p t) d -> p t d", t=NT)
    h_rows_v = h_rows.rearrange("(p t) d -> p t d", t=NT)
    WIDE = 112

    def load_tokens(eng, to, of, signal):
        eng.dma_start(to[0:WIDE], of[0:WIDE]).then_inc(signal, 16)
        eng.dma_start(to[WIDE:P], of[WIDE:P]).then_inc(signal, 16)

    def turned(b):
        return bank[b][:, 0:KD * PW].rearrange("p (k c) -> p k c", k=KD)

    block = nc.Block()
    block.__enter__()

    @block.sync
    def _(sp):
        for i in range(NT // 2):
            load_tokens(sp, x_sb[:, 2 * i:2 * i + 2, :], x_v[:, 2 * i:2 * i + 2, :], x_loaded[i])
        sp.dma_start(u_raw[:], u.rearrange("(k p) r -> p k r", p=128)).then_inc(gnn_loaded, 16)
        sp.dma_start(s_row[:], s.partition_broadcast(P)).then_inc(gnn_loaded, 16)
        sp.dma_start(wqkv_raw[:], wqkv_t.rearrange("(k p) c -> p k c", p=128)).then_inc(wqkv_loaded, 16)
        sp.dma_start(src_sb[:], src).then_inc(edges_loaded, 16)
        sp.dma_start(dst_sb[:], dst).then_inc(edges_loaded, 16)
        sp.dma_start(weight_sb[:], edge_weight).then_inc(edges_loaded, 16)
        sp.wait_ge(t_done, done(NT - 1))
        sp.dma_start(t_rows.rearrange("(p t) r -> p t r", t=NT), t_sb[:]).then_inc(t_stored, 16)
        sp.wait_ge(agg_closed, 1)
        sp.dma_start(wout_raw[:], wout_t.rearrange("(k p) c -> p k c", p=128)).then_inc(wout_loaded, 16)
        for i in range(2):
            sp.dma_start(vt2_raw[RANK * i:RANK * (i + 1)], vt).then_inc(update_loaded, 16)
        for to, of in ((bias_row, gnn_bias), (bout_row, bout), (g_row, ln1_g), (b_row, ln1_b)):
            sp.dma_start(to[:], of.partition_broadcast(P)).then_inc(update_loaded, 16)
        sp.dma_start(wr_raw[:], wr.rearrange("(k p) r -> p k r", p=128)).then_inc(update_loaded, 16)
        for i in range(2):
            sp.dma_start(codebook2[DR * i:DR * (i + 1)], codebook_t).then_inc(update_loaded, 16)
        with sp.Fori(0, NT // 2) as it:
            for par in range(2):
                t = 2 * it + par
                sp.wait_ge(h_done, done(t))
                sp.dma_start(h_rows_v[:, t, :], h_tile[par][:]).then_inc(h_stored[par], 16)
        for par in range(2):
            sp.wait_ge(h_stored[par], 16 * (NT // 2))
        sp.wait_ge(picked, NT)
        sp.wait_ge(l_mm, done(NT - 1))
        sp.dma_start(ws1_raw[:], ws1.rearrange("(k p) f -> p k f", p=128)).then_inc(ws1_loaded, 16)
        sp.dma_start(ws2_raw[:], ws2.rearrange("(k p) f -> p k f", p=128)).then_inc(ws2_loaded, 16)
        sp.dma_start(bs1_sb[:], bs1_cols).then_inc(ws2_loaded, 16)
        sp.dma_start(bs2_row[:], bs2.partition_broadcast(P)).then_inc(ws2_loaded, 16)
        sp.wait_ge(tile_expert_done, 1)
        sp.dma_start(tile_expert_d, tile_expert[:]).then_inc(tile_expert_stored, 16)
        sp.wait_ge(tile_expert_stored, 16)
        sp.dma_start(tile_expert_row[:], tile_expert_d.rearrange("p a -> a p")).then_inc(tile_expert_loaded, 16)
        sp.wait_ge(table_written, 16 * 2 * NT)
        sp.dma_start(slot_token[:], slot_table.rearrange("(p j) a -> p (j a)", p=128)).then_inc(table_loaded, 16)
        sp.wait_ge(shared_done, NT)
        sp.dma_start(b2_sb[:], b2).then_inc(ffw_loaded, 16)
        for to, of in ((wf1_raw, wf1.rearrange("(k p) f -> p k f", p=128)), (wf2_raw, wf2.rearrange("(k p) f -> p k f", p=128)),
                       (g_col, ffln_g_cols), (b_col, ffln_b_cols), (bf1_raw, bf1_cols), (bf2_row, bf2.partition_broadcast(P))):
            sp.dma_start(to[:], of).then_inc(ffw_loaded, 16)
        sp.wait_ge(tile_expert_loaded, 16)
        sp.wait_ge(combine_turned, NT)
        with sp.Fori(0, STEPS) as it:
            for n in range(W_RING):
                j = W_RING * it + n
                expert = sp.value_load(tile_expert_row[0:1, bass.ds(j, 1)], min_val=0, max_val=NE - 1)
                sp.wait_ge(down_mm, tile_freed(j, W_RING))
                sp.dma_start(w_ring[n][:], experts[bass.ds(expert, 1), :, :].rearrange("a p c -> p (a c)")).then_inc(w_loaded[n], 16)
        for t in range(NT):
            sp.wait_ge(result_done, t + 1)
            load_tokens(sp, out_v[:, t, :], result[t % 2], result_stored[t % 2])
        for par in range(2):
            sp.wait_ge(result_stored[par], 32 * (NT // 2))

    @block.gpsimd
    def _(pool):
        pool.sem_inc(res_done, AHEAD)
        pool.sem_inc(pair_index_done, 3)

        def keep_hm(t):
            pool.wait_ge(hm_done, t + 1)
            pool.wait_ge(bf2_added, t + 1)
            pool.tensor_tensor(x_sb[:, t, :], x_sb[:, t, :], hmoe[t % 2][:], ALU.add).then_inc(hm_kept, 1)

        pool.iota(node_i32[:], [[1, NT], [NT, PW]], base=0, channel_multiplier=0).then_inc(made, 1)
        pool.memset(ident[:], 0.0).then_inc(made, 1)
        pool.memset(before[:], 0.0).then_inc(made, 1)
        pool.memset(ones[:], 1.0).then_inc(made, 1)
        pool.memset(eps_col[:], EPS).then_inc(made, 1)
        pool.memset(zero_w[:].bitcast(F32), 0.0).then_inc(made, 1)
        pool.wait_ge(made, MADE_FILLS)
        pool.affine_select(out=ident[:], in_=ident[:], compare_op=ALU.not_equal, fill=1.0, base=0,
                           pattern=[[-1, 128]], channel_multiplier=1).then_inc(made, 1)
        pool.affine_select(out=before[:], in_=before[:], compare_op=ALU.is_ge, fill=1.0, base=0,
                           pattern=[[-1, P]], channel_multiplier=1).then_inc(made, 1)
        pool.iota(expert_i32[:], [[1, NE]], base=0, channel_multiplier=0).then_inc(made, 1)
        pool.iota(tile_start_i32[:], [[0, 1]], base=0, channel_multiplier=SLOTS).then_inc(made, 1)
        pool.iota(token_id[:], [[1, NT]], base=0, channel_multiplier=NT).then_inc(made, 1)
        pool.memset(no_token[:], 0).then_inc(made, 1)
        pool.wait_ge(made, MADE_IDS)
        pool.dma_start(slot_table.rearrange("(p j) a -> p (j a)", p=128), no_token[:]).then_inc(table_cleared, 16)
        pool.wait_ge(made_dve, MADE_NODE_COLS)
        pool.memset(onehot[0][:].bitcast(F32), 0.0).then_inc(made, 1)
        pool.wait_ge(edges_loaded, 48)
        with pool.Fori(0, NT // 2) as it:
            for step in range(4):
                half = step % 2
                batch = 4 * it + step
                pool.wait_ge(rows_lo_done, freed(batch))
                pool.tensor_copy(batch_dst[half][:], dst_sb[:, bass.ds(batch * BC, BC)]).then_inc(indices_done, 1)
                pool.wait_ge(t_stored, 16)
                pool.wait_ge(indices_done, batch + 1)
                for c in range(BC):
                    pool.indirect_dma_start(rows[half][:, c, :], None, t_rows,
                                            bass.IndirectOffsetOnAxis(ap=batch_dst[half][:, c:c + 1], axis=0)
                                            ).then_inc(gathered[half], 16)
        pool.wait_ge(halves_lo, SPLIT["wqkv"])
        pool.wait_ge(update_loaded, 144)
        pool.wait_ge(agg_closed, 1)
        pool.memset(hT_hi[:, :, :, P:PW].bitcast(F32), 0.0).then_inc(pads_zeroed, 1)
        pool.memset(hT_lo[:, :, :, P:PW].bitcast(F32), 0.0).then_inc(pads_zeroed, 1)
        pool.memset(ctx[:], 0.0).then_inc(ctx_zeroed, 1)
        with pool.Fori(0, NT) as t:
            pool.tensor_tensor(x_sb[:, t, :], x_sb[:, t, :], bout_row[:], ALU.add).then_inc(xb_done, 1)
        with pool.Fori(0, NT // 2) as it:
            for par in range(2):
                t = 2 * it + par
                pool.wait_ge(z_done, done(t))
                pool.wait_ge(x1_done, done(t))
                pool.tensor_tensor(x_sb[:, t, :], x1[par][:], z[par][:], ALU.add).then_inc(res_done, 1)
        pool.wait_ge(table_cleared, 16)
        pool.wait_ge(table_at_done, 1)
        for which in range(2):
            for t in range(NT):
                pool.indirect_dma_start(slot_table, bass.IndirectOffsetOnAxis(ap=table_at[:, which, t:t + 1], axis=0),
                                        token_id[:, t:t + 1], None).then_inc(table_written, 16)
        pool.wait_ge(shared_done, NT)
        pool.wait_ge(table_loaded, 16)
        with pool.Fori(0, STEPS) as it:
            for v in range(3):
                q = 3 * it + v
                pool.wait_ge(pair_turned, tile_freed(q, 3))
                pool.tensor_copy(pair_idx[v][:], slot_token[:, bass.ds(q, 1)]).then_inc(pair_index_done, 1)
                pool.wait_ge(table_loaded, 16)
                pool.wait_ge(pair_index_done, q + 4)
                pool.indirect_dma_start(pair_rows[v][:], None, h_rows,
                                        bass.IndirectOffsetOnAxis(ap=pair_idx[v][:], axis=0)).then_inc(pair_fetched[v], 16)
        pool.wait_ge(ffw_loaded, 112)
        pool.memset(ffT_hi[:, :, :, P:PW].bitcast(F32), 0.0).then_inc(pads_zeroed, 1)
        pool.memset(ffT_lo[:, :, :, P:PW].bitcast(F32), 0.0).then_inc(pads_zeroed, 1)
        pool.wait_ge(res_done, done(NT - 1))
        for t in range(NT):
            pool.tensor_tensor(x_sb[:, t, :], x_sb[:, t, :], bf2_row[:], ALU.add).then_inc(bf2_added, 1)
        for par in range(2):
            pool.wait_ge(down_stored[par], 32 * (TILES // 2))
        for t in range(NT):
            if t >= 2:
                pool.wait_ge(hm_done, t - 1)
            for which, to in ((0, eo_first), (1, eo_second)):
                pool.indirect_dma_start(to[t % 2][:], None, expert_rows,
                                        bass.IndirectOffsetOnAxis(ap=slots[:, which, t:t + 1], axis=0)).then_inc(eo_fetched[t % 2], 16)
            if t >= 1:
                keep_hm(t - 1)
        keep_hm(NT - 1)

    @block.scalar
    def _(act):
        for signal in (xnt_hi_done, rows_scaled, rows_hi_done, q_exp_done, k_copied, v_copied,
                       q_tile_done, qT_hi_done, agg_hi_done, hT_hi_done, rT_done, x1_std_done, z_std_done):
            act.sem_inc(signal, AHEAD)
        act.sem_inc(up_act, W_RING)
        act.wait_ge(gnn_loaded, 32)
        act.activation(u_hl[:, :, 0:RANK], u_raw[:], ACT.Copy).then_inc(halves_hi, 1)
        act.wait_ge(moments_done, NT)
        act.wait_ge(made, MADE_FILLS)
        act.activation(std[:], moments[:, :, 1], ACT.Sqrt, bias=eps_col[:]).then_inc(std_done, 1)

        with act.Fori(0, NT // 2) as it:
            for par in range(2):
                t = 2 * it + par
                act.wait_ge(xn_turned, done(t))
                act.wait_ge(t_mm, freed(t))
                act.activation(xnt_hi[par][:, :, 0:P], turned(6 + par)[:, :, 0:P], ACT.Copy).then_inc(xnt_hi_done, 1)
        act.wait_ge(wqkv_loaded, 16)
        for k in range(KD):
            act.activation(wqkv_hi[:, k, :], wqkv_raw[:, k, :], ACT.Copy).then_inc(halves_hi, 1)
        act.wait_ge(halves_lo, SPLIT["wqkv"])

        def scale_rows(batch, half, turn):
            act.wait_ge(gathered[half], 16 * BC * (turn + 1))
            for c in range(BC):
                last = act.activation(rows[half][:, c, :], rows[half][:, c, :], ACT.Copy,
                                      scale=weight_sb[:, bass.ds(batch * BC + c, 1)])
            last.then_inc(rows_scaled, 1)
            act.wait_ge(rows_scaled, done(batch))
            act.wait_ge(chunk_mm, BC * (batch - 1) + CHUNK_AHEAD)
            act.activation(rows_hl[half][:, :, 0:RANK], rows[half][:], ACT.Copy).then_inc(rows_hi_done, 1)

        act.wait_ge(t_mm, done(NT - 1))
        act.wait_ge(edges_loaded, 48)
        act.wait_ge(made_dve, MADE_EDGES)
        with act.Fori(0, NT // 2) as it:
            for par in range(2):
                t = 2 * it + par
                act.wait_ge(xn_turned, done(NT + t))
                act.wait_ge(v_mm, freed(t))
                act.activation(xnt_hi[par][:, :, 0:P], turned(6 + par)[:, :, 0:P], ACT.Copy).then_inc(xnt_hi_done, 1)
                scale_rows(2 * t, 0, t)
                act.wait_ge(q_sub_done, done(t))
                act.activation(q_exp[par][:], q_exp[par][:], ACT.Exp).then_inc(q_exp_done, 1)
                act.wait_ge(k_mm, done(t))
                act.activation(k_sb[:, t, :], bank[4][0:P, :], ACT.Copy).then_inc(k_copied, 1)
                act.wait_ge(v_mm, done(t))
                act.activation(v_sb[:, t, :, 0:128], bank[5][0:P, :].rearrange("p (a c) -> p a c", a=PAIRS),
                               ACT.Copy).then_inc(v_copied, 1)
                scale_rows(2 * t + 1, 1, t)
        act.wait_ge(agg_closed, 1)
        for b, (lo, hi) in enumerate(GROUPS):
            act.activation(agg_sb[:, lo:hi, :], bank[b][:, 0:(hi - lo) * PW].rearrange("p (t c) -> p t c", c=PW),
                           ACT.Copy).then_inc(agg_copied, 1)
        act.wait_ge(wout_loaded, 16)
        act.activation(wout_hi[:], wout_raw[:], ACT.Copy).then_inc(halves_hi, 1)
        act.wait_ge(update_loaded, 144)
        act.activation(vt2_hi[:], vt2_raw[:], ACT.Copy).then_inc(halves_hi, 1)
        act.wait_ge(update_loaded, 144)
        act.activation(wr_hl[:, :, 0:DR], wr_raw[:], ACT.Copy).then_inc(halves_hi, 1)
        with act.Fori(0, NT) as t:
            act.wait_ge(k_sub_done, t + 1)
            act.activation(k_sb[:, t, :], k_sb[:, t, :], ACT.Exp).then_inc(k_exp_done, 1)
        act.wait_ge(ctx_turned, 1)
        act.activation(ctxT_hi[:], bank[5][:, :].rearrange("p (a c) -> p a c", a=PAIRS), ACT.Copy).then_inc(ctxT_hi_done, 1)
        for pair in range(PAIRS):
            act.wait_ge(m_mm, pair + 1)
            act.activation(m_hi[:, pair, :], bank[(3, 4, 6, 7)[pair]][:, :], ACT.Copy).then_inc(m_hi_done, 1)
        with act.Fori(0, NT // 2) as it:
            for par in range(2):
                t = 2 * it + par
                act.wait_ge(q_turned, freed(t))
                act.activation(q_tile[par][:], q_sb[:, t, :], ACT.Copy).then_inc(q_tile_done, 1)
                act.wait_ge(g_mm, freed(t))
                act.activation(agg_hi[par][:], agg_sb[:, t, :], ACT.Copy).then_inc(agg_hi_done, 1)
            for par in range(2):
                t = 2 * it + par
                act.wait_ge(q_turned, done(t))
                act.wait_ge(y_mm, freed(t))
                act.activation(qT_hi[par][:, :, 0:P], turned(7 * par)[:, :, 0:P], ACT.Copy).then_inc(qT_hi_done, 1)
            for par in range(2):
                t = 2 * it + par
                act.wait_ge(x1_moments_done, done(t))
                act.wait_ge(x1_rstd_done, freed(t))
                act.activation(x1_std[par][:], x1_moments[par][:, 1:2], ACT.Sqrt, bias=eps_col[:]).then_inc(x1_std_done, 1)
            for par in range(2):
                t = 2 * it + par
                act.wait_ge(z_var_done, done(t))
                act.wait_ge(z_rstd_done, freed(t))
                act.activation(z_std[par][:], z_var[par][:], ACT.Sqrt, bias=eps_col[:]).then_inc(z_std_done, 1)
            for par in range(2):
                t = 2 * it + par
                act.wait_ge(h_turned, done(t))
                act.activation(hT_hi[:, :, t, 0:P], turned(7 * par)[:, :, 0:P], ACT.Copy).then_inc(hT_hi_done, 1)
            for par in range(2):
                t = 2 * it + par
                act.wait_ge(r_mm, done(t))
                act.wait_ge(l_mm, freed(t))
                act.activation(rT[par][:], bank[3 + par][:, 0:PW], ACT.Copy).then_inc(rT_done, 1)

        act.wait_ge(ws1_loaded, 16)
        act.activation(ws1_hi[:], ws1_raw[:], ACT.Copy).then_inc(halves_hi, 1)
        act.wait_ge(ws2_loaded, 48)
        act.activation(ws2_hi[:], ws2_raw[:], ACT.Copy).then_inc(halves_hi, 1)
        act.wait_ge(gap_done, 1)
        act.activation(gap[:], gap[:], ACT.Exp).then_inc(gap_exp, 1)
        act.wait_ge(ws2_loaded, 48)
        for g, (lo, hi) in enumerate(GROUPS):
            for fb in range(SB):
                n = g * SB + fb
                act.wait_ge(shared_up, n + 1)
                if n >= 2:
                    act.wait_ge(shared_lo_done, n - 1)
                act.activation(shared_h[fb % 2][:, 0:(hi - lo) * PW], bank[3 + fb % 2][:, 0:(hi - lo) * PW], ACT.Silu,
                               bias=bs1_sb[:, fb:fb + 1]).then_inc(shared_act, 1)
        act.wait_ge(combine_turned, NT)
        for g, (lo, hi) in enumerate(GROUPS):
            act.activation(combineT[:, lo:hi, 0:P], bank[g][0:NE, 0:128 * (hi - lo)].rearrange("p (t c) -> p t c", c=128)[:, :, 0:P],
                           ACT.Copy).then_inc(combineT_done, 1)
        act.wait_ge(wf1_g_done, KD)
        act.activation(wf1_hi[:], wf1_g[:], ACT.Copy).then_inc(halves_hi, 1)
        act.activation(wf2_hi[:], wf2_raw[:], ACT.Copy).then_inc(halves_hi, 1)

        def store_down(j, par, turn):
            act.wait_ge(down_mm, tile_done(j))
            act.wait_ge(down_stored[par], 32 * turn)
            act.activation(down[par][:], bank[6 + par][:, 0:D // 2], ACT.Copy).then_inc(down_copied, 1)
            act.wait_ge(down_copied, j + 1)
            for half in range(2):
                act.dma_start(expert_rows[bass.ds(j * SLOTS, SLOTS), half * (D // 2):(half + 1) * (D // 2)],
                              down[par][SLOTS * half:SLOTS * (half + 1), :]).then_inc(down_stored[par], 16)

        def act_step(it, first):
            for n in range(W_RING):
                j = W_RING * it + n
                par = n % 2
                act.wait_ge(up_turned, tile_done(j))
                act.wait_ge(down_mm, tile_freed(j, 2))
                for half in range(2):
                    last = act.activation(upT[par][:, half, :], bank[4 + par][:, SLOTS * half:SLOTS * (half + 1)], ACT.Silu,
                                          bias=w_ring[n][:, KD * DFF + 2 * D + half:KD * DFF + 2 * D + half + 1])
                last.then_inc(up_act, 1)
                if not (first and n == 0):
                    store_down(j - 1, 1 - par, (W_RING // 2) * it + (n - 1) // 2)

        act_step(0, True)
        with act.Fori(1, STEPS) as it:
            act_step(it, False)
        store_down(TILES - 1, 1, TILES // 2 - 1)
        for g, (lo, hi) in enumerate(GROUPS):
            for t in range(lo, hi):
                act.wait_ge(hm_moments_done, t + 1)
                if t >= 2:
                    act.wait_ge(hm_rstd_done, t - 1)
                act.activation(hm_std[t % 2][:], hm_moments[t % 2][:, 1:2], ACT.Sqrt, bias=eps_col[:]).then_inc(hm_std_done, 1)
                act.wait_ge(ff_turned, t + 1)
                if g >= 1:
                    act.wait_ge(ff_up, 2 * g)
                act.activation(ffT_hi[:, :, t - lo, 0:P], turned(t % 2)[:, :, 0:P], ACT.Copy).then_inc(ffT_hi_done, 1)
            for half in range(2):
                act.wait_ge(ff_up, 2 * g + half + 1)
                if g >= 1:
                    act.wait_ge(ff_h_lo_done, 2 * g + half - 1)
                act.activation(ff_h[half][:, 0:(hi - lo) * PW], bank[2 + half][:, 0:(hi - lo) * PW], ACT.Silu,
                               bias=bf1_sb[:, half:half + 1]).then_inc(ff_act, 1)

    @block.vector
    def _(dve):
        for signal in (xn_done, xnt_lo_done, t_done, rows_lo_done, q_sub_done, k_top_done, qT_lo_done,
                       agg_lo_done, g_sum_done, y_sum_done, x1_done, x1_parts_done, x1_moments_done, z_var_done, x1_rstd_done, z_done, z_rstd_done,
                       h_done, hT_lo_done, logits_done):
            dve.sem_inc(signal, AHEAD)
        for signal in (pairT_done, up_copied):
            dve.sem_inc(signal, W_RING)
        own = Steps()
        dve.wait_ge(made, MADE_NODES)
        dve.tensor_copy(node_of_col[:], node_i32[:]).then_inc(made_dve, 1)
        dve.wait_ge(made, MADE_IDS)
        dve.tensor_copy(expert_id[:], expert_i32[:]).then_inc(made_dve, 1)
        dve.tensor_copy(tile_start[:], tile_start_i32[:]).then_inc(made_dve, 1)
        for t in range(NT):
            if t % 2 == 0:
                dve.wait_ge(x_loaded[t // 2], 32)
            dve.bn_stats(stats[:, t, :], x_sb[:, t, :]).then_inc(dve_step, own.one())
        for t in range(NT):
            dve.wait_ge(dve_step, own.now())
            dve.bn_aggr(moments[:, t, :], stats[:, t, :]).then_inc(moments_done, 1)
        dve.wait_ge(std_done, 1)
        dve.reciprocal(rstd[:], std[:]).then_inc(dve_step, own.one())
        dve.wait_ge(halves_hi, SPLIT["u"])
        dve.tensor_tensor(u_hl[:, :, RANK:2 * RANK], u_raw[:], u_hl[:, :, 0:RANK].bitcast(F32),
                          ALU.subtract).then_inc(halves_lo, 1)
        dve.wait_ge(dve_step, own.now())
        dve.wait_ge(gnn_loaded, 32)

        def normed(t, par, item):
            dve.wait_ge(xn_turned, freed(item))
            dve.tensor_scalar(xn[par][:], x_sb[:, t, :], moments[:, t, 0:1], rstd[:, bass.ds(t, 1)],
                              ALU.subtract, ALU.mult).then_inc(xn_done, 1)

        def xnt_low(par, item):
            dve.wait_ge(xnt_hi_done, done(item))
            dve.tensor_tensor(xnt_lo[par][:, :, 0:P], turned(6 + par)[:, :, 0:P],
                              xnt_hi[par][:, :, 0:P].bitcast(F32), ALU.subtract).then_inc(xnt_lo_done, 1)

        with dve.Fori(0, NT // 2) as it, own.loop(it, NT // 2, 4):
            for par in range(2):
                normed(2 * it + par, par, 2 * it + par)
            for par in range(2):
                xnt_low(par, 2 * it + par)
            for par in range(2):
                t = 2 * it + par
                dve.wait_ge(t_mm, done(t))
                dve.tensor_copy(t_sb[:, t, :], bank[4 + par][0:P, 0:RANK]).then_inc(dve_step, own.one())
                dve.wait_ge(dve_step, own.now())
                dve.tensor_tensor(t_sb[:, t, :], t_sb[:, t, :], bank[4 + par][0:P, RANK:2 * RANK], ALU.add).then_inc(dve_step, own.one())
                dve.wait_ge(dve_step, own.now())
                dve.tensor_tensor(t_sb[:, t, :], t_sb[:, t, :], s_row[:], ALU.mult).then_inc(t_done, 1)
        for k in range(KD):
            dve.wait_ge(halves_hi, SPLIT["wqkv"] - KD + k + 1)
            dve.tensor_tensor(wqkv_lo[:, k, :], wqkv_raw[:, k, :], wqkv_hi[:, k, :].bitcast(F32),
                              ALU.subtract).then_inc(halves_lo, 1)
        dve.wait_ge(edges_loaded, 48)
        dve.tensor_copy(src_f[:], src_sb[:]).then_inc(made_dve, 1)
        dve.wait_ge(halves_lo, SPLIT["wqkv"])
        dve.memset(v_sb[:, :, :, 128:130], 1.0).then_inc(made_dve, 1)
        dve.memset(k_top[:], -3.0e38).then_inc(made_dve, 1)
        dve.wait_ge(made_dve, MADE_EDGES)
        dve.wait_ge(agg_opened, 1)

        def onehots(batch, half, first, last):
            for c in range(first, last):
                chunk = batch * BC + c
                dve.wait_ge(chunk_mm, chunk + 1 - OH_RING + CHUNK_AHEAD)
                dve.tensor_scalar(onehot[(half * BC + c) % OH_RING][:], node_of_col[:].rearrange("p t c -> p (t c)"),
                                  src_f[:, bass.ds(chunk, 1)], None, ALU.is_equal).then_inc(onehot_done, 1)

        def rows_low(batch, half):
            dve.wait_ge(rows_hi_done, done(batch))
            dve.tensor_tensor(rows_hl[half][:, :, RANK:2 * RANK], rows[half][:],
                              rows_hl[half][:, :, 0:RANK].bitcast(F32), ALU.subtract).then_inc(rows_lo_done, 1)

        with dve.Fori(0, NT // 2) as it, own.loop(it, NT // 2, 8):
            for par in range(2):
                t = 2 * it + par
                normed(t, par, NT + t)
                rows_low(2 * t, 0)
                onehots(2 * t, 0, 0, 4)
                xnt_low(par, NT + t)
                onehots(2 * t, 0, 4, BC)
                psq = bank[3][0:P, :].rearrange("p (h c) -> p h c", h=HEADS)
                qe = q_exp[par][:].rearrange("p (h c) -> p h c", h=HEADS)
                dve.wait_ge(q_mm, done(t))
                dve.reduce_max(q_top[:], psq, AX.X).then_inc(dve_step, own.one())
                dve.wait_ge(dve_step, own.now())
                dve.tensor_tensor(qe, psq, q_top[:].unsqueeze(2).broadcast_to([P, HEADS, RANK]),
                                  ALU.subtract).then_inc(q_sub_done, 1)
                rows_low(2 * t + 1, 1)
                onehots(2 * t + 1, 1, 0, 3)
                dve.wait_ge(k_mm, done(t))
                dve.wait_ge(k_top_done, freed(t, 1))
                dve.tensor_tensor(k_top[:], k_top[:], bank[4][0:P, :], ALU.max).then_inc(k_top_done, 1)
                dve.wait_ge(q_exp_done, done(t))
                dve.reduce_sum(q_sum[:], qe, AX.X).then_inc(dve_step, own.one())
                dve.wait_ge(dve_step, own.now())
                dve.reciprocal(q_inv[:], q_sum[:]).then_inc(dve_step, own.one())
                dve.wait_ge(dve_step, own.now())
                dve.tensor_tensor(q_sb[:, t, :].rearrange("p (h c) -> p h c", h=HEADS), qe,
                                  q_inv[:].unsqueeze(2).broadcast_to([P, HEADS, RANK]), ALU.mult).then_inc(dve_step, own.one())
                onehots(2 * t + 1, 1, 3, BC)
        dve.wait_ge(agg_closed, 1)
        dve.wait_ge(k_top_turned, 1)
        dve.reduce_max(k_top_col[:], turned(6)[:, :, 0:P], AX.X).then_inc(dve_step, own.one())
        dve.wait_ge(dve_step, own.now())
        dve.tensor_copy(k_top_wide[:], k_top_col[:].unsqueeze(2).broadcast_to([128, PAIRS, P])).then_inc(k_top_wide_done, 1)
        dve.wait_ge(k_copied, done(NT - 1))
        dve.wait_ge(k_top_back, 1)
        with dve.Fori(0, NT) as t:
            dve.tensor_tensor(k_sb[:, t, :], k_sb[:, t, :], bank[7][0:P, :], ALU.subtract).then_inc(k_sub_done, 1)
        dve.wait_ge(halves_hi, SPLIT["wout"])
        dve.tensor_tensor(wout_lo[:], wout_raw[:], wout_hi[:].bitcast(F32), ALU.subtract).then_inc(halves_lo, 1)
        dve.wait_ge(halves_hi, SPLIT["vt"])
        dve.tensor_tensor(vt2_lo[:], vt2_raw[:], vt2_hi[:].bitcast(F32), ALU.subtract).then_inc(halves_lo, 1)
        dve.wait_ge(halves_hi, SPLIT["wr"])
        dve.tensor_tensor(wr_hl[:, :, DR:2 * DR], wr_raw[:], wr_hl[:, :, 0:DR].bitcast(F32),
                          ALU.subtract).then_inc(halves_lo, 1)
        dve.wait_ge(ctx_mm, PAIRS)
        dve.wait_ge(ctx_zeroed, 1)
        for pair in range(PAIRS):
            at = 132 * (pair % 2)
            dve.reciprocal(k_inv[:, pair:pair + 1], bank[3 + pair // 2][:, at + 128:at + 129]).then_inc(dve_step, own.one())
        dve.wait_ge(dve_step, own.now())
        for pair in range(PAIRS):
            at = 132 * (pair % 2)
            for h in range(2):
                part = slice(64 * h, 64 * (h + 1))
                dve.tensor_scalar(ctx[part, pair, part], bank[3 + pair // 2][part, at + 64 * h:at + 64 * (h + 1)],
                                  k_inv[part, pair:pair + 1], None, ALU.mult).then_inc(ctx_done, 1)
        dve.wait_ge(ctxT_hi_done, 1)
        dve.tensor_tensor(ctxT_lo[:], bank[5][:, :].rearrange("p (a c) -> p a c", a=PAIRS), ctxT_hi[:].bitcast(F32),
                          ALU.subtract).then_inc(ctxT_lo_done, 1)
        for pair in range(PAIRS):
            dve.wait_ge(m_hi_done, pair + 1)
            dve.tensor_tensor(m_lo[:, pair, :], bank[(3, 4, 6, 7)[pair]][:, :], m_hi[:, pair, :].bitcast(F32),
                              ALU.subtract).then_inc(m_lo_done, 1)
        dve.wait_ge(update_loaded, 144)
        dve.wait_ge(xb_done, NT)
        with dve.Fori(0, NT // 2) as it, own.loop(it, NT // 2, 2):
            tiles = [(par, 2 * it + par) for par in range(2)]
            for par, t in tiles:
                dve.wait_ge(agg_hi_done, done(t))
                dve.tensor_tensor(agg_lo[par][:], agg_sb[:, t, :], agg_hi[par][:].bitcast(F32),
                                  ALU.subtract).then_inc(agg_lo_done, 1)
            for par, t in tiles:
                dve.wait_ge(qT_hi_done, done(t))
                dve.tensor_tensor(qT_lo[par][:, :, 0:P], turned(7 * par)[:, :, 0:P],
                                  qT_hi[par][:, :, 0:P].bitcast(F32), ALU.subtract).then_inc(qT_lo_done, 1)
            for par, t in tiles:
                dve.wait_ge(g_mm, done(t))
                dve.tensor_tensor(mixed[par][:], bank[3 + par][0:P, :], bias_row[:], ALU.add).then_inc(g_sum_done, 1)
            for par, t in tiles:
                dve.wait_ge(y_mm, done(t))
                dve.wait_ge(g_sum_done, done(t))
                dve.scalar_tensor_tensor(mixed[par][:], mixed[par][:], 0.0, bank[1 + par][0:P, :],
                                         ALU.max, ALU.add).then_inc(y_sum_done, 1)
            for par, t in tiles:
                dve.wait_ge(y_sum_done, done(t))
                dve.wait_ge(res_done, freed(t))
                dve.tensor_tensor(x1[par][:], mixed[par][:], x_sb[:, t, :], ALU.add).then_inc(x1_done, 1)
            for par, t in tiles:
                dve.wait_ge(x1_done, done(t))
                dve.bn_stats(x1_parts[par][:], x1[par][:]).then_inc(x1_parts_done, 1)
            for par, t in tiles:
                dve.wait_ge(moments_done, NT)
                dve.wait_ge(x1_parts_done, done(t))
                dve.bn_aggr(x1_moments[par][:], x1_parts[par][:]).then_inc(x1_moments_done, 1)
            for par, t in tiles:
                dve.wait_ge(x1_std_done, done(t))
                dve.reciprocal(x1_rstd[par][:], x1_std[par][:]).then_inc(x1_rstd_done, 1)
            for par, t in tiles:
                dve.wait_ge(x1_rstd_done, done(t))
                dve.tensor_scalar(z_var[par][:], x1_moments[par][:, 1:2], x1_rstd[par][:], x1_rstd[par][:],
                                  ALU.mult, ALU.mult).then_inc(z_var_done, 1)
            for par, t in tiles:
                dve.tensor_scalar(z[par][:], x1[par][:], x1_moments[par][:, 0:1], x1_rstd[par][:],
                                  ALU.subtract, ALU.mult).then_inc(z_done, 1)
            for par, t in tiles:
                dve.wait_ge(z_std_done, done(t))
                dve.reciprocal(z_rstd[par][:], z_std[par][:]).then_inc(z_rstd_done, 1)
            for par, t in tiles:
                dve.wait_ge(z_rstd_done, done(t))
                dve.wait_ge(h_turned, freed(t))
                dve.wait_ge(h_stored[par], 16 * it)
                dve.scalar_tensor_tensor(h_tile[par][:], z[par][:], z_rstd[par][:], g_row[:],
                                         ALU.mult, ALU.mult).then_inc(dve_step, own.one())
            for par, t in tiles:
                dve.wait_ge(dve_step, own.now())
                dve.tensor_tensor(h_tile[par][:], h_tile[par][:], b_row[:], ALU.add).then_inc(h_done, 1)
            for par, t in tiles:
                dve.wait_ge(hT_hi_done, done(t))
                dve.tensor_tensor(hT_lo[:, :, t, 0:P], turned(7 * par)[:, :, 0:P],
                                  hT_hi[:, :, t, 0:P].bitcast(F32), ALU.subtract).then_inc(hT_lo_done, 1)
            for par, t in tiles:
                dve.wait_ge(l_mm, done(t))
                dve.tensor_scalar(logits[:, t, :], bank[5 + par][0:P, 0:NE], 1.0 / TEMP, None,
                                  ALU.mult).then_inc(logits_done, 1)
        for t in range(NT):
            dve.wait_ge(logits_done, done(t))
            dve.max(top_logit[:, t, :], logits[:, t, :]).then_inc(dve_step, own.one())
        for t in range(NT):
            dve.wait_ge(dve_step, own.now())
            dve.max_index(top_expert[:, t, :], top_logit[:, t, :], logits[:, t, :]).then_inc(picked, 1)

        dve.wait_ge(picked, NT)
        dve.tensor_copy(picks[:], top_expert[:, :, 0:2]).then_inc(dve_step, own.one())
        dve.tensor_tensor(gap[:], top_logit[:, :, 1], top_logit[:, :, 0], ALU.subtract).then_inc(gap_done, 1)
        dve.wait_ge(dve_step, own.now())
        dve.wait_ge(made_dve, MADE_EXPERT_IDS)
        every = expert_id[:].unsqueeze(1).broadcast_to([P, NT, NE])
        for which, to in enumerate((first_pick, second_pick)):
            dve.tensor_tensor(to[:], every, picks[:, :, which:which + 1].broadcast_to([P, NT, NE]),
                              ALU.is_equal).then_inc(dve_step, own.one())
        dve.memset(earlier[:, 0, :], 0.0).then_inc(earlier_done, 1)
        dve.wait_ge(dve_step, own.now())
        dve.wait_ge(dve_step, own.now())
        dve.tensor_tensor(picked_any[:], first_pick[:], second_pick[:], ALU.add).then_inc(dve_step, own.one())
        dve.wait_ge(dve_step, own.now())
        for t in range(NT):
            dve.wait_ge(earlier_done, t + 1)
            dve.tensor_tensor(earlier[:, t + 1, :], earlier[:, t, :], picked_any[:, t, :], ALU.add).then_inc(earlier_done, 1)
        dve.wait_ge(gap_exp, 1)
        dve.tensor_scalar(gate2[:], gap[:], 1.0, None, ALU.add).then_inc(dve_step, own.one())
        dve.wait_ge(dve_step, own.now())
        dve.reciprocal(gate1[:], gate2[:]).then_inc(dve_step, own.one())
        dve.wait_ge(dve_step, own.now())
        dve.tensor_tensor(gate2[:], gate1[:], gap[:], ALU.mult).then_inc(dve_step, own.one())
        dve.wait_ge(res_done, done(NT - 1))
        for raw, hi_, lo_, ready in ((ws1_raw, ws1_hi, ws1_lo, SPLIT["ws1"]),
                                             (ws2_raw, ws2_hi, ws2_lo, SPLIT["ws2"])):
            dve.wait_ge(halves_hi, ready)
            dve.tensor_tensor(lo_[:], raw[:], hi_[:].bitcast(F32), ALU.subtract).then_inc(halves_lo, 1)
        dve.wait_ge(count_mm, 1)
        dve.tensor_scalar(padded_i32[:], bank[2][0:P, 0:NE], float(SLOTS - 1), None, ALU.add).then_inc(dve_step, own.one())
        dve.wait_ge(dve_step, own.now())
        dve.tensor_scalar(padded_i32[:], padded_i32[:], 6, 6, ALU.arith_shift_right, ALU.arith_shift_left).then_inc(dve_step, own.one())
        dve.wait_ge(dve_step, own.now())
        dve.tensor_copy(padded[:], padded_i32[:]).then_inc(dve_step, own.one())
        dve.wait_ge(dve_step, own.now())
        src_scan = padded
        shifts = (1, 2, 4, 8, 16, 32)
        for n, shift in enumerate(shifts):
            to = scan[n % 2]
            dve.wait_ge(dve_step, own.now())
            dve.tensor_copy(to[:, 0:shift], src_scan[:, 0:shift]).then_inc(dve_step, own.one())
            dve.tensor_tensor(to[:, shift:NE], src_scan[:, shift:NE], src_scan[:, 0:NE - shift], ALU.add).then_inc(dve_step, own.one())
            src_scan = to
        ends = src_scan
        dve.wait_ge(dve_step, own.now())
        dve.tensor_tensor(starts[:], ends[:], padded[:], ALU.subtract).then_inc(dve_step, own.one())
        dve.tensor_scalar(scan[0][:], ends[:], tile_start[:], None, ALU.is_le).then_inc(dve_step, own.one())
        dve.wait_ge(dve_step, own.now())
        dve.reduce_sum(tile_expert_f[:], scan[0][:], AX.X).then_inc(dve_step, own.one())
        dve.wait_ge(dve_step, own.now())
        dve.tensor_scalar(tile_expert[:], tile_expert_f[:], float(NE - 1), None, ALU.min).then_inc(tile_expert_done, 1)
        dve.wait_ge(rank_mm, 2)
        for n in range(2):
            dve.tensor_tensor(slot_all[:, 5 * n:5 * (n + 1), :],
                              bank[n][0:P, 0:5 * NE].rearrange("p (t e) -> p t e", e=NE),
                              starts[:].unsqueeze(1).broadcast_to([P, 5, NE]), ALU.add).then_inc(dve_step, own.one())
        dve.wait_ge(dve_step, own.now())
        for which, pick in enumerate((first_pick, second_pick)):
            if which:
                dve.wait_ge(dve_step, own.now())
            dve.tensor_tensor(work[:], slot_all[:], pick[:], ALU.mult).then_inc(dve_step, own.one())
            dve.wait_ge(dve_step, own.now())
            dve.reduce_sum(slots_f[:, which, :], work[:], AX.X).then_inc(dve_step, own.one())
        dve.wait_ge(dve_step, own.now())
        dve.tensor_copy(slots[:], slots_f[:]).then_inc(dve_step, own.one())
        dve.wait_ge(dve_step, own.now())
        dve.tensor_scalar(slot_low[:], slots[:], 127, None, ALU.bitwise_and).then_inc(dve_step, own.one())
        dve.tensor_scalar(slot_high[:], slots[:], 7, None, ALU.arith_shift_right).then_inc(dve_step, own.one())
        dve.wait_ge(dve_step, own.now())
        dve.scalar_tensor_tensor(table_at[:], slot_low[:], float(PAIR_TILES), slot_high[:], ALU.mult, ALU.add).then_inc(table_at_done, 1)
        dve.tensor_tensor(slot_all[:], first_pick[:], gate1[:].unsqueeze(2).broadcast_to([P, NT, NE]), ALU.mult).then_inc(dve_step, own.one())
        dve.tensor_tensor(work[:], second_pick[:], gate2[:].unsqueeze(2).broadcast_to([P, NT, NE]), ALU.mult).then_inc(dve_step, own.one())
        dve.wait_ge(dve_step, own.now())
        dve.tensor_tensor(work[:], work[:], slot_all[:], ALU.add).then_inc(combine_done, 1)
        dve.wait_ge(ws2_loaded, 48)
        dve.tensor_scalar(bs2_row[:], bs2_row[:], SHARED_SCALE, None, ALU.mult).then_inc(dve_step, own.one())
        dve.wait_ge(dve_step, own.now())
        for g, (lo, hi) in enumerate(GROUPS):
            width = (hi - lo) * PW
            for fb in range(SB):
                n = g * SB + fb
                dve.wait_ge(shared_act, n + 1)
                if g:
                    dve.wait_ge(shared_down, lo)
                dve.tensor_copy(shared_hT_hi[:, fb, 0:width], shared_h[fb % 2][:, 0:width]).then_inc(dve_step, own.one())
                dve.wait_ge(dve_step, own.now())
                dve.tensor_tensor(shared_hT_lo[:, fb, 0:width], shared_h[fb % 2][:, 0:width],
                                  shared_hT_hi[:, fb, 0:width].bitcast(F32), ALU.subtract).then_inc(shared_lo_done, 1)
            for t in range(lo, hi):
                dve.wait_ge(shared_down, t + 1)
                dve.scalar_tensor_tensor(shared[:, t, :], bank[5 + t % 2][0:P, :], SHARED_SCALE, bs2_row[:],
                                         ALU.mult, ALU.add).then_inc(shared_done, 1)
        dve.wait_ge(ffw_loaded, 112)
        for k in range(KD):
            dve.tensor_scalar(wf1_g[:, k, :], wf1_raw[:, k, :], g_col[:, k:k + 1], None, ALU.mult).then_inc(wf1_g_done, 1)
        dve.wait_ge(halves_hi, SPLIT["wf1"])
        dve.tensor_tensor(wf1_lo[:], wf1_g[:], wf1_hi[:].bitcast(F32), ALU.subtract).then_inc(halves_lo, 1)
        dve.wait_ge(halves_hi, SPLIT["wf2"])
        dve.tensor_tensor(wf2_lo[:], wf2_raw[:], wf2_hi[:].bitcast(F32), ALU.subtract).then_inc(halves_lo, 1)
        dve.wait_ge(bf1_mm, 2)
        dve.tensor_tensor(bf1_sb[:], bank[3][:, 0:2], bf1_raw[:], ALU.add).then_inc(bf1_done, 1)
        dve.wait_ge(shared_done, NT)
        for t in range(NT):
            dve.wait_ge(b2_mm, t + 1)
            dve.tensor_tensor(shared[:, t, :], shared[:, t, :], bank[5 + t % 2][0:P, :], ALU.add).then_inc(b2_added, 1)
        with dve.Fori(0, STEPS) as it:
            for n in range(W_RING):
                j = W_RING * it + n
                if n % 2 == 0:
                    v = n // 2
                    q = 3 * it + v
                    dve.wait_ge(pair_turned, tile_done(q))
                    dve.wait_ge(up_mm, tile_freed(j, W_RING))
                    dve.tensor_copy(pair_rowsT[v][:], bank[v % 2][:, :].rearrange("p (k c) -> p k c", k=KD)).then_inc(pairT_done, 1)
                par = n % 2
                dve.wait_ge(up_mm, tile_done(j))
                dve.wait_ge(up_turned, tile_freed(j, 2))
                dve.tensor_copy(up[par][:], bank[2 + par][:, 0:128]).then_inc(up_copied, 1)
        for g, (lo, hi) in enumerate(GROUPS):
            for t in range(lo, hi):
                par = t % 2
                dve.wait_ge(eo_fetched[par], 32 * (t // 2 + 1))
                if t >= 2:
                    dve.wait_ge(hm_kept, t - 1)
                dve.scalar_tensor_tensor(hmoe[par][:], eo_first[par][:], gate1[:, t:t + 1], shared[:, t, :], ALU.mult,
                                         ALU.add).then_inc(dve_step, own.one())
                dve.wait_ge(dve_step, own.now())
                dve.scalar_tensor_tensor(hmoe[par][:], eo_second[par][:], gate2[:, t:t + 1], hmoe[par][:], ALU.mult,
                                         ALU.add).then_inc(hm_done, 1)
                dve.wait_ge(hm_done, t + 1)
                dve.bn_stats(hm_parts[par][:], hmoe[par][:]).then_inc(dve_step, own.one())
                dve.wait_ge(dve_step, own.now())
                dve.bn_aggr(hm_moments[par][:], hm_parts[par][:]).then_inc(hm_moments_done, 1)
                dve.wait_ge(hm_std_done, t + 1)
                dve.reciprocal(hm_rstd[par][:], hm_std[par][:]).then_inc(hm_rstd_done, 1)
                dve.wait_ge(hm_rstd_done, t + 1)
                if t >= 2:
                    dve.wait_ge(ff_turned, t - 1)
                dve.tensor_scalar(ff_in[par][:], hmoe[par][:], hm_moments[par][:, 0:1], hm_rstd[par][:],
                                  ALU.subtract, ALU.mult).then_inc(ff_in_done, 1)
                dve.wait_ge(ffT_hi_done, t + 1)
                dve.tensor_tensor(ffT_lo[:, :, t - lo, 0:P], turned(par)[:, :, 0:P],
                                  ffT_hi[:, :, t - lo, 0:P].bitcast(F32), ALU.subtract).then_inc(ffT_lo_done, 1)
            width = (hi - lo) * PW
            for half in range(2):
                n = 2 * g + half
                dve.wait_ge(ff_act, n + 1)
                if g:
                    dve.wait_ge(ff_down, lo)
                dve.tensor_copy(ff_hT_hi[:, half, 0:width], ff_h[half][:, 0:width]).then_inc(dve_step, own.one())
                dve.wait_ge(dve_step, own.now())
                dve.tensor_tensor(ff_hT_lo[:, half, 0:width], ff_h[half][:, 0:width],
                                  ff_hT_hi[:, half, 0:width].bitcast(F32), ALU.subtract).then_inc(ff_h_lo_done, 1)
            for t in range(lo, hi):
                dve.wait_ge(ff_down, t + 1)
                dve.wait_ge(hm_kept, t + 1)
                if t >= 2:
                    dve.wait_ge(result_stored[t % 2], 32 * (t // 2))
                dve.tensor_tensor(result[t % 2][:], bank[4 + t % 2][0:P, :], x_sb[:, t, :], ALU.add).then_inc(result_done, 1)

    @block.tensor
    def _(pe):
        for signal in (xn_turned, t_mm, q_mm, k_mm, v_mm, q_turned, g_mm, y_mm, h_turned, r_mm, l_mm):
            pe.sem_inc(signal, AHEAD)
        for signal in (pair_turned, up_mm, up_turned, down_mm):
            pe.sem_inc(signal, W_RING)
        pe.sem_inc(chunk_mm, CHUNK_AHEAD)

        def turn(tile, to, signal):
            for k in range(KD):
                last = pe.transpose(turned(to)[:, k, 0:P], tile[:, 128 * k:128 * (k + 1)], ident[0:P, 0:P])
            last.then_inc(signal, 1)

        def turn_x(par, item):
            pe.wait_ge(xn_done, done(item))
            pe.wait_ge(xnt_lo_done, freed(item))
            turn(xn[par], 6 + par, xn_turned)

        def product(to, terms, signal):
            for i, (a, b) in enumerate(terms):
                last = pe.matmul(to, a, b, start=(i == 0), stop=(i == len(terms) - 1))
            last.then_inc(signal, 1)

        def split_terms(a_hi, a_lo, b_hi, b_lo, blocks):
            terms = []
            for k in range(blocks):
                terms += [(a_hi(k), b_hi(k)), (a_hi(k), b_lo(k)), (a_lo(k), b_hi(k))]
            return terms

        pe.wait_ge(made, MADE_IDENT)
        pe.wait_ge(halves_lo, SPLIT["u"])
        with pe.Fori(0, NT // 2) as it:
            for par in range(2):
                turn_x(par, 2 * it + par)
            for par in range(2):
                t = 2 * it + par
                pe.wait_ge(xnt_lo_done, done(t))
                pe.wait_ge(t_done, freed(t))
                product(bank[4 + par][0:P, 0:2 * RANK],
                        [(half[par][:, k, 0:P], u_hl[:, k, :]) for k in range(KD) for half in (xnt_hi, xnt_lo)], t_mm)
        pe.wait_ge(made, MADE_ZEROS)
        agg = [bank[b][:, 0:(hi - lo) * PW] for b, (lo, hi) in enumerate(GROUPS)]
        for b, (lo, hi) in enumerate(GROUPS):
            last = pe.matmul(agg[b], zero_w[:], onehot[0][:, lo * PW:hi * PW], start=True, stop=False,
                             skip_group_check=True)
        last.then_inc(agg_opened, 1)

        def sum_edges(batch, half, first, last_c):
            pe.wait_ge(rows_lo_done, done(batch))
            for c in range(first, last_c):
                pe.wait_ge(onehot_done, batch * BC + c + 1)
                for b, (lo, hi) in enumerate(GROUPS):
                    last = pe.matmul(agg[b], rows_hl[half][:, c, :],
                                     onehot[(half * BC + c) % OH_RING][:, lo * PW:hi * PW],
                                     start=False, stop=False, skip_group_check=True)
                last.then_inc(chunk_mm, 1)

        pe.wait_ge(halves_lo, SPLIT["wqkv"])
        pe.wait_ge(t_done, done(NT - 1))
        with pe.Fori(0, NT // 2) as it:
            for par in range(2):
                t = 2 * it + par
                turn_x(par, NT + t)
                sum_edges(2 * t, 0, 0, 4)
                pe.wait_ge(xnt_lo_done, done(NT + t))
                for part, (signal, readers) in enumerate(((q_mm, (q_sub_done,)), (k_mm, (k_top_done, k_copied)),
                                                          (v_mm, (v_copied,)))):
                    for reader in readers:
                        pe.wait_ge(reader, freed(t, 1))
                    cols = slice(D * part, D * (part + 1))
                    product(bank[3 + part][0:P, :],
                            split_terms(lambda k: xnt_hi[par][:, k, 0:P], lambda k: xnt_lo[par][:, k, 0:P],
                                        lambda k: wqkv_hi[:, k, cols], lambda k: wqkv_lo[:, k, cols], KD), signal)
                sum_edges(2 * t, 0, 4, BC)
                sum_edges(2 * t + 1, 1, 0, BC)
        for b, (lo, hi) in enumerate(GROUPS):
            last = pe.matmul(agg[b], zero_w[:], onehot[0][:, lo * PW:hi * PW], start=False, stop=True,
                             skip_group_check=True)
        last.then_inc(agg_closed, 1)
        pe.wait_ge(k_top_done, done(NT - 1))
        pe.wait_ge(xnt_lo_done, done(2 * NT - 1))
        turn(k_top, 6, k_top_turned)
        pe.wait_ge(k_top_wide_done, 1)
        for k in range(PAIRS):
            last = pe.transpose(bank[7][0:P, 128 * k:128 * (k + 1)], k_top_wide[:, k, :], ident[:])
        last.then_inc(k_top_back, 1)
        pe.wait_ge(v_copied, done(NT - 1))
        pe.wait_ge(q_sub_done, done(NT - 1))
        for pair in range(PAIRS):
            at = 132 * (pair % 2)
            for t in range(NT):
                pe.wait_ge(k_exp_done, t + 1)
                last = pe.matmul(bank[3 + pair // 2][:, at:at + 130], k_sb[:, t, 128 * pair:128 * (pair + 1)],
                                 v_sb[:, t, pair, :], start=(t == 0), stop=(t == NT - 1))
            last.then_inc(ctx_mm, 1)
        pe.wait_ge(ctx_done, 2 * PAIRS)
        for pair in range(PAIRS):
            last = pe.transpose(bank[5][:, 128 * pair:128 * (pair + 1)], ctx[:, pair, :], ident[:])
        last.then_inc(ctx_turned, 1)
        pe.wait_ge(ctxT_lo_done, 1)
        pe.wait_ge(halves_lo, SPLIT["wout"])
        for pair in range(PAIRS):
            product(bank[(3, 4, 6, 7)[pair]][:, :],
                    [(ctxT_hi[:, pair, :], wout_hi[:, pair, :]), (ctxT_hi[:, pair, :], wout_lo[:, pair, :]),
                     (ctxT_lo[:, pair, :], wout_hi[:, pair, :])], m_mm)
        pe.wait_ge(m_lo_done, PAIRS)
        pe.wait_ge(pads_zeroed, 2)
        pe.wait_ge(halves_lo, SPLIT["vt"])
        pe.wait_ge(halves_lo, SPLIT["wr"])
        pe.wait_ge(agg_copied, 3)
        with pe.Fori(0, NT // 2) as it:
            tiles = [(par, 2 * it + par) for par in range(2)]
            for par, t in tiles:
                pe.wait_ge(q_tile_done, done(t))
                pe.wait_ge(hT_lo_done, freed(t))
                turn(q_tile[par], 7 * par, q_turned)
            for par, t in tiles:
                pe.wait_ge(agg_lo_done, done(t))
                pe.wait_ge(g_sum_done, freed(t))
                pe.wait_ge(rT_done, freed(t))
                product(bank[3 + par][0:P, :], [(agg_hi[par][:, 0:P], vt2_hi[:]), (agg_hi[par][:, 0:P], vt2_lo[:]),
                                                (agg_lo[par][:, 0:P], vt2_hi[:])], g_mm)
            for par, t in tiles:
                pe.wait_ge(qT_lo_done, done(t))
                pe.wait_ge(y_sum_done, freed(t))
                product(bank[1 + par][0:P, :],
                        split_terms(lambda k: qT_hi[par][:, k, 0:P], lambda k: qT_lo[par][:, k, 0:P],
                                    lambda k: m_hi[:, k, :], lambda k: m_lo[:, k, :], PAIRS), y_mm)
            for par, t in tiles:
                pe.wait_ge(h_done, done(t))
                turn(h_tile[par], 7 * par, h_turned)
            for par, t in tiles:
                pe.wait_ge(hT_lo_done, done(t))
                product(bank[3 + par][:, 0:PW],
                        [(wr_hl[:, k, :], half[:, k, t, :]) for k in range(KD) for half in (hT_hi, hT_lo)], r_mm)
            for par, t in tiles:
                pe.wait_ge(rT_done, done(t))
                pe.wait_ge(logits_done, freed(t))
                product(bank[5 + par][0:P, 0:NE], [(rT[par][:, 0:P], codebook2[:])], l_mm)

        def shared_up_products(g):
            lo, hi = GROUPS[g]
            for fb in range(SB):
                n = g * SB + fb
                if n >= 2:
                    pe.wait_ge(shared_act, n - 1)
                cols = slice(128 * fb, 128 * (fb + 1))
                product(bank[3 + fb % 2][:, 0:(hi - lo) * PW],
                        split_terms(lambda k: ws1_hi[:, k, cols], lambda k: ws1_lo[:, k, cols],
                                    lambda k: hT_hi[:, k, lo:hi, :].rearrange("p t c -> p (t c)"),
                                    lambda k: hT_lo[:, k, lo:hi, :].rearrange("p t c -> p (t c)"), KD), shared_up)

        def shared_down_products(g):
            lo, hi = GROUPS[g]
            pe.wait_ge(shared_lo_done, (g + 1) * SB)
            for t in range(lo, hi):
                if t >= 2:
                    pe.wait_ge(shared_done, t - 1)
                cols = slice((t - lo) * PW, (t - lo) * PW + P)
                product(bank[5 + t % 2][0:P, :],
                        split_terms(lambda k: shared_hT_hi[:, k, cols], lambda k: shared_hT_lo[:, k, cols],
                                    lambda k: ws2_hi[:, k, :], lambda k: ws2_lo[:, k, :], SB), shared_down)

        pe.wait_ge(made, MADE_BEFORE)
        pe.wait_ge(earlier_done, NT + 1)
        for n in range(2):
            tiles_ = slice(5 * n, 5 * (n + 1))
            product(bank[n][0:P, 0:5 * NE], [(before[:], picked_any[:, tiles_, :].rearrange("p t e -> p (t e)")),
                                             (ones[:], earlier[:, tiles_, :].rearrange("p t e -> p (t e)"))], rank_mm)
        product(bank[2][0:P, 0:NE], [(ones[:], earlier[:, NT, :])], count_mm)
        pe.wait_ge(halves_lo, SPLIT["ws1"])
        shared_up_products(0)
        pe.wait_ge(halves_lo, SPLIT["ws2"])
        shared_down_products(0)
        for g in range(1, len(GROUPS)):
            shared_up_products(g)
            shared_down_products(g)
        pe.wait_ge(combine_done, 1)
        for g, (lo, hi) in enumerate(GROUPS):
            for t in range(lo, hi):
                pe.transpose(bank[g][0:NE, 128 * (t - lo):128 * (t - lo) + P], work[:, t, :], ident[0:P, 0:P]).then_inc(combine_turned, 1)
        pe.wait_ge(ffw_loaded, 112)
        for half in range(2):
            product(bank[3][:, half:half + 1],
                    [(wf1_raw[:, k, 128 * half:128 * (half + 1)], b_col[:, k:k + 1]) for k in range(KD)], bf1_mm)
        pe.wait_ge(combineT_done, len(GROUPS))
        pe.wait_ge(shared_done, NT)
        for t in range(NT):
            if t >= 2:
                pe.wait_ge(b2_added, t - 1)
            product(bank[5 + t % 2][0:P, :], [(combineT[:, t, 0:P], b2_sb[:])], b2_mm)
        pe.wait_ge(b2_added, NT)
        pe.wait_ge(bf1_done, 1)

        def up_products(it, n):
            j = W_RING * it + n
            par = n % 2
            if n % 2 == 0:
                v = n // 2
                q = 3 * it + v
                pe.wait_ge(pair_fetched[v], 16 * (it + 1))
                pe.wait_ge(pairT_done, tile_freed(q, 1 if v == 0 else 2))
                for k in range(KD):
                    last = pe.transpose(bank[v % 2][:, 128 * k:128 * (k + 1)], pair_rows[v][:, 128 * k:128 * (k + 1)], ident[:])
                last.then_inc(pair_turned, 1)
                pe.wait_ge(pairT_done, tile_done(q))
            pe.wait_ge(w_loaded[n], 16 * (it + 1))
            pe.wait_ge(up_copied, tile_freed(j, 2))
            for k in range(KD):
                for half in range(2):
                    last = pe.matmul(bank[2 + par][SLOTS * half:SLOTS * (half + 1), 0:128],
                                     pair_rowsT[n // 2][:, k, SLOTS * par:SLOTS * (par + 1)],
                                     w_ring[n][:, k * DFF + 128 * half:k * DFF + 128 * (half + 1)],
                                     start=(k == 0), stop=(k == KD - 1), skip_group_check=True)
            last.then_inc(up_mm, 1)

        def up_transpose(j, par):
            pe.wait_ge(up_copied, tile_done(j))
            pe.wait_ge(up_act, tile_freed(j, 2))
            pe.transpose(bank[4 + par][:, 0:128], up[par][:], ident[:]).then_inc(up_turned, 1)

        def down_products(j, par, n, turn):
            pe.wait_ge(up_act, tile_done(j))
            pe.wait_ge(down_copied, turn)
            for k in range(2):
                for half in range(2):
                    last = pe.matmul(bank[6 + par][SLOTS * half:SLOTS * (half + 1), 0:D // 2], upT[par][:, k, :],
                                     w_ring[n][:, KD * DFF + k * D + half * (D // 2):KD * DFF + k * D + (half + 1) * (D // 2)],
                                     start=(k == 0), stop=(k == 1), skip_group_check=True)
            last.then_inc(down_mm, 1)

        def pe_step(it, first):
            for n in range(W_RING):
                j = W_RING * it + n
                up_products(it, n)
                if not (first and n < 1):
                    up_transpose(j - 1, (n - 1) % 2)
                if not (first and n < 2):
                    down_products(j - 2, n % 2, (n - 2) % W_RING, j - 3 if not (first and n < 4) else 0)

        pe_step(0, True)
        with pe.Fori(1, STEPS) as it:
            pe_step(it, False)
        up_transpose(TILES - 1, 1)
        for j in (TILES - 2, TILES - 1):
            down_products(j, j % 2, j % W_RING, j - 1)
        pe.wait_ge(halves_lo, SPLIT["wf1"])
        pe.wait_ge(halves_lo, SPLIT["wf2"])
        pe.wait_ge(pads_zeroed, 4)
        pe.wait_ge(pairT_done, tile_done(TILES // 2 - 1))
        pe.wait_ge(down_copied, TILES)
        pe.wait_ge(up_act, tile_done(TILES - 1))
        for g, (lo, hi) in enumerate(GROUPS):
            width = (hi - lo) * PW
            for t in range(lo, hi):
                pe.wait_ge(ff_in_done, t + 1)
                if t >= 2:
                    pe.wait_ge(ffT_lo_done, t - 1)
                turn(ff_in[t % 2], t % 2, ff_turned)
            pe.wait_ge(ffT_lo_done, hi)
            for half in range(2):
                if g:
                    pe.wait_ge(ff_act, 2 * (g - 1) + half + 1)
                cols = slice(128 * half, 128 * (half + 1))
                product(bank[2 + half][:, 0:width],
                        split_terms(lambda k: wf1_hi[:, k, cols], lambda k: wf1_lo[:, k, cols],
                                    lambda k: ffT_hi[:, k, 0:hi - lo, :].rearrange("p t c -> p (t c)"),
                                    lambda k: ffT_lo[:, k, 0:hi - lo, :].rearrange("p t c -> p (t c)"), KD), ff_up)
            pe.wait_ge(ff_h_lo_done, 2 * (g + 1))
            for t in range(lo, hi):
                if t >= 2:
                    pe.wait_ge(result_done, t - 1)
                cols = slice((t - lo) * PW, (t - lo) * PW + P)
                product(bank[4 + t % 2][0:P, :],
                        split_terms(lambda k: ff_hT_hi[:, k, cols], lambda k: ff_hT_lo[:, k, cols],
                                    lambda k: wf2_hi[:, k, :], lambda k: wf2_lo[:, k, :], 2), ff_down)

    block.__exit__(None, None, None)


_ORDER = ["x", "src", "dst", "edge_weight", "u", "s", "vt", "gnn_bias", "wqkv_t", "wout_t", "bout", "ln1_g", "ln1_b",
          "wr", "codebook_t", "experts", "b2", "ws1", "bs1_cols", "ws2", "bs2", "ffln_g_cols", "ffln_b_cols", "wf1",
          "bf1_cols", "wf2", "bf2"]


def laid_out(i):
    import numpy as np

    def col(v):
        return v.reshape(-1, 128).T

    w1, w2, b1 = i["L0_ffn_W1"], i["L0_ffn_W2"], i["L0_ffn_b1"]
    experts = np.concatenate([
        w1.reshape(NE, KD, 128, DFF).transpose(0, 2, 1, 3).reshape(NE, 128, KD * DFF),
        w2.reshape(NE, 2, 128, D).transpose(0, 2, 1, 3).reshape(NE, 128, 2 * D),
        b1.reshape(NE, 2, 128).transpose(0, 2, 1)], axis=2)
    row = lambda v: v.reshape(1, -1)
    return {
        "x": i["x"], "src": i["src"].reshape(P, EC), "dst": i["dst"].reshape(P, EC),
        "edge_weight": i["edge_weight"].reshape(P, EC), "u": i["L0_gnn_U"], "s": row(i["L0_gnn_s"]),
        "vt": i["L0_gnn_Vt"], "gnn_bias": row(i["L0_gnn_bias"]), "wqkv_t": i["L0_mix_Wqkv"].T,
        "wout_t": i["L0_mix_Wout"].T, "bout": row(i["L0_mix_bout"]), "ln1_g": row(i["L0_ffn_ln1_g"]),
        "ln1_b": row(i["L0_ffn_ln1_b"]), "wr": i["L0_ffn_Wr"], "codebook_t": i["L0_ffn_codebook"].T,
        "experts": experts, "b2": i["L0_ffn_b2"], "ws1": i["L0_ffn_Ws1"], "bs1_cols": col(i["L0_ffn_bs1"]),
        "ws2": i["L0_ffn_Ws2"], "bs2": row(i["L0_ffn_bs2"]), "ffln_g_cols": col(i["L0_ffn_ffln_g"]),
        "ffln_b_cols": col(i["L0_ffn_ffln_b"]), "wf1": i["L0_ffn_Wf1"], "bf1_cols": col(i["L0_ffn_bf1"]),
        "wf2": i["L0_ffn_Wf2"], "bf2": row(i["L0_ffn_bf2"]),
    }


def kernel(**inputs):
    import numpy as np
    import concourse.bacc as bacc
    from concourse.bass_utils import run_bass_kernel_spmd

    nc = bacc.Bacc("TRN2", target_bir_lowering=False, num_devices=1)
    arrays, args = {}, []
    laid = laid_out({k: np.asarray(v) for k, v in inputs.items()})
    for name in _ORDER:
        a = np.ascontiguousarray(laid[name])
        arrays[f"in_{name}"] = a
        args.append(nc.dram_tensor(f"in_{name}", a.shape, mybir.dt.from_np(a.dtype), kind="ExternalInput").ap())
    args.append(nc.dram_tensor("result", (N, D), F32, kind="ExternalOutput").ap())
    gps_layer(nc, *args)
    r = run_bass_kernel_spmd(nc, [arrays], core_ids=[0])
    return r.results[0]["result"]
```

```python
from contextlib import contextmanager

import concourse.bass as bass
from concourse import mybir

F32 = mybir.dt.float32
F16 = mybir.dt.float16
BF16 = mybir.dt.bfloat16
F32R = mybir.dt.float32r
I32 = mybir.dt.int32
U32 = mybir.dt.uint32
ALU = mybir.AluOpType
ACT = mybir.ActivationFunctionType
AX = mybir.AxisListType

N = 1250
D = 512
E_EDGES = 20000
P = 125
NT = N // P
PW = P + 1
KD = D // 128
RANK = 64
HEADS = 8
PAIRS = HEADS // 2
EC = E_EDGES // P
BC = 8
OH_RING = 4
BANK = 512
EPS = 1e-5

NE = 64
DR = 64
DFF = 256
DSH = 1024
SB = DSH // 128
TEMP = 0.7
SHARED_SCALE = 0.25
SLOTS = 64
TILES = (2 * N + (SLOTS - 1) * NE) // SLOTS
GROUPS = [(0, 4), (4, 7), (7, 10)]

PAIR_TILES = TILES // 2
BODY = 6
STEPS = TILES // BODY
UNSURE = -(-(TILES * SLOTS - 2 * N // SLOTS * SLOTS) // N)
STEPS_MIN = 2 * N // (SLOTS * BODY)
W_RING = 8
W_AHEAD = 2
STORE_LAG = 4
EARLY_LOADS = W_RING // 2
RELAY_LAG = 2
W1_COLS = KD * DFF
B1_AT = W1_COLS + 2 * D
W_COLS = B1_AT + 2

SPLIT = {"u": 1, "wqkv": 1 + KD, "wout": 2 + KD, "vt": 3 + KD, "wr": 4 + KD, "ws1": 5 + KD, "ws2": 6 + KD, "wf1": 7 + KD,
         "wf2": 8 + KD}
MADE_NODES, MADE_FILLS, MADE_IDENT, MADE_BEFORE, MADE_IDS, MADE_ZEROS = 1, 6, 7, 8, 12, 13
MADE_NODE_COLS, MADE_EXPERT_IDS, MADE_EDGES = 1, 3, 6

ZEROED_HT, ZEROED_CTX, ZEROED_FFT = 2, 3, 5
TABLE_ENDS, TABLE_BODIES, TABLE_TILES, TABLE_SLOTS = 1, 2, 3, 4

AHEAD = 2
CHUNK_AHEAD = 32


def done(n):
    return n + 1 + AHEAD


def freed(n, ring=2):
    return n + 1 + AHEAD - ring


def tile_done(j):
    return j + 1 + BODY


def tile_freed(j, ring):
    return j + 1 + BODY - ring


def copied(j):
    return j + 2


def slot_of(expert):
    return (expert + EARLY_LOADS) & (W_RING - 1)


class Steps:

    def __init__(self):
        self.n, self.turns = 0, 0

    def one(self):
        self.n += 1
        return 1

    def now(self):
        return self.n + self.turns

    @contextmanager
    def loop(self, it, count, each):
        start, self.turns = self.n, it * each
        yield
        assert self.n == start + each, self.n - start
        self.n, self.turns = start + each * count, 0


class Region:

    def __init__(self, nc, start, end):
        self.nc, self.at, self.end = nc, start, end

    def place(self, name, shape, dtype=F32):
        size = mybir.dt.size(dtype)
        for n in shape[1:]:
            size *= n
        tensor = self.nc.alloc_sbuf_tensor_at(name, shape, dtype, offset=self.at)
        self.at += (size + 31) // 32 * 32
        assert self.at <= self.end, (name, self.at, self.end)
        return tensor


def gps_layer(nc, x, src, dst, edge_weight, u, s, vt, gnn_bias, wqkv_t, wout_t, bout, ln1_g, ln1_b, wr, codebook_t,
              experts, b2, ws1, bs1_cols, ws2, bs2, ffln_g_cols, ffln_b_cols, wf1, bf1_cols, wf2, bf2, out):
    base = (nc.sbuf_base + 31) // 32 * 32
    top = nc.sbuf_usable_end // 32 * 32

    keep = Region(nc, base, top)
    x_sb = keep.place("x_sb", [P, NT, D])
    ident = keep.place("ident", [128, 128])
    before = keep.place("before", [P, P], BF16)
    ones = keep.place("ones", [P, P], BF16)
    zero_w = keep.place("zero_w", [P, 128], F32R)
    eps_col = keep.place("eps_col", [P, 1])
    stats = keep.place("stats", [P, NT, 6])
    moments = keep.place("moments", [P, NT, 2])
    std = keep.place("std", [P, NT])
    rstd = keep.place("rstd", [P, NT])
    logits = keep.place("logits", [P, NT, NE])
    top_logit = keep.place("top_logit", [P, NT, 8])
    top_expert = keep.place("top_expert", [P, NT, 8], U32)
    expert_id = keep.place("expert_id", [P, NE])
    expert_i32 = keep.place("expert_i32", [P, NE], I32)
    tile_start_i32 = keep.place("tile_start_i32", [P, 1], I32)
    tile_start = keep.place("tile_start", [P, 1])
    token_id = keep.place("token_id", [P, NT], I32)
    picks = keep.place("picks", [P, NT, 2])
    gap = keep.place("gap", [P, NT])
    gate1 = keep.place("gate1", [P, NT])
    gate2 = keep.place("gate2", [P, NT])
    gates_up = keep.place("gates_up", [P, 2, NT])
    slots_f = keep.place("slots_f", [P, 2, NT])
    slots = keep.place("slots", [P, 2, NT], I32)
    slot_low = keep.place("slot_low", [P, 2, NT], I32)
    slot_high = keep.place("slot_high", [P, 2, NT], I32)
    table_at = keep.place("table_at", [P, 2, NT], I32)
    padded_i32 = keep.place("padded_i32", [P, NE], I32)
    padded = keep.place("padded", [P, NE])
    scan = [keep.place(f"scan{i}", [P, NE]) for i in range(2)]
    starts = keep.place("starts", [P, NE])
    tile_expert_f = keep.place("tile_expert_f", [P, 1])
    tile_expert = keep.place("tile_expert", [P, 1], I32)
    tile_expert_row = keep.place("tile_expert_row", [1, P], I32)
    bodies = keep.place("bodies", [P, 2], I32)
    expert_end = keep.place("expert_end", [P, NE], I32)
    slot_token = keep.place("slot_token", [128, PAIR_TILES], I32)
    no_token = keep.place("no_token", [128, PAIR_TILES], I32)
    bs1_sb = keep.place("bs1_sb", [128, SB])
    mid = Region(nc, keep.at, top)
    q_sb = mid.place("q_sb", [P, NT, D])
    agg_sb = mid.place("agg_sb", [128, NT, PW])
    kv = Region(nc, mid.at, top)
    k_sb = kv.place("k_sb", [P, NT, D])
    v_sb = kv.place("v_sb", [P, NT, PAIRS, 130])
    kv_start, kv_end = mid.at, kv.at
    wqkv_raw = Region(nc, kv_start, kv_end).place("wqkv_raw", [128, KD, 3 * D])
    pe_ = Region(nc, kv_end, top)
    wqkv_hi = pe_.place("wqkv_hi", [128, KD, 3 * D], F32R)
    wqkv_lo = pe_.place("wqkv_lo", [128, KD, 3 * D], F32R)
    u_raw = pe_.place("u_raw", [128, KD, RANK])
    u_hl = pe_.place("u_hl", [128, KD, 2 * RANK], F32R)
    s_row = pe_.place("s_row", [P, RANK])
    t_sb = pe_.place("t_sb", [P, NT, RANK])
    xn = [pe_.place(f"xn{i}", [P, D]) for i in range(2)]
    xnt_hi = [pe_.place(f"xnt_hi{i}", [128, KD, PW], F32R) for i in range(2)]
    xnt_lo = [pe_.place(f"xnt_lo{i}", [128, KD, PW], F32R) for i in range(2)]
    node_of_col = pe_.place("node_of_col", [P, NT, PW], F16)
    node_i32 = nc.alloc_sbuf_tensor_at("node_i32", [P, NT, PW], I32, offset=pe_.at)
    onehot = [pe_.place(f"onehot{i}", [P, NT * PW], F32R) for i in range(OH_RING)]
    rows = [pe_.place(f"rows{i}", [P, BC, RANK]) for i in range(2)]
    rows_hl = [pe_.place(f"rows_hl{i}", [P, BC, 2 * RANK], F32R) for i in range(2)]
    q_exp = [pe_.place(f"q_exp{i}", [P, D]) for i in range(2)]
    q_top = pe_.place("q_top", [P, HEADS])
    q_sum = pe_.place("q_sum", [P, HEADS])
    q_inv = pe_.place("q_inv", [P, HEADS])
    k_top = pe_.place("k_top", [P, D])
    dst_sb = pe_.place("dst_sb", [P, EC], I32)
    src_sb = pe_.place("src_sb", [P, EC], I32)
    src_f = pe_.place("src_f", [P, EC])
    weight_sb = pe_.place("weight_sb", [P, EC])
    batch_dst = [pe_.place(f"batch_dst{i}", [P, BC], I32) for i in range(2)]
    late = Region(nc, kv_end, top)
    hT_hi = late.place("hT_hi", [128, KD, NT, PW], F32R)
    hT_lo = late.place("hT_lo", [128, KD, NT, PW], F32R)
    after_hT = late.at
    vt2_raw = late.place("vt2_raw", [128, D])
    vt2_hi = late.place("vt2_hi", [128, D], F32R)
    vt2_lo = late.place("vt2_lo", [128, D], F32R)
    bias_row = late.place("bias_row", [P, D])
    bout_row = late.place("bout_row", [P, D])
    g_row = late.place("g_row", [P, D])
    b_row = late.place("b_row", [P, D])
    wr_raw = late.place("wr_raw", [128, KD, DR])
    wr_hl = late.place("wr_hl", [128, KD, 2 * DR], F32R)
    codebook2 = late.place("codebook2", [128, NE])
    wout_raw = late.place("wout_raw", [128, PAIRS, D])
    wout_hi = late.place("wout_hi", [128, PAIRS, D], F32R)
    wout_lo = late.place("wout_lo", [128, PAIRS, D], F32R)
    m_hi = late.place("m_hi", [128, PAIRS, D], F32R)
    m_lo = late.place("m_lo", [128, PAIRS, D], F32R)
    ctx = late.place("ctx", [128, PAIRS, 128])
    ctxT_hi = late.place("ctxT_hi", [128, PAIRS, 128], F32R)
    ctxT_lo = late.place("ctxT_lo", [128, PAIRS, 128], F32R)
    k_inv = late.place("k_inv", [128, PAIRS])
    k_top_col = late.place("k_top_col", [128, PAIRS])
    k_top_wide = late.place("k_top_wide", [128, PAIRS, P])
    upd = Region(nc, kv_start, kv_end)
    q_tile = [upd.place(f"q_tile{i}", [P, D]) for i in range(2)]
    qT_hi = [upd.place(f"qT_hi{i}", [128, PAIRS, PW], F32R) for i in range(2)]
    qT_lo = [upd.place(f"qT_lo{i}", [128, PAIRS, PW], F32R) for i in range(2)]
    agg_hi = [upd.place(f"agg_hi{i}", [128, PW], F32R) for i in range(2)]
    agg_lo = [upd.place(f"agg_lo{i}", [128, PW], F32R) for i in range(2)]
    mixed = [upd.place(f"mixed{i}", [P, D]) for i in range(2)]
    x1 = [upd.place(f"x1_{i}", [P, D]) for i in range(2)]
    z = [upd.place(f"z{i}", [P, D]) for i in range(2)]
    h_tile = [upd.place(f"h_tile{i}", [P, D]) for i in range(2)]
    rT = [upd.place(f"rT{i}", [128, PW]) for i in range(2)]
    x1_parts = [upd.place(f"x1_parts{i}", [P, 6]) for i in range(2)]
    x1_moments = [upd.place(f"x1_moments{i}", [P, 2]) for i in range(2)]
    x1_std = [upd.place(f"x1_std{i}", [P, 1]) for i in range(2)]
    x1_rstd = [upd.place(f"x1_rstd{i}", [P, 1]) for i in range(2)]
    z_var = [upd.place(f"z_var{i}", [P, 1]) for i in range(2)]
    z_std = [upd.place(f"z_std{i}", [P, 1]) for i in range(2)]
    z_rstd = [upd.place(f"z_rstd{i}", [P, 1]) for i in range(2)]

    zone1 = Region(nc, keep.at, kv_end)
    shared = zone1.place("shared", [P, NT, D])
    after_shared = zone1.at
    ws1_hi = zone1.place("ws1_hi", [128, KD, DSH], F32R)
    ws1_lo = zone1.place("ws1_lo", [128, KD, DSH], F32R)
    shared_h = [zone1.place(f"shared_h{i}", [128, 4 * PW]) for i in range(2)]
    bs2_row = zone1.place("bs2_row", [P, D])
    work = zone1.place("work", [P, NT, NE])
    zone2 = Region(nc, after_hT, top)
    ws2_hi = zone2.place("ws2_hi", [128, SB, D], F32R)
    ws2_lo = zone2.place("ws2_lo", [128, SB, D], F32R)
    ws1_raw = nc.alloc_sbuf_tensor_at("ws1_raw", [128, KD, DSH], F32, offset=zone2.at)
    ws2_raw = nc.alloc_sbuf_tensor_at("ws2_raw", [128, SB, D], F32, offset=zone2.at + 4 * KD * DSH)
    shared_hT_hi = zone2.place("shared_hT_hi", [128, SB, 4 * PW], F32R)
    shared_hT_lo = zone2.place("shared_hT_lo", [128, SB, 4 * PW], F32R)
    zone2.at += 512
    combineT = nc.alloc_sbuf_tensor_at("combineT", [NE, NT, P], F32, offset=zone2.at)
    first_pick = zone2.place("first_pick", [P, NT, NE], BF16)
    second_pick = zone2.place("second_pick", [P, NT, NE], BF16)
    picked_any = zone2.place("picked_any", [P, NT, NE], BF16)
    earlier = zone2.place("earlier", [P, NT + 1, NE], BF16)
    b2_sb = zone2.place("b2_sb", [NE, D])
    slot_all = zone2.place("slot_all", [P, NT, NE])
    moe = Region(nc, after_shared, top)
    wf1_hi = moe.place("wf1_hi", [128, KD, DFF], F32R)
    wf1_lo = moe.place("wf1_lo", [128, KD, DFF], F32R)
    wf2_hi = moe.place("wf2_hi", [128, 2, D], F32R)
    wf2_lo = moe.place("wf2_lo", [128, 2, D], F32R)
    g_col = moe.place("g_col", [128, KD])
    b_col = moe.place("b_col", [128, KD])
    bf1_raw = moe.place("bf1_raw", [128, 2])
    bf1_sb = moe.place("bf1_sb", [128, 2])
    bf2_row = moe.place("bf2_row", [P, D])
    before_loop = Region(nc, moe.at, after_shared + 8 * KD * DSH)
    wf1_raw = before_loop.place("wf1_raw", [128, KD, DFF])
    wf1_g = before_loop.place("wf1_g", [128, KD, DFF])
    wf2_raw = before_loop.place("wf2_raw", [128, 2, D])
    ring_start = moe.at
    w_ring = moe.place("w_ring", [128, W_RING, W_COLS])
    assert ring_start + EARLY_LOADS * W_COLS * 4 >= kv_end and moe.at <= after_hT
    pair_idx = [moe.place(f"pair_idx{i}", [128, 1], I32) for i in range(3)]
    pair_rows = [moe.place("pair_rows0", [128, D])]
    assert moe.at <= after_hT
    pair_rows += [moe.place(f"pair_rows{i}", [128, D]) for i in (1, 2)]
    w_tile = [moe.place(f"w_tile{i}", [128, W_COLS]) for i in range(BODY)]
    pair_rowsT = [moe.place(f"pair_rowsT{i}", [128, KD, 128]) for i in range(3)]
    up = [moe.place(f"up{i}", [128, 128]) for i in range(2)]
    upT = [moe.place(f"upT{i}", [128, 2, SLOTS]) for i in range(2)]
    down = [moe.place(f"down{i}", [128, 2, D // 2]) for i in range(3)]
    last_ = Region(nc, ring_start, ring_start + W_RING * W_COLS * 4)
    eo_first = [last_.place(f"eo_first{i}", [P, D]) for i in range(2)]
    eo_second = [last_.place(f"eo_second{i}", [P, D]) for i in range(2)]
    hmoe = [last_.place(f"hmoe{i}", [P, D]) for i in range(2)]
    ff_in = [last_.place(f"ff_in{i}", [P, D]) for i in range(2)]
    hm_parts = [last_.place(f"hm_parts{i}", [P, 6]) for i in range(2)]
    hm_moments = [last_.place(f"hm_moments{i}", [P, 2]) for i in range(2)]
    hm_std = [last_.place(f"hm_std{i}", [P, 1]) for i in range(2)]
    hm_rstd = [last_.place(f"hm_rstd{i}", [P, 1]) for i in range(2)]
    ffT_hi = last_.place("ffT_hi", [128, KD, 4, PW], F32R)
    ffT_lo = last_.place("ffT_lo", [128, KD, 4, PW], F32R)
    ff_h = [last_.place(f"ff_h{i}", [128, 4 * PW]) for i in range(2)]
    ff_hT_hi = last_.place("ff_hT_hi", [128, 2, 4 * PW], F32R)
    ff_hT_lo = last_.place("ff_hT_lo", [128, 2, 4 * PW], F32R)
    result = [last_.place(f"result{i}", [P, D]) for i in range(2)]

    bank = [nc.alloc_psum_tensor(f"bank{i}", [128, BANK], F32) for i in range(8)]

    t_rows = nc.dram_tensor("t_rows", (N, RANK), F32, kind="Internal").ap()
    h_rows = nc.dram_tensor("h_rows", (N, D), F32, kind="Internal").ap()

    slot_table = nc.dram_tensor("slot_table", (128 * PAIR_TILES, 1), I32, kind="Internal").ap()
    tile_expert_d = nc.dram_tensor("tile_expert_d", (P, 1), I32, kind="Internal").ap()
    expert_rows = nc.dram_tensor("expert_rows", (TILES * SLOTS, D), F32, kind="Internal").ap()

    def sem(name):
        return nc.alloc_semaphore(name)

    def sems(names):
        return [sem(n) for n in names.split()]

    x_loaded = [sem(f"x_loaded{i}") for i in range(NT // 2)]
    wqkv_loaded, edges_loaded = sems(
        "wqkv_loaded edges_loaded")
    moments_done, std_done = sems(
        "moments_done std_done")
    xn_done, xn_turned, xnt_hi_done, xnt_lo_done, t_mm, t_done = sems(
        "xn_done xn_turned xnt_hi_done xnt_lo_done t_mm t_done")
    t_stored, agg_opened, indices_done, chunk_mm, onehot_done = sems(
        "t_stored agg_opened indices_done chunk_mm onehot_done")
    gathered = [sem(f"gathered{i}") for i in range(2)]
    rows_scaled, rows_hi_done, rows_lo_done = sems("rows_scaled rows_hi_done rows_lo_done")
    q_mm, k_mm, v_mm, q_sub_done, q_exp_done = sems(
        "q_mm k_mm v_mm q_sub_done q_exp_done")
    k_top_done, k_copied, v_copied, agg_closed, agg_copied = sems("k_top_done k_copied v_copied agg_closed agg_copied")
    wout_loaded, = sems(
        "wout_loaded")
    k_top_turned, k_top_wide_done, k_top_back, k_sub_done, k_exp_done = sems(
        "k_top_turned k_top_wide_done k_top_back k_sub_done k_exp_done")
    ctx_mm, ctx_done, ctx_turned, ctxT_hi_done, ctxT_lo_done = sems(
        "ctx_mm ctx_done ctx_turned ctxT_hi_done ctxT_lo_done")
    m_mm, m_hi_done, m_lo_done = sems(
        "m_mm m_hi_done m_lo_done")
    xb_done, q_tile_done, q_turned, qT_hi_done, qT_lo_done, agg_hi_done, agg_lo_done, g_mm, y_mm = sems(
        "xb_done q_tile_done q_turned qT_hi_done qT_lo_done agg_hi_done agg_lo_done g_mm y_mm")
    g_sum_done, y_sum_done, x1_done, x1_moments_done, x1_std_done, x1_rstd_done, z_var_done = sems(
        "g_sum_done y_sum_done x1_done x1_moments_done x1_std_done x1_rstd_done z_var_done")
    z_done, z_std_done, z_rstd_done = sems("z_done z_std_done z_rstd_done")
    res_done, h_done, h_turned, hT_hi_done, hT_lo_done, r_mm, rT_done, l_mm, logits_done, picked = sems(
        "res_done h_done h_turned hT_hi_done hT_lo_done r_mm rT_done l_mm logits_done picked")
    zeroed = sem("zeroed")
    gnn_loaded, update_loaded = sems("gnn_loaded update_loaded")
    pair_index_done, x1_parts_done = sems("pair_index_done x1_parts_done")
    made, made_dve, dve_step, halves_hi, halves_lo = sems("made made_dve dve_step halves_hi halves_lo")
    h_stored = [sem(f"h_stored{i}") for i in range(2)]
    ws1_loaded, ws2_loaded = sems("ws1_loaded ws2_loaded")
    earlier_done, gap_done = sems(
        "earlier_done gap_done")
    gap_exp, rank_mm = sems("gap_exp rank_mm")
    tables_done, tile_expert_moved, table_written, table_moved = sems(
        "tables_done tile_expert_moved table_written table_moved")
    shared_up, shared_act, shared_lo_done, shared_down, shared_done = sems(
        "shared_up shared_act shared_lo_done shared_down shared_done")
    combine_done, combine_turned, combineT_done = sems(
        "combine_done combine_turned combineT_done")
    ffw_loaded, wf1_g_done, bf1_mm, bf1_done = sems(
        "ffw_loaded wf1_g_done bf1_mm bf1_done")
    experts_here, w_copied = sems("experts_here w_copied")
    w_loaded = [sem(f"w_loaded{i}") for i in range(W_RING)]
    pair_fetched = [sem(f"pair_fetched{i}") for i in range(3)]
    pair_turned, pairT_done, up_mm, up_copied, up_turned, up_act, down_mm, down_copied = sems(
        "pair_turned pairT_done up_mm up_copied up_turned up_act down_mm down_copied")
    down_stored = [sem(f"down_stored{i}") for i in range(3)]
    eo_fetched = [sem(f"eo_fetched{i}") for i in range(2)]
    hm_done, hm_moments_done, hm_std_done, hm_rstd_done, ff_in_done, hm_kept, bf2_added = sems(
        "hm_done hm_moments_done hm_std_done hm_rstd_done ff_in_done hm_kept bf2_added")
    ff_turned, ffT_hi_done, ffT_lo_done, ff_up, ff_act, ff_h_lo_done, ff_down, result_done = sems(
        "ff_turned ffT_hi_done ffT_lo_done ff_up ff_act ff_h_lo_done ff_down result_done")
    result_stored = [sem(f"result_stored{i}") for i in range(2)]

    x_v = x.rearrange("(p t) d -> p t d", t=NT)
    out_v = out.rearrange("(p t) d -> p t d", t=NT)
    h_rows_v = h_rows.rearrange("(p t) d -> p t d", t=NT)
    WIDE = 112

    def load_tokens(eng, to, of, signal):
        eng.dma_start(to[0:WIDE], of[0:WIDE]).then_inc(signal, 16)
        eng.dma_start(to[WIDE:P], of[WIDE:P]).then_inc(signal, 16)

    def turned(b):
        return bank[b][:, 0:KD * PW].rearrange("p (k c) -> p k c", k=KD)

    block = nc.Block()
    block.__enter__()

    @block.sync
    def _(sp):
        for i in range(NT // 2):
            load_tokens(sp, x_sb[:, 2 * i:2 * i + 2, :], x_v[:, 2 * i:2 * i + 2, :], x_loaded[i])
        sp.dma_start(u_raw[:], u.rearrange("(k p) r -> p k r", p=128)).then_inc(gnn_loaded, 16)
        sp.dma_start(s_row[:], s.partition_broadcast(P)).then_inc(gnn_loaded, 16)
        sp.dma_start(wqkv_raw[:], wqkv_t.rearrange("(k p) c -> p k c", p=128)).then_inc(wqkv_loaded, 16)
        sp.dma_start(src_sb[:], src).then_inc(edges_loaded, 16)
        sp.dma_start(dst_sb[:], dst).then_inc(edges_loaded, 16)
        sp.dma_start(weight_sb[:], edge_weight).then_inc(edges_loaded, 16)
        sp.wait_ge(made, MADE_IDS)
        sp.dma_start(slot_table.rearrange("(p j) a -> p (j a)", p=128), no_token[:]).then_inc(table_moved, 16)
        sp.wait_ge(t_done, done(NT - 1))
        sp.dma_start(t_rows.rearrange("(p t) r -> p t r", t=NT), t_sb[:]).then_inc(t_stored, 16)
        sp.wait_ge(agg_closed, 1)
        sp.dma_start(wout_raw[:], wout_t.rearrange("(k p) c -> p k c", p=128)).then_inc(wout_loaded, 16)
        for i in range(2):
            sp.dma_start(vt2_raw[RANK * i:RANK * (i + 1)], vt).then_inc(update_loaded, 16)
        for to, of in ((bias_row, gnn_bias), (bout_row, bout), (g_row, ln1_g), (b_row, ln1_b)):
            sp.dma_start(to[:], of.partition_broadcast(P)).then_inc(update_loaded, 16)
        sp.dma_start(wr_raw[:], wr.rearrange("(k p) r -> p k r", p=128)).then_inc(update_loaded, 16)
        for i in range(2):
            sp.dma_start(codebook2[DR * i:DR * (i + 1)], codebook_t).then_inc(update_loaded, 16)
        sp.wait_ge(k_top_wide_done, 1)
        for n in range(UNSURE):
            sp.dma_start(expert_rows[TILES * SLOTS - (n + 1) * N:TILES * SLOTS - n * N, :].rearrange("(p t) d -> p t d", t=NT),
                         q_sb[:]).then_inc(table_moved, 16)
        with sp.Fori(0, NT // 2) as it:
            for par in range(2):
                t = 2 * it + par
                sp.wait_ge(h_done, done(t))
                sp.dma_start(h_rows_v[:, t, :], h_tile[par][:]).then_inc(h_stored[par], 16)
        for par in range(2):
            sp.wait_ge(h_stored[par], 16 * (NT // 2))
        sp.wait_ge(picked, NT)
        sp.wait_ge(l_mm, done(NT - 1))
        sp.dma_start(ws1_raw[:], ws1.rearrange("(k p) f -> p k f", p=128)).then_inc(ws1_loaded, 16)
        sp.dma_start(ws2_raw[:], ws2.rearrange("(k p) f -> p k f", p=128)).then_inc(ws2_loaded, 16)
        sp.dma_start(bs1_sb[:], bs1_cols).then_inc(ws2_loaded, 16)
        sp.dma_start(bs2_row[:], bs2.partition_broadcast(P)).then_inc(ws2_loaded, 16)
        sp.dma_start(b2_sb[:], b2).then_inc(ws2_loaded, 16)
        sp.wait_ge(tables_done, TABLE_TILES)
        sp.dma_start(tile_expert_d, tile_expert[:]).then_inc(tile_expert_moved, 16)
        sp.wait_ge(tile_expert_moved, 16)
        sp.dma_start(tile_expert_row[:], tile_expert_d.rearrange("p a -> a p")).then_inc(tile_expert_moved, 16)
        sp.wait_ge(table_written, 16 * 2 * NT)
        sp.dma_start(slot_token[:], slot_table.rearrange("(p j) a -> p (j a)", p=128)).then_inc(table_moved, 16)
        sp.wait_ge(shared_up, len(GROUPS) * SB)
        for to, of in ((wf1_raw, wf1.rearrange("(k p) f -> p k f", p=128)), (wf2_raw, wf2.rearrange("(k p) f -> p k f", p=128)),
                       (g_col, ffln_g_cols), (b_col, ffln_b_cols), (bf1_raw, bf1_cols), (bf2_row, bf2.partition_broadcast(P))):
            sp.dma_start(to[:], of).then_inc(ffw_loaded, 16)
        for e in range(EARLY_LOADS):
            sp.dma_start(w_ring[:, slot_of(e), :], experts[e]).then_inc(w_loaded[e], 16)
        sp.wait_ge(shared_done, NT)
        sp.wait_ge(halves_lo, SPLIT["wf2"])
        sp.wait_ge(bf1_done, 1)
        sp.wait_ge(tables_done, TABLE_ENDS)

        def relay(e, turn):
            sp.wait_ge(w_loaded[e], 16 * turn)
            sp.sem_inc(experts_here, 1)

        for e in range(EARLY_LOADS, W_RING):
            sp.dma_start(w_ring[:, slot_of(e), :], experts[e]).then_inc(w_loaded[e], 16)
        for e in range(W_RING - RELAY_LAG):
            relay(e, 1)
        with sp.Fori(1, NE // W_RING) as it:
            for e in range(W_RING):
                end = sp.value_load(expert_end[0:1, bass.ds(W_RING * it + (e - W_RING), 1)], min_val=0, max_val=TILES)
                sp.wait_ge(w_copied, end + 1)
                sp.dma_start(w_ring[:, slot_of(e), :], experts[bass.ds(W_RING * it + e, 1), :, :].rearrange("a p c -> p (a c)")
                             ).then_inc(w_loaded[e], 16)
                if e < RELAY_LAG:
                    relay(e - RELAY_LAG + W_RING, it)
                else:
                    relay(e - RELAY_LAG, it + 1)
        for e in range(W_RING - RELAY_LAG, W_RING):
            relay(e, NE // W_RING)
        for t in range(NT):
            sp.wait_ge(result_done, t + 1)
            load_tokens(sp, out_v[:, t, :], result[t % 2], result_stored[t % 2])
        for par in range(2):
            sp.wait_ge(result_stored[par], 32 * (NT // 2))

    @block.gpsimd
    def _(pool):
        pool.sem_inc(res_done, AHEAD)
        pool.sem_inc(pair_index_done, 3)

        def keep_hm(t):
            pool.wait_ge(hm_done, t + 1)
            pool.wait_ge(bf2_added, t + 1)
            pool.tensor_tensor(x_sb[:, t, :], x_sb[:, t, :], hmoe[t % 2][:], ALU.add).then_inc(hm_kept, 1)

        pool.iota(node_i32[:], [[1, NT], [NT, PW]], base=0, channel_multiplier=0).then_inc(made, 1)
        pool.memset(ident[:], 0.0).then_inc(made, 1)
        pool.memset(before[:], 0.0).then_inc(made, 1)
        pool.memset(ones[:], 1.0).then_inc(made, 1)
        pool.memset(eps_col[:], EPS).then_inc(made, 1)
        pool.memset(zero_w[:].bitcast(F32), 0.0).then_inc(made, 1)
        pool.wait_ge(made, MADE_FILLS)
        pool.affine_select(out=ident[:], in_=ident[:], compare_op=ALU.not_equal, fill=1.0, base=0,
                           pattern=[[-1, 128]], channel_multiplier=1).then_inc(made, 1)
        pool.affine_select(out=before[:], in_=before[:], compare_op=ALU.is_ge, fill=1.0, base=0,
                           pattern=[[-1, P]], channel_multiplier=1).then_inc(made, 1)
        pool.iota(expert_i32[:], [[1, NE]], base=0, channel_multiplier=0).then_inc(made, 1)
        pool.iota(tile_start_i32[:], [[0, 1]], base=0, channel_multiplier=SLOTS).then_inc(made, 1)
        pool.iota(token_id[:], [[1, NT]], base=0, channel_multiplier=NT).then_inc(made, 1)
        pool.memset(no_token[:], 0).then_inc(made, 1)
        pool.wait_ge(made_dve, MADE_NODE_COLS)
        pool.memset(onehot[0][:].bitcast(F32), 0.0).then_inc(made, 1)
        pool.wait_ge(edges_loaded, 48)
        with pool.Fori(0, NT // 2) as it:
            for step in range(4):
                half = step % 2
                batch = 4 * it + step
                pool.wait_ge(rows_lo_done, freed(batch))
                pool.tensor_copy(batch_dst[half][:], dst_sb[:, bass.ds(batch * BC, BC)]).then_inc(indices_done, 1)
                pool.wait_ge(t_stored, 16)
                pool.wait_ge(indices_done, batch + 1)
                for c in range(BC):
                    pool.indirect_dma_start(rows[half][:, c, :], None, t_rows,
                                            bass.IndirectOffsetOnAxis(ap=batch_dst[half][:, c:c + 1], axis=0)
                                            ).then_inc(gathered[half], 16)
        pool.wait_ge(halves_lo, SPLIT["wqkv"])
        pool.wait_ge(update_loaded, 144)
        pool.wait_ge(agg_closed, 1)
        pool.memset(hT_hi[:, :, :, P:PW].bitcast(F32), 0.0).then_inc(zeroed, 1)
        pool.memset(hT_lo[:, :, :, P:PW].bitcast(F32), 0.0).then_inc(zeroed, 1)
        pool.memset(ctx[:], 0.0).then_inc(zeroed, 1)
        with pool.Fori(0, NT) as t:
            pool.tensor_tensor(x_sb[:, t, :], x_sb[:, t, :], bout_row[:], ALU.add).then_inc(xb_done, 1)
        with pool.Fori(0, NT // 2) as it:
            for par in range(2):
                t = 2 * it + par
                pool.wait_ge(z_done, done(t))
                pool.wait_ge(x1_done, done(t))
                pool.tensor_tensor(x_sb[:, t, :], x1[par][:], z[par][:], ALU.add).then_inc(res_done, 1)
        pool.wait_ge(table_moved, 16 * (1 + UNSURE))
        pool.wait_ge(tables_done, TABLE_SLOTS)
        for which in range(2):
            for t in range(NT):
                pool.indirect_dma_start(slot_table, bass.IndirectOffsetOnAxis(ap=table_at[:, which, t:t + 1], axis=0),
                                        token_id[:, t:t + 1], None).then_inc(table_written, 16)
        pool.wait_ge(shared_up, len(GROUPS) * SB)
        pool.wait_ge(table_moved, 16 * (2 + UNSURE))

        def fetch_pair(q, v):
            pool.wait_ge(pair_turned, tile_freed(q, 3))
            pool.tensor_copy(pair_idx[v][:], slot_token[:, bass.ds(q, 1)]).then_inc(pair_index_done, 1)
            pool.wait_ge(table_moved, 16 * (2 + UNSURE))
            pool.wait_ge(pair_index_done, q + 4)
            pool.indirect_dma_start(pair_rows[v][:], None, h_rows,
                                    bass.IndirectOffsetOnAxis(ap=pair_idx[v][:], axis=0)).then_inc(pair_fetched[v], 16)

        def store_pair(q, v):
            for par in range(2):
                j = 2 * q + par
                pool.wait_ge(down_copied, j + 1)
                pool.dma_start(expert_rows[bass.ds(j * SLOTS, SLOTS), :].rearrange("s (h c) -> h s c", h=2),
                               down[v][:, par, :]).then_inc(down_stored[v], 16)

        pool.wait_ge(tables_done, TABLE_BODIES)
        run = pool.value_load(bodies[0:1, 0:1], min_val=STEPS_MIN, max_val=STEPS)
        run_less_one = pool.value_load(bodies[0:1, 1:2], min_val=STEPS_MIN - 1, max_val=STEPS - 1)
        fetch_pair(0, 0)
        pool.wait_ge(ffw_loaded, 96)
        pool.wait_ge(res_done, done(NT - 1))
        for t in range(NT):
            pool.tensor_tensor(x_sb[:, t, :], x_sb[:, t, :], bf2_row[:], ALU.add).then_inc(bf2_added, 1)
        pool.wait_ge(shared_done, NT)
        for q in range(1, 6):
            fetch_pair(q, q % 3)
            if q >= STORE_LAG:
                store_pair(q - STORE_LAG, (q - STORE_LAG) % 3)
        with pool.Fori(2, STEPS) as it:
            with pool.If(it <= run):
                for v in range(3):
                    fetch_pair(3 * it + v, v)
                    store_pair(3 * it + v - STORE_LAG, (v - STORE_LAG) % 3)
        with pool.If(run >= STEPS):
            for q in range(TILES // 2 - STORE_LAG, TILES // 2):
                store_pair(q, q % 3)
            for v in range(3):
                pool.wait_ge(down_stored[v], 32 * STEPS)
        with pool.If(run < STEPS):
            for v, stored in enumerate((run, run, run_less_one)):
                pool.wait_ge(down_stored[v], 32 * stored)
        pool.wait_ge(w_copied, copied(TILES - 1))
        pool.memset(ffT_hi[:, :, :, P:PW].bitcast(F32), 0.0).then_inc(zeroed, 1)
        pool.memset(ffT_lo[:, :, :, P:PW].bitcast(F32), 0.0).then_inc(zeroed, 1)
        for t in range(NT):
            if t >= 2:
                pool.wait_ge(hm_done, t - 1)
            for which, to in ((0, eo_first), (1, eo_second)):
                pool.indirect_dma_start(to[t % 2][:], None, expert_rows,
                                        bass.IndirectOffsetOnAxis(ap=slots[:, which, t:t + 1], axis=0)).then_inc(eo_fetched[t % 2], 16)
            if t >= 1:
                keep_hm(t - 1)
        keep_hm(NT - 1)

    @block.scalar
    def _(act):
        for signal in (xnt_hi_done, rows_scaled, rows_hi_done, q_exp_done, k_copied, v_copied,
                       q_tile_done, qT_hi_done, agg_hi_done, hT_hi_done, rT_done, x1_std_done, z_std_done):
            act.sem_inc(signal, AHEAD)
        for signal in (up_act, pairT_done):
            act.sem_inc(signal, BODY)
        act.wait_ge(gnn_loaded, 32)
        act.activation(u_hl[:, :, 0:RANK], u_raw[:], ACT.Copy).then_inc(halves_hi, 1)
        act.wait_ge(moments_done, NT)
        act.wait_ge(made, MADE_FILLS)
        act.activation(std[:], moments[:, :, 1], ACT.Sqrt, bias=eps_col[:]).then_inc(std_done, 1)

        with act.Fori(0, NT // 2) as it:
            for par in range(2):
                t = 2 * it + par
                act.wait_ge(xn_turned, done(t))
                act.wait_ge(t_mm, freed(t))
                act.activation(xnt_hi[par][:, :, 0:P], turned(6 + par)[:, :, 0:P], ACT.Copy).then_inc(xnt_hi_done, 1)
        act.wait_ge(wqkv_loaded, 16)
        for k in range(KD):
            act.activation(wqkv_hi[:, k, :], wqkv_raw[:, k, :], ACT.Copy).then_inc(halves_hi, 1)
        act.wait_ge(halves_lo, SPLIT["wqkv"])

        def scale_rows(batch, half, turn):
            act.wait_ge(gathered[half], 16 * BC * (turn + 1))
            for c in range(BC):
                last = act.activation(rows[half][:, c, :], rows[half][:, c, :], ACT.Copy,
                                      scale=weight_sb[:, bass.ds(batch * BC + c, 1)])
            last.then_inc(rows_scaled, 1)
            act.wait_ge(rows_scaled, done(batch))
            act.wait_ge(chunk_mm, BC * (batch - 1) + CHUNK_AHEAD)
            act.activation(rows_hl[half][:, :, 0:RANK], rows[half][:], ACT.Copy).then_inc(rows_hi_done, 1)

        act.wait_ge(t_mm, done(NT - 1))
        act.wait_ge(edges_loaded, 48)
        act.wait_ge(made_dve, MADE_EDGES)

        def xnt_high(t, par):
            act.wait_ge(xn_turned, done(NT + t))
            act.wait_ge(v_mm, freed(t))
            act.activation(xnt_hi[par][:, :, 0:P], turned(6 + par)[:, :, 0:P], ACT.Copy).then_inc(xnt_hi_done, 1)

        def act_tiles(it, final=False):
            for par in range(2):
                t = 2 * it + par
                more = not (final and par)
                scale_rows(2 * t + 1, 1, t)
                act.wait_ge(q_sub_done, done(t))
                act.activation(q_exp[par][:], q_exp[par][:], ACT.Exp).then_inc(q_exp_done, 1)
                if more:
                    xnt_high(t + 1, 1 - par)
                act.wait_ge(k_mm, done(t))
                act.activation(k_sb[:, t, :], bank[4][0:P, :], ACT.Copy).then_inc(k_copied, 1)
                if more:
                    scale_rows(2 * t + 2, 0, t + 1)
                act.wait_ge(v_mm, done(t))
                act.activation(v_sb[:, t, :, 0:128], bank[5][0:P, :].rearrange("p (a c) -> p a c", a=PAIRS),
                               ACT.Copy).then_inc(v_copied, 1)

        xnt_high(0, 0)
        scale_rows(0, 0, 0)
        with act.Fori(0, NT // 2 - 1) as it:
            act_tiles(it)
        act_tiles(NT // 2 - 1, final=True)
        act.wait_ge(agg_closed, 1)
        for b, (lo, hi) in enumerate(GROUPS):
            act.activation(agg_sb[:, lo:hi, :], bank[b][:, 0:(hi - lo) * PW].rearrange("p (t c) -> p t c", c=PW),
                           ACT.Copy).then_inc(agg_copied, 1)
        act.wait_ge(wout_loaded, 16)
        act.activation(wout_hi[:], wout_raw[:], ACT.Copy).then_inc(halves_hi, 1)
        act.wait_ge(update_loaded, 144)
        act.activation(vt2_hi[:], vt2_raw[:], ACT.Copy).then_inc(halves_hi, 1)
        act.wait_ge(update_loaded, 144)
        act.activation(wr_hl[:, :, 0:DR], wr_raw[:], ACT.Copy).then_inc(halves_hi, 1)
        with act.Fori(0, NT) as t:
            act.wait_ge(k_sub_done, t + 1)
            act.activation(k_sb[:, t, :], k_sb[:, t, :], ACT.Exp).then_inc(k_exp_done, 1)
        act.wait_ge(ctx_turned, 1)
        act.activation(ctxT_hi[:], bank[5][:, :].rearrange("p (a c) -> p a c", a=PAIRS), ACT.Copy).then_inc(ctxT_hi_done, 1)
        for pair in range(PAIRS):
            act.wait_ge(m_mm, pair + 1)
            act.activation(m_hi[:, pair, :], bank[(3, 4, 6, 7)[pair]][:, :], ACT.Copy).then_inc(m_hi_done, 1)
        with act.Fori(0, NT // 2) as it:
            for par in range(2):
                t = 2 * it + par
                act.wait_ge(q_turned, freed(t))
                act.activation(q_tile[par][:], q_sb[:, t, :], ACT.Copy).then_inc(q_tile_done, 1)
                act.wait_ge(g_mm, freed(t))
                act.activation(agg_hi[par][:], agg_sb[:, t, :], ACT.Copy).then_inc(agg_hi_done, 1)
            for par in range(2):
                t = 2 * it + par
                act.wait_ge(q_turned, done(t))
                act.wait_ge(y_mm, freed(t))
                act.activation(qT_hi[par][:, :, 0:P], turned(7 * par)[:, :, 0:P], ACT.Copy).then_inc(qT_hi_done, 1)
            for par in range(2):
                t = 2 * it + par
                act.wait_ge(x1_moments_done, done(t))
                act.wait_ge(x1_rstd_done, freed(t))
                act.activation(x1_std[par][:], x1_moments[par][:, 1:2], ACT.Sqrt, bias=eps_col[:]).then_inc(x1_std_done, 1)
            for par in range(2):
                t = 2 * it + par
                act.wait_ge(z_var_done, done(t))
                act.wait_ge(z_rstd_done, freed(t))
                act.activation(z_std[par][:], z_var[par][:], ACT.Sqrt, bias=eps_col[:]).then_inc(z_std_done, 1)
            for par in range(2):
                t = 2 * it + par
                act.wait_ge(h_turned, done(t))
                act.activation(hT_hi[:, :, t, 0:P], turned(7 * par)[:, :, 0:P], ACT.Copy).then_inc(hT_hi_done, 1)
            for par in range(2):
                t = 2 * it + par
                act.wait_ge(r_mm, done(t))
                act.wait_ge(l_mm, freed(t))
                act.activation(rT[par][:], bank[3 + par][:, 0:PW], ACT.Copy).then_inc(rT_done, 1)

        act.wait_ge(ws1_loaded, 16)
        act.activation(ws1_hi[:], ws1_raw[:], ACT.Copy).then_inc(halves_hi, 1)
        act.wait_ge(ws2_loaded, 64)
        act.activation(ws2_hi[:], ws2_raw[:], ACT.Copy).then_inc(halves_hi, 1)
        act.wait_ge(gap_done, 1)
        act.activation(gap[:], gap[:], ACT.Exp).then_inc(gap_exp, 1)
        act.wait_ge(ws2_loaded, 64)
        for g, (lo, hi) in enumerate(GROUPS):
            for fb in range(SB):
                n = g * SB + fb
                act.wait_ge(shared_up, n + 1)
                if n >= 2:
                    act.wait_ge(shared_lo_done, n - 1)
                act.activation(shared_h[fb % 2][:, 0:(hi - lo) * PW], bank[3 + fb % 2][:, 0:(hi - lo) * PW], ACT.Silu,
                               bias=bs1_sb[:, fb:fb + 1]).then_inc(shared_act, 1)
            if g == 0:
                act.wait_ge(combine_turned, NT)
                for n, (first, end) in enumerate(GROUPS):
                    act.activation(combineT[:, first:end, :], bank[n][0:NE, 0:128 * (end - first)].rearrange("p (t c) -> p t c", c=128)[:, :, 0:P],
                                   ACT.Copy).then_inc(combineT_done, 1)
        act.wait_ge(wf1_g_done, KD)
        act.activation(wf1_hi[:], wf1_g[:], ACT.Copy).then_inc(halves_hi, 1)
        act.activation(wf2_hi[:], wf2_raw[:], ACT.Copy).then_inc(halves_hi, 1)

        def take_down(j, n, turn):
            v, par = n // 2, n % 2
            act.wait_ge(down_mm, tile_done(j))
            if par == 0:
                act.wait_ge(down_stored[v], 32 * turn)
            act.activation(down[v][:, par, :], bank[6 + par][:, 0:D // 2], ACT.Copy).then_inc(down_copied, 1)

        def turn_pair(q, v):
            act.wait_ge(pair_turned, tile_done(q))
            act.wait_ge(up_mm, tile_freed(2 * q, BODY))
            act.activation(pair_rowsT[v][:], bank[v % 2][:, :].rearrange("p (k c) -> p k c", k=KD), ACT.Copy).then_inc(pairT_done, 1)

        def act_step(it, first=False, final=False):
            for n in range(BODY):
                j = BODY * it + n
                par = n % 2
                if n % 2 == 0 and not (final and n + 2 == BODY):
                    v = n // 2 + 1
                    turn_pair(BODY // 2 * it + v, v % 3)
                act.wait_ge(up_turned, tile_done(j))
                act.wait_ge(down_mm, tile_freed(j, 2))
                act.wait_ge(w_copied, copied(j))
                for half in range(2):
                    last = act.activation(upT[par][:, half, :], bank[4 + par][:, SLOTS * half:SLOTS * (half + 1)], ACT.Silu,
                                          bias=w_tile[n][:, B1_AT + half:B1_AT + half + 1])
                last.then_inc(up_act, 1)
                if not (first and n == 0):
                    take_down(j - 1, (n - 1) % BODY, it)

        def act_skip(it, final=False):
            act.wait_ge(pairT_done, tile_done(BODY // 2 * it))
            act.sem_inc(pairT_done, BODY // 2 - final)
            act.wait_ge(up_act, tile_done(BODY * it - 1))
            act.sem_inc(up_act, BODY)
            act.wait_ge(down_copied, BODY * it - 1)
            act.sem_inc(down_copied, BODY + final)

        turn_pair(0, 0)
        act.wait_ge(tables_done, TABLE_BODIES)
        run = act.value_load(bodies[0:1, 0:1], min_val=STEPS_MIN, max_val=STEPS)
        act_step(0, first=True)
        with act.Fori(1, STEPS - 1) as it:
            with act.If(it < run):
                act_step(it)
            with act.If(it >= run):
                act_skip(it)
        with act.If(run >= STEPS):
            act_step(STEPS - 1, final=True)
            take_down(TILES - 1, BODY - 1, STEPS - 1)
        with act.If(run < STEPS):
            act_skip(STEPS - 1, final=True)
        for g, (lo, hi) in enumerate(GROUPS):
            for t in range(lo, hi):
                act.wait_ge(hm_moments_done, t + 1)
                if t >= 2:
                    act.wait_ge(hm_rstd_done, t - 1)
                act.activation(hm_std[t % 2][:], hm_moments[t % 2][:, 1:2], ACT.Sqrt, bias=eps_col[:]).then_inc(hm_std_done, 1)
                act.wait_ge(ff_turned, t + 1)
                if g >= 1:
                    act.wait_ge(ff_up, 2 * g)
                act.activation(ffT_hi[:, :, t - lo, 0:P], turned(t % 2)[:, :, 0:P], ACT.Copy).then_inc(ffT_hi_done, 1)
            for half in range(2):
                act.wait_ge(ff_up, 2 * g + half + 1)
                if g >= 1:
                    act.wait_ge(ff_h_lo_done, 2 * g + half - 1)
                act.activation(ff_h[half][:, 0:(hi - lo) * PW], bank[2 + half][:, 0:(hi - lo) * PW], ACT.Silu,
                               bias=bf1_sb[:, half:half + 1]).then_inc(ff_act, 1)

    @block.vector
    def _(dve):
        for signal in (xn_done, xnt_lo_done, t_done, rows_lo_done, q_sub_done, k_top_done, qT_lo_done,
                       agg_lo_done, g_sum_done, y_sum_done, x1_done, x1_parts_done, x1_moments_done, z_var_done, x1_rstd_done, z_done, z_rstd_done,
                       h_done, hT_lo_done, logits_done):
            dve.sem_inc(signal, AHEAD)
        dve.sem_inc(up_copied, BODY)
        dve.sem_inc(w_copied, 1)
        own = Steps()
        dve.wait_ge(made, MADE_NODES)
        dve.tensor_copy(node_of_col[:], node_i32[:]).then_inc(made_dve, 1)
        dve.wait_ge(made, MADE_IDS)
        dve.tensor_copy(expert_id[:], expert_i32[:]).then_inc(made_dve, 1)
        dve.tensor_copy(tile_start[:], tile_start_i32[:]).then_inc(made_dve, 1)
        for t in range(NT):
            if t % 2 == 0:
                dve.wait_ge(x_loaded[t // 2], 32)
            dve.bn_stats(stats[:, t, :], x_sb[:, t, :]).then_inc(dve_step, own.one())
        for t in range(NT):
            dve.wait_ge(dve_step, own.now())
            dve.bn_aggr(moments[:, t, :], stats[:, t, :]).then_inc(moments_done, 1)
        dve.wait_ge(std_done, 1)
        dve.reciprocal(rstd[:], std[:]).then_inc(dve_step, own.one())
        dve.wait_ge(halves_hi, SPLIT["u"])
        dve.tensor_tensor(u_hl[:, :, RANK:2 * RANK], u_raw[:], u_hl[:, :, 0:RANK].bitcast(F32),
                          ALU.subtract).then_inc(halves_lo, 1)
        dve.wait_ge(dve_step, own.now())
        dve.wait_ge(gnn_loaded, 32)

        def normed(t, par, item):
            dve.wait_ge(xn_turned, freed(item))
            dve.tensor_scalar(xn[par][:], x_sb[:, t, :], moments[:, t, 0:1], rstd[:, bass.ds(t, 1)],
                              ALU.subtract, ALU.mult).then_inc(xn_done, 1)

        def xnt_low(par, item):
            dve.wait_ge(xnt_hi_done, done(item))
            dve.tensor_tensor(xnt_lo[par][:, :, 0:P], turned(6 + par)[:, :, 0:P],
                              xnt_hi[par][:, :, 0:P].bitcast(F32), ALU.subtract).then_inc(xnt_lo_done, 1)

        with dve.Fori(0, NT // 2) as it, own.loop(it, NT // 2, 4):
            for par in range(2):
                normed(2 * it + par, par, 2 * it + par)
            for par in range(2):
                xnt_low(par, 2 * it + par)
            for par in range(2):
                t = 2 * it + par
                dve.wait_ge(t_mm, done(t))
                dve.tensor_copy(t_sb[:, t, :], bank[4 + par][0:P, 0:RANK]).then_inc(dve_step, own.one())
                dve.wait_ge(dve_step, own.now())
                dve.tensor_tensor(t_sb[:, t, :], t_sb[:, t, :], bank[4 + par][0:P, RANK:2 * RANK], ALU.add).then_inc(dve_step, own.one())
                dve.wait_ge(dve_step, own.now())
                dve.tensor_tensor(t_sb[:, t, :], t_sb[:, t, :], s_row[:], ALU.mult).then_inc(t_done, 1)
        for k in range(KD):
            dve.wait_ge(halves_hi, SPLIT["wqkv"] - KD + k + 1)
            dve.tensor_tensor(wqkv_lo[:, k, :], wqkv_raw[:, k, :], wqkv_hi[:, k, :].bitcast(F32),
                              ALU.subtract).then_inc(halves_lo, 1)
        dve.wait_ge(edges_loaded, 48)
        dve.tensor_copy(src_f[:], src_sb[:]).then_inc(made_dve, 1)
        dve.wait_ge(halves_lo, SPLIT["wqkv"])
        dve.memset(v_sb[:, :, :, 128:130], 1.0).then_inc(made_dve, 1)
        dve.memset(k_top[:], -3.0e38).then_inc(made_dve, 1)
        dve.wait_ge(made_dve, MADE_EDGES)
        dve.wait_ge(agg_opened, 1)

        def onehots(batch, half, first, last):
            for c in range(first, last):
                chunk = batch * BC + c
                dve.wait_ge(chunk_mm, chunk + 1 - OH_RING + CHUNK_AHEAD)
                dve.tensor_scalar(onehot[(half * BC + c) % OH_RING][:], node_of_col[:].rearrange("p t c -> p (t c)"),
                                  src_f[:, bass.ds(chunk, 1)], None, ALU.is_equal).then_inc(onehot_done, 1)

        def rows_low(batch, half):
            dve.wait_ge(rows_hi_done, done(batch))
            dve.tensor_tensor(rows_hl[half][:, :, RANK:2 * RANK], rows[half][:],
                              rows_hl[half][:, :, 0:RANK].bitcast(F32), ALU.subtract).then_inc(rows_lo_done, 1)

        def softmax_q_start(t, par):
            psq = bank[3][0:P, :].rearrange("p (h c) -> p h c", h=HEADS)
            dve.wait_ge(q_mm, done(t))
            dve.reduce_max(q_top[:], psq, AX.X).then_inc(dve_step, own.one())
            dve.wait_ge(dve_step, own.now())
            dve.tensor_tensor(q_exp[par][:].rearrange("p (h c) -> p h c", h=HEADS), psq,
                              q_top[:].unsqueeze(2).broadcast_to([P, HEADS, RANK]), ALU.subtract).then_inc(q_sub_done, 1)

        def softmax_q_end(t, par):
            qe = q_exp[par][:].rearrange("p (h c) -> p h c", h=HEADS)
            dve.wait_ge(q_exp_done, done(t))
            dve.reduce_sum(q_sum[:], qe, AX.X).then_inc(dve_step, own.one())
            dve.wait_ge(dve_step, own.now())
            dve.reciprocal(q_inv[:], q_sum[:]).then_inc(dve_step, own.one())
            dve.wait_ge(dve_step, own.now())
            dve.tensor_tensor(q_sb[:, t, :].rearrange("p (h c) -> p h c", h=HEADS), qe,
                              q_inv[:].unsqueeze(2).broadcast_to([P, HEADS, RANK]), ALU.mult).then_inc(dve_step, own.one())

        def dve_edge_tiles(it, final=False):
            for par in range(2):
                t = 2 * it + par
                more = not (final and par)
                for c in range(2 * BC):
                    onehots(2 * t + c // BC, c // BC, c % BC, c % BC + 1)
                    if c == 1 and more:
                        normed(t + 1, 1 - par, NT + t + 1)
                    if c == 5:
                        rows_low(2 * t + 1, 1)
                    if c == 8:
                        softmax_q_start(t, par)
                    if c == 11 and more:
                        xnt_low(1 - par, NT + t + 1)
                    if c == 12:
                        softmax_q_end(t, par)
                    if c == 13:
                        dve.wait_ge(k_top_done, freed(t, 1))
                        dve.wait_ge(k_copied, done(t))
                        dve.tensor_tensor(k_top[:], k_top[:], k_sb[:, t, :], ALU.max).then_inc(k_top_done, 1)
                    if c == 14 and more:
                        rows_low(2 * t + 2, 0)

        normed(0, 0, NT)
        xnt_low(0, NT)
        rows_low(0, 0)
        with dve.Fori(0, NT // 2 - 1) as it, own.loop(it, NT // 2 - 1, 8):
            dve_edge_tiles(it)
        dve_edge_tiles(NT // 2 - 1, final=True)
        dve.wait_ge(agg_closed, 1)
        dve.wait_ge(k_top_turned, 1)
        dve.reduce_max(k_top_col[:], turned(6)[:, :, 0:P], AX.X).then_inc(dve_step, own.one())
        dve.wait_ge(dve_step, own.now())
        dve.tensor_copy(k_top_wide[:], k_top_col[:].unsqueeze(2).broadcast_to([128, PAIRS, P])).then_inc(k_top_wide_done, 1)
        dve.wait_ge(k_copied, done(NT - 1))
        dve.wait_ge(k_top_back, 1)
        with dve.Fori(0, NT) as t:
            dve.tensor_tensor(k_sb[:, t, :], k_sb[:, t, :], bank[7][0:P, :], ALU.subtract).then_inc(k_sub_done, 1)
        dve.wait_ge(halves_hi, SPLIT["wout"])
        dve.tensor_tensor(wout_lo[:], wout_raw[:], wout_hi[:].bitcast(F32), ALU.subtract).then_inc(halves_lo, 1)
        dve.wait_ge(halves_hi, SPLIT["vt"])
        dve.tensor_tensor(vt2_lo[:], vt2_raw[:], vt2_hi[:].bitcast(F32), ALU.subtract).then_inc(halves_lo, 1)
        dve.wait_ge(halves_hi, SPLIT["wr"])
        dve.tensor_tensor(wr_hl[:, :, DR:2 * DR], wr_raw[:], wr_hl[:, :, 0:DR].bitcast(F32),
                          ALU.subtract).then_inc(halves_lo, 1)
        dve.wait_ge(ctx_mm, PAIRS)
        dve.wait_ge(zeroed, ZEROED_CTX)
        for pair in range(PAIRS):
            at = 132 * (pair % 2)
            dve.reciprocal(k_inv[:, pair:pair + 1], bank[3 + pair // 2][:, at + 128:at + 129]).then_inc(dve_step, own.one())
        dve.wait_ge(dve_step, own.now())
        for pair in range(PAIRS):
            at = 132 * (pair % 2)
            for h in range(2):
                part = slice(64 * h, 64 * (h + 1))
                dve.tensor_scalar(ctx[part, pair, part], bank[3 + pair // 2][part, at + 64 * h:at + 64 * (h + 1)],
                                  k_inv[part, pair:pair + 1], None, ALU.mult).then_inc(ctx_done, 1)
        dve.wait_ge(ctxT_hi_done, 1)
        dve.tensor_tensor(ctxT_lo[:], bank[5][:, :].rearrange("p (a c) -> p a c", a=PAIRS), ctxT_hi[:].bitcast(F32),
                          ALU.subtract).then_inc(ctxT_lo_done, 1)
        for pair in range(PAIRS):
            dve.wait_ge(m_hi_done, pair + 1)
            dve.tensor_tensor(m_lo[:, pair, :], bank[(3, 4, 6, 7)[pair]][:, :], m_hi[:, pair, :].bitcast(F32),
                              ALU.subtract).then_inc(m_lo_done, 1)
        dve.wait_ge(update_loaded, 144)
        dve.wait_ge(xb_done, NT)
        with dve.Fori(0, NT // 2) as it, own.loop(it, NT // 2, 2):
            tiles = [(par, 2 * it + par) for par in range(2)]
            for par, t in tiles:
                dve.wait_ge(agg_hi_done, done(t))
                dve.tensor_tensor(agg_lo[par][:], agg_sb[:, t, :], agg_hi[par][:].bitcast(F32),
                                  ALU.subtract).then_inc(agg_lo_done, 1)
            for par, t in tiles:
                dve.wait_ge(qT_hi_done, done(t))
                dve.tensor_tensor(qT_lo[par][:, :, 0:P], turned(7 * par)[:, :, 0:P],
                                  qT_hi[par][:, :, 0:P].bitcast(F32), ALU.subtract).then_inc(qT_lo_done, 1)
            for par, t in tiles:
                dve.wait_ge(g_mm, done(t))
                dve.tensor_tensor(mixed[par][:], bank[3 + par][0:P, :], bias_row[:], ALU.add).then_inc(g_sum_done, 1)
            for par, t in tiles:
                dve.wait_ge(y_mm, done(t))
                dve.wait_ge(g_sum_done, done(t))
                dve.scalar_tensor_tensor(mixed[par][:], mixed[par][:], 0.0, bank[1 + par][0:P, :],
                                         ALU.max, ALU.add).then_inc(y_sum_done, 1)
            for par, t in tiles:
                dve.wait_ge(y_sum_done, done(t))
                dve.wait_ge(res_done, freed(t))
                dve.tensor_tensor(x1[par][:], mixed[par][:], x_sb[:, t, :], ALU.add).then_inc(x1_done, 1)
            for par, t in tiles:
                dve.wait_ge(x1_done, done(t))
                dve.bn_stats(x1_parts[par][:], x1[par][:]).then_inc(x1_parts_done, 1)
            for par, t in tiles:
                dve.wait_ge(moments_done, NT)
                dve.wait_ge(x1_parts_done, done(t))
                dve.bn_aggr(x1_moments[par][:], x1_parts[par][:]).then_inc(x1_moments_done, 1)
            for par, t in tiles:
                dve.wait_ge(x1_std_done, done(t))
                dve.reciprocal(x1_rstd[par][:], x1_std[par][:]).then_inc(x1_rstd_done, 1)
            for par, t in tiles:
                dve.wait_ge(x1_rstd_done, done(t))
                dve.tensor_scalar(z_var[par][:], x1_moments[par][:, 1:2], x1_rstd[par][:], x1_rstd[par][:],
                                  ALU.mult, ALU.mult).then_inc(z_var_done, 1)
            for par, t in tiles:
                dve.tensor_scalar(z[par][:], x1[par][:], x1_moments[par][:, 0:1], x1_rstd[par][:],
                                  ALU.subtract, ALU.mult).then_inc(z_done, 1)
            for par, t in tiles:
                dve.wait_ge(z_std_done, done(t))
                dve.reciprocal(z_rstd[par][:], z_std[par][:]).then_inc(z_rstd_done, 1)
            for par, t in tiles:
                dve.wait_ge(z_rstd_done, done(t))
                dve.wait_ge(h_turned, freed(t))
                dve.wait_ge(h_stored[par], 16 * it)
                dve.scalar_tensor_tensor(h_tile[par][:], z[par][:], z_rstd[par][:], g_row[:],
                                         ALU.mult, ALU.mult).then_inc(dve_step, own.one())
            for par, t in tiles:
                dve.wait_ge(dve_step, own.now())
                dve.tensor_tensor(h_tile[par][:], h_tile[par][:], b_row[:], ALU.add).then_inc(h_done, 1)
            for par, t in tiles:
                dve.wait_ge(hT_hi_done, done(t))
                dve.tensor_tensor(hT_lo[:, :, t, 0:P], turned(7 * par)[:, :, 0:P],
                                  hT_hi[:, :, t, 0:P].bitcast(F32), ALU.subtract).then_inc(hT_lo_done, 1)
            for par, t in tiles:
                dve.wait_ge(l_mm, done(t))
                dve.tensor_scalar(logits[:, t, :], bank[5 + par][0:P, 0:NE], 1.0 / TEMP, None,
                                  ALU.mult).then_inc(logits_done, 1)
        for t in range(NT):
            dve.wait_ge(logits_done, done(t))
            dve.max(top_logit[:, t, :], logits[:, t, :]).then_inc(dve_step, own.one())
        for t in range(NT):
            dve.wait_ge(dve_step, own.now())
            dve.max_index(top_expert[:, t, :], top_logit[:, t, :], logits[:, t, :]).then_inc(picked, 1)

        dve.wait_ge(picked, NT)
        dve.tensor_copy(picks[:], top_expert[:, :, 0:2]).then_inc(dve_step, own.one())
        dve.tensor_tensor(gap[:], top_logit[:, :, 1], top_logit[:, :, 0], ALU.subtract).then_inc(gap_done, 1)
        dve.wait_ge(dve_step, own.now())
        dve.wait_ge(made_dve, MADE_EXPERT_IDS)
        every = expert_id[:].unsqueeze(1).broadcast_to([P, NT, NE])
        for which, to in enumerate((first_pick, second_pick)):
            dve.tensor_tensor(to[:], every, picks[:, :, which:which + 1].broadcast_to([P, NT, NE]),
                              ALU.is_equal).then_inc(dve_step, own.one())
        dve.memset(earlier[:, 0, :], 0.0).then_inc(earlier_done, 1)
        dve.wait_ge(dve_step, own.now())
        dve.wait_ge(dve_step, own.now())
        dve.tensor_tensor(picked_any[:], first_pick[:], second_pick[:], ALU.add).then_inc(dve_step, own.one())
        dve.wait_ge(dve_step, own.now())
        for t in range(NT):
            dve.wait_ge(earlier_done, t + 1)
            dve.tensor_tensor(earlier[:, t + 1, :], earlier[:, t, :], picked_any[:, t, :], ALU.add).then_inc(earlier_done, 1)
        dve.wait_ge(gap_exp, 1)
        dve.tensor_scalar(gate2[:], gap[:], 1.0, None, ALU.add).then_inc(dve_step, own.one())
        dve.wait_ge(dve_step, own.now())
        dve.reciprocal(gate1[:], gate2[:]).then_inc(dve_step, own.one())
        dve.wait_ge(dve_step, own.now())
        dve.tensor_tensor(gate2[:], gate1[:], gap[:], ALU.mult).then_inc(dve_step, own.one())
        dve.wait_ge(res_done, done(NT - 1))
        for raw, hi_, lo_, ready in ((ws1_raw, ws1_hi, ws1_lo, SPLIT["ws1"]),
                                             (ws2_raw, ws2_hi, ws2_lo, SPLIT["ws2"])):
            dve.wait_ge(halves_hi, ready)
            dve.tensor_tensor(lo_[:], raw[:], hi_[:].bitcast(F32), ALU.subtract).then_inc(halves_lo, 1)
        dve.wait_ge(rank_mm, 3)
        dve.tensor_scalar(padded_i32[:], bank[2][0:P, 0:NE], float(SLOTS - 1), None, ALU.add).then_inc(dve_step, own.one())
        dve.wait_ge(dve_step, own.now())
        dve.tensor_scalar(padded_i32[:], padded_i32[:], 6, 6, ALU.arith_shift_right, ALU.arith_shift_left).then_inc(dve_step, own.one())
        dve.wait_ge(dve_step, own.now())
        dve.tensor_copy(padded[:], padded_i32[:]).then_inc(dve_step, own.one())
        dve.wait_ge(dve_step, own.now())
        src_scan = padded
        shifts = (1, 2, 4, 8, 16, 32)
        for n, shift in enumerate(shifts):
            to = scan[n % 2]
            dve.wait_ge(dve_step, own.now())
            dve.tensor_copy(to[:, 0:shift], src_scan[:, 0:shift]).then_inc(dve_step, own.one())
            dve.tensor_tensor(to[:, shift:NE], src_scan[:, shift:NE], src_scan[:, 0:NE - shift], ALU.add).then_inc(dve_step, own.one())
            src_scan = to
        ends = src_scan
        dve.wait_ge(dve_step, own.now())
        dve.tensor_tensor(starts[:], ends[:], padded[:], ALU.subtract).then_inc(dve_step, own.one())
        dve.tensor_copy(expert_end[:], ends[:]).then_inc(dve_step, own.one())
        dve.wait_ge(dve_step, own.now())
        dve.tensor_scalar(expert_end[:], expert_end[:], 6, None, ALU.arith_shift_right).then_inc(tables_done, 1)
        dve.tensor_scalar(tile_expert_f[:], ends[:, NE - 1:NE], 1.0 / (SLOTS * BODY), (BODY + 1 - (BODY - 1) / 2) / BODY,
                          ALU.mult, ALU.add).then_inc(dve_step, own.one())
        dve.wait_ge(dve_step, own.now())
        dve.tensor_scalar(bodies[:, 0:1], tile_expert_f[:], float(STEPS), None, ALU.min).then_inc(dve_step, own.one())
        dve.wait_ge(dve_step, own.now())
        dve.tensor_scalar(bodies[:, 1:2], bodies[:, 0:1], 1.0, None, ALU.subtract).then_inc(tables_done, 1)
        dve.tensor_scalar(scan[0][:], ends[:], tile_start[:], None, ALU.is_le).then_inc(dve_step, own.one())
        dve.wait_ge(dve_step, own.now())
        dve.reduce_sum(tile_expert_f[:], scan[0][:], AX.X).then_inc(dve_step, own.one())
        dve.wait_ge(dve_step, own.now())
        dve.tensor_scalar(tile_expert[:], tile_expert_f[:], float(NE - 1), None, ALU.min).then_inc(tables_done, 1)
        dve.wait_ge(rank_mm, 2)
        for n in range(2):
            dve.tensor_tensor(slot_all[:, 5 * n:5 * (n + 1), :],
                              bank[n][0:P, 0:5 * NE].rearrange("p (t e) -> p t e", e=NE),
                              starts[:].unsqueeze(1).broadcast_to([P, 5, NE]), ALU.add).then_inc(dve_step, own.one())
        dve.wait_ge(dve_step, own.now())
        for which, pick in enumerate((first_pick, second_pick)):
            if which:
                dve.wait_ge(dve_step, own.now())
            dve.tensor_tensor(work[:], slot_all[:], pick[:], ALU.mult).then_inc(dve_step, own.one())
            dve.wait_ge(dve_step, own.now())
            dve.reduce_sum(slots_f[:, which, :], work[:], AX.X).then_inc(dve_step, own.one())
        dve.wait_ge(dve_step, own.now())
        dve.tensor_copy(slots[:], slots_f[:]).then_inc(dve_step, own.one())
        dve.wait_ge(dve_step, own.now())
        dve.tensor_scalar(slot_low[:], slots[:], 127, None, ALU.bitwise_and).then_inc(dve_step, own.one())
        dve.tensor_scalar(slot_high[:], slots[:], 7, None, ALU.arith_shift_right).then_inc(dve_step, own.one())
        dve.wait_ge(dve_step, own.now())
        dve.scalar_tensor_tensor(table_at[:], slot_low[:], float(PAIR_TILES), slot_high[:], ALU.mult, ALU.add).then_inc(tables_done, 1)
        dve.tensor_scalar(gates_up[:, 0, :], gate1[:], 1.0 / SHARED_SCALE, None, ALU.mult).then_inc(dve_step, own.one())
        dve.tensor_scalar(gates_up[:, 1, :], gate2[:], 1.0 / SHARED_SCALE, None, ALU.mult).then_inc(dve_step, own.one())
        dve.wait_ge(dve_step, own.now())
        dve.tensor_tensor(slot_all[:], first_pick[:], gates_up[:, 0, :].unsqueeze(2).broadcast_to([P, NT, NE]), ALU.mult).then_inc(dve_step, own.one())
        dve.tensor_tensor(work[:], second_pick[:], gates_up[:, 1, :].unsqueeze(2).broadcast_to([P, NT, NE]), ALU.mult).then_inc(dve_step, own.one())
        dve.wait_ge(dve_step, own.now())
        dve.tensor_tensor(work[:], work[:], slot_all[:], ALU.add).then_inc(combine_done, 1)
        dve.wait_ge(table_moved, 16 * (1 + UNSURE))
        dve.wait_ge(ws2_loaded, 64)
        dve.tensor_scalar(bs2_row[:], bs2_row[:], SHARED_SCALE, None, ALU.mult).then_inc(dve_step, own.one())
        dve.wait_ge(dve_step, own.now())
        for g, (lo, hi) in enumerate(GROUPS):
            width = (hi - lo) * PW
            for fb in range(SB):
                n = g * SB + fb
                dve.wait_ge(shared_act, n + 1)
                if g:
                    dve.wait_ge(shared_down, lo)
                dve.tensor_copy(shared_hT_hi[:, fb, 0:width], shared_h[fb % 2][:, 0:width]).then_inc(dve_step, own.one())
                dve.wait_ge(dve_step, own.now())
                dve.tensor_tensor(shared_hT_lo[:, fb, 0:width], shared_h[fb % 2][:, 0:width],
                                  shared_hT_hi[:, fb, 0:width].bitcast(F32), ALU.subtract).then_inc(shared_lo_done, 1)
            if hi == NT:
                dve.wait_ge(ffw_loaded, 96)
                for k in range(KD):
                    dve.tensor_scalar(wf1_g[:, k, :], wf1_raw[:, k, :], g_col[:, k:k + 1], None, ALU.mult).then_inc(wf1_g_done, 1)
                dve.wait_ge(halves_hi, SPLIT["wf1"])
                dve.tensor_tensor(wf1_lo[:], wf1_g[:], wf1_hi[:].bitcast(F32), ALU.subtract).then_inc(halves_lo, 1)
                dve.wait_ge(halves_hi, SPLIT["wf2"])
                dve.tensor_tensor(wf2_lo[:], wf2_raw[:], wf2_hi[:].bitcast(F32), ALU.subtract).then_inc(halves_lo, 1)
            for t in range(lo, hi):
                dve.wait_ge(shared_down, t + 1)
                dve.scalar_tensor_tensor(shared[:, t, :], bank[5 + t % 2][0:P, :], SHARED_SCALE, bs2_row[:],
                                         ALU.mult, ALU.add).then_inc(shared_done, 1)

        dve.wait_ge(bf1_mm, 2)
        dve.tensor_tensor(bf1_sb[:], bank[3][:, 0:2], bf1_raw[:], ALU.add).then_inc(bf1_done, 1)

        def expert_of(j):
            return dve.value_load(tile_expert_row[0:1, bass.ds(j, 1)], min_val=0, max_val=NE - 1)

        def copy_weights(j, n, expert):
            dve.wait_ge(experts_here, expert + 1)
            dve.wait_ge(down_mm, tile_freed(j, BODY))
            dve.tensor_copy(w_tile[n][:], w_ring[:, bass.ds(slot_of(expert), 1), :].rearrange("p a c -> p (a c)")).then_inc(w_copied, 1)

        def dve_tiles(it, last):
            for n in range(BODY):
                j = BODY * it + n
                par = n % 2
                more = not (last and n + W_AHEAD >= BODY)
                if more:
                    expert = expert_of(j + W_AHEAD)
                dve.wait_ge(up_mm, tile_done(j))
                dve.wait_ge(up_turned, tile_freed(j, 2))
                dve.tensor_copy(up[par][:], bank[2 + par][:, 0:128]).then_inc(up_copied, 1)
                if more:
                    copy_weights(j + W_AHEAD, (n + W_AHEAD) % BODY, expert)

        def dve_skip(it, copies):
            dve.wait_ge(up_copied, tile_done(BODY * it - 1))
            dve.sem_inc(up_copied, BODY)
            dve.wait_ge(w_copied, copied(BODY * it + W_AHEAD - 1))
            dve.sem_inc(w_copied, copies)

        dve.wait_ge(tile_expert_moved, 32)
        for j in range(W_AHEAD):
            copy_weights(j, j, expert_of(j))
        run = dve.value_load(bodies[0:1, 0:1], min_val=STEPS_MIN, max_val=STEPS)
        with dve.Fori(0, STEPS - 1) as it:
            with dve.If(it < run):
                dve_tiles(it, False)
            with dve.If(it >= run):
                dve_skip(it, BODY)
        with dve.If(run >= STEPS):
            dve_tiles(STEPS - 1, True)
        with dve.If(run < STEPS):
            dve_skip(STEPS - 1, BODY - W_AHEAD)
        for g, (lo, hi) in enumerate(GROUPS):
            for t in range(lo, hi):
                par = t % 2
                dve.wait_ge(eo_fetched[par], 32 * (t // 2 + 1))
                if t >= 2:
                    dve.wait_ge(hm_kept, t - 1)
                dve.scalar_tensor_tensor(hmoe[par][:], eo_first[par][:], gate1[:, t:t + 1], shared[:, t, :], ALU.mult,
                                         ALU.add).then_inc(dve_step, own.one())
                dve.wait_ge(dve_step, own.now())
                dve.scalar_tensor_tensor(hmoe[par][:], eo_second[par][:], gate2[:, t:t + 1], hmoe[par][:], ALU.mult,
                                         ALU.add).then_inc(hm_done, 1)
                dve.wait_ge(hm_done, t + 1)
                dve.bn_stats(hm_parts[par][:], hmoe[par][:]).then_inc(dve_step, own.one())
                dve.wait_ge(dve_step, own.now())
                dve.bn_aggr(hm_moments[par][:], hm_parts[par][:]).then_inc(hm_moments_done, 1)
                dve.wait_ge(hm_std_done, t + 1)
                dve.reciprocal(hm_rstd[par][:], hm_std[par][:]).then_inc(hm_rstd_done, 1)
                dve.wait_ge(hm_rstd_done, t + 1)
                if t >= 2:
                    dve.wait_ge(ff_turned, t - 1)
                dve.tensor_scalar(ff_in[par][:], hmoe[par][:], hm_moments[par][:, 0:1], hm_rstd[par][:],
                                  ALU.subtract, ALU.mult).then_inc(ff_in_done, 1)
                dve.wait_ge(ffT_hi_done, t + 1)
                dve.tensor_tensor(ffT_lo[:, :, t - lo, 0:P], turned(par)[:, :, 0:P],
                                  ffT_hi[:, :, t - lo, 0:P].bitcast(F32), ALU.subtract).then_inc(ffT_lo_done, 1)
            width = (hi - lo) * PW
            for half in range(2):
                n = 2 * g + half
                dve.wait_ge(ff_act, n + 1)
                if g:
                    dve.wait_ge(ff_down, lo)
                dve.tensor_copy(ff_hT_hi[:, half, 0:width], ff_h[half][:, 0:width]).then_inc(dve_step, own.one())
                dve.wait_ge(dve_step, own.now())
                dve.tensor_tensor(ff_hT_lo[:, half, 0:width], ff_h[half][:, 0:width],
                                  ff_hT_hi[:, half, 0:width].bitcast(F32), ALU.subtract).then_inc(ff_h_lo_done, 1)
            for t in range(lo, hi):
                dve.wait_ge(ff_down, t + 1)
                dve.wait_ge(hm_kept, t + 1)
                if t >= 2:
                    dve.wait_ge(result_stored[t % 2], 32 * (t // 2))
                dve.tensor_tensor(result[t % 2][:], bank[4 + t % 2][0:P, :], x_sb[:, t, :], ALU.add).then_inc(result_done, 1)

    @block.tensor
    def _(pe):
        for signal in (xn_turned, t_mm, q_mm, k_mm, v_mm, q_turned, g_mm, y_mm, h_turned, r_mm, l_mm):
            pe.sem_inc(signal, AHEAD)
        for signal in (pair_turned, up_mm, up_turned, down_mm):
            pe.sem_inc(signal, BODY)
        pe.sem_inc(chunk_mm, CHUNK_AHEAD)

        def turn(tile, to, signal):
            for k in range(KD):
                last = pe.transpose(turned(to)[:, k, 0:P], tile[:, 128 * k:128 * (k + 1)], ident[0:P, 0:P])
            last.then_inc(signal, 1)

        def turn_x(par, item):
            pe.wait_ge(xn_done, done(item))
            pe.wait_ge(xnt_lo_done, freed(item))
            turn(xn[par], 6 + par, xn_turned)

        def product(to, terms, signal):
            for i, (a, b) in enumerate(terms):
                last = pe.matmul(to, a, b, start=(i == 0), stop=(i == len(terms) - 1))
            last.then_inc(signal, 1)

        def split_terms(a_hi, a_lo, b_hi, b_lo, blocks):
            terms = []
            for k in range(blocks):
                terms += [(a_hi(k), b_hi(k)), (a_hi(k), b_lo(k)), (a_lo(k), b_hi(k))]
            return terms

        pe.wait_ge(made, MADE_IDENT)
        pe.wait_ge(halves_lo, SPLIT["u"])
        with pe.Fori(0, NT // 2) as it:
            for par in range(2):
                turn_x(par, 2 * it + par)
            for par in range(2):
                t = 2 * it + par
                pe.wait_ge(xnt_lo_done, done(t))
                pe.wait_ge(t_done, freed(t))
                product(bank[4 + par][0:P, 0:2 * RANK],
                        [(half[par][:, k, 0:P], u_hl[:, k, :]) for k in range(KD) for half in (xnt_hi, xnt_lo)], t_mm)
        pe.wait_ge(made, MADE_ZEROS)
        agg = [bank[b][:, 0:(hi - lo) * PW] for b, (lo, hi) in enumerate(GROUPS)]
        for b, (lo, hi) in enumerate(GROUPS):
            last = pe.matmul(agg[b], zero_w[:], onehot[0][:, lo * PW:hi * PW], start=True, stop=False,
                             skip_group_check=True)
        last.then_inc(agg_opened, 1)

        def sum_edges(batch, half, first, last_c):
            pe.wait_ge(rows_lo_done, done(batch))
            for c in range(first, last_c):
                pe.wait_ge(onehot_done, batch * BC + c + 1)
                for b, (lo, hi) in enumerate(GROUPS):
                    last = pe.matmul(agg[b], rows_hl[half][:, c, :],
                                     onehot[(half * BC + c) % OH_RING][:, lo * PW:hi * PW],
                                     start=False, stop=False, skip_group_check=True)
                last.then_inc(chunk_mm, 1)

        pe.wait_ge(halves_lo, SPLIT["wqkv"])
        pe.wait_ge(t_done, done(NT - 1))

        def project(t, par, part, first, end):
            signal, readers = ((q_mm, (q_sub_done,)), (k_mm, (k_copied,)), (v_mm, (v_copied,)))[part]
            if first == 0 and end > 0:
                for reader in readers:
                    pe.wait_ge(reader, freed(t, 1))
            cols = slice(D * part, D * (part + 1))
            terms = split_terms(lambda k: xnt_hi[par][:, k, 0:P], lambda k: xnt_lo[par][:, k, 0:P],
                                lambda k: wqkv_hi[:, k, cols], lambda k: wqkv_lo[:, k, cols], KD)
            for i in range(first, end):
                last = pe.matmul(bank[3 + part][0:P, :], terms[i][0], terms[i][1], start=(i == 0), stop=(i == len(terms) - 1),
                                 skip_group_check=True)
                if i == len(terms) - 1:
                    last.then_inc(signal, 1)

        def pe_edge_tiles(it, final=False):
            for par in range(2):
                t = 2 * it + par
                pe.wait_ge(xnt_lo_done, done(NT + t))
                for c in range(2 * BC):
                    sum_edges(2 * t + c // BC, c // BC, c % BC, c % BC + 1)
                    begin, end = 3 * 3 * KD * c // (2 * BC), 3 * 3 * KD * (c + 1) // (2 * BC)
                    for part in range(3):
                        at = 3 * KD * part
                        lo, hi = max(begin - at, 0), min(end - at, 3 * KD)
                        if lo < hi:
                            project(t, par, part, lo, hi)
                    if c == BC - 1 and not (final and par):
                        turn_x(1 - par, NT + t + 1)

        turn_x(0, NT)
        with pe.Fori(0, NT // 2 - 1) as it:
            pe_edge_tiles(it)
        pe_edge_tiles(NT // 2 - 1, final=True)
        for b, (lo, hi) in enumerate(GROUPS):
            last = pe.matmul(agg[b], zero_w[:], onehot[0][:, lo * PW:hi * PW], start=False, stop=True,
                             skip_group_check=True)
        last.then_inc(agg_closed, 1)
        pe.wait_ge(k_top_done, done(NT - 1))
        pe.wait_ge(xnt_lo_done, done(2 * NT - 1))
        turn(k_top, 6, k_top_turned)
        pe.wait_ge(k_top_wide_done, 1)
        for k in range(PAIRS):
            last = pe.transpose(bank[7][0:P, 128 * k:128 * (k + 1)], k_top_wide[:, k, :], ident[:])
        last.then_inc(k_top_back, 1)
        pe.wait_ge(v_copied, done(NT - 1))
        pe.wait_ge(q_sub_done, done(NT - 1))
        for pair in range(PAIRS):
            at = 132 * (pair % 2)
            for t in range(NT):
                pe.wait_ge(k_exp_done, t + 1)
                last = pe.matmul(bank[3 + pair // 2][:, at:at + 130], k_sb[:, t, 128 * pair:128 * (pair + 1)],
                                 v_sb[:, t, pair, :], start=(t == 0), stop=(t == NT - 1))
            last.then_inc(ctx_mm, 1)
        pe.wait_ge(ctx_done, 2 * PAIRS)
        for pair in range(PAIRS):
            last = pe.transpose(bank[5][:, 128 * pair:128 * (pair + 1)], ctx[:, pair, :], ident[:])
        last.then_inc(ctx_turned, 1)
        pe.wait_ge(ctxT_lo_done, 1)
        pe.wait_ge(halves_lo, SPLIT["wout"])
        for pair in range(PAIRS):
            product(bank[(3, 4, 6, 7)[pair]][:, :],
                    [(ctxT_hi[:, pair, :], wout_hi[:, pair, :]), (ctxT_hi[:, pair, :], wout_lo[:, pair, :]),
                     (ctxT_lo[:, pair, :], wout_hi[:, pair, :])], m_mm)
        pe.wait_ge(m_lo_done, PAIRS)
        pe.wait_ge(zeroed, ZEROED_HT)
        pe.wait_ge(halves_lo, SPLIT["vt"])
        pe.wait_ge(halves_lo, SPLIT["wr"])
        pe.wait_ge(agg_copied, 3)
        with pe.Fori(0, NT // 2) as it:
            tiles = [(par, 2 * it + par) for par in range(2)]
            for par, t in tiles:
                pe.wait_ge(q_tile_done, done(t))
                pe.wait_ge(hT_lo_done, freed(t))
                turn(q_tile[par], 7 * par, q_turned)
            for par, t in tiles:
                pe.wait_ge(agg_lo_done, done(t))
                pe.wait_ge(g_sum_done, freed(t))
                pe.wait_ge(rT_done, freed(t))
                product(bank[3 + par][0:P, :], [(agg_hi[par][:, 0:P], vt2_hi[:]), (agg_hi[par][:, 0:P], vt2_lo[:]),
                                                (agg_lo[par][:, 0:P], vt2_hi[:])], g_mm)
            for par, t in tiles:
                pe.wait_ge(qT_lo_done, done(t))
                pe.wait_ge(y_sum_done, freed(t))
                product(bank[1 + par][0:P, :],
                        split_terms(lambda k: qT_hi[par][:, k, 0:P], lambda k: qT_lo[par][:, k, 0:P],
                                    lambda k: m_hi[:, k, :], lambda k: m_lo[:, k, :], PAIRS), y_mm)
            for par, t in tiles:
                pe.wait_ge(h_done, done(t))
                turn(h_tile[par], 7 * par, h_turned)
            for par, t in tiles:
                pe.wait_ge(hT_lo_done, done(t))
                product(bank[3 + par][:, 0:PW],
                        [(wr_hl[:, k, :], half[:, k, t, :]) for k in range(KD) for half in (hT_hi, hT_lo)], r_mm)
            for par, t in tiles:
                pe.wait_ge(rT_done, done(t))
                pe.wait_ge(logits_done, freed(t))
                product(bank[5 + par][0:P, 0:NE], [(rT[par][:, 0:P], codebook2[:])], l_mm)

        def shared_up_products(g):
            lo, hi = GROUPS[g]
            for fb in range(SB):
                n = g * SB + fb
                if n >= 2:
                    pe.wait_ge(shared_act, n - 1)
                cols = slice(128 * fb, 128 * (fb + 1))
                product(bank[3 + fb % 2][:, 0:(hi - lo) * PW],
                        split_terms(lambda k: ws1_hi[:, k, cols], lambda k: ws1_lo[:, k, cols],
                                    lambda k: hT_hi[:, k, lo:hi, :].rearrange("p t c -> p (t c)"),
                                    lambda k: hT_lo[:, k, lo:hi, :].rearrange("p t c -> p (t c)"), KD), shared_up)

        def shared_down_products(g):
            lo, hi = GROUPS[g]
            pe.wait_ge(shared_lo_done, (g + 1) * SB)
            for t in range(lo, hi):
                if t >= 2:
                    pe.wait_ge(shared_done, t - 1)
                cols = slice((t - lo) * PW, (t - lo) * PW + P)
                product(bank[5 + t % 2][0:P, :],
                        split_terms(lambda k: shared_hT_hi[:, k, cols], lambda k: shared_hT_lo[:, k, cols],
                                    lambda k: ws2_hi[:, k, :], lambda k: ws2_lo[:, k, :], SB)
                        + [(combineT[:, t, :], b2_sb[:])], shared_down)

        pe.wait_ge(made, MADE_BEFORE)
        pe.wait_ge(earlier_done, NT + 1)
        for n in range(2):
            tiles_ = slice(5 * n, 5 * (n + 1))
            product(bank[n][0:P, 0:5 * NE], [(before[:], picked_any[:, tiles_, :].rearrange("p t e -> p (t e)")),
                                             (ones[:], earlier[:, tiles_, :].rearrange("p t e -> p (t e)"))], rank_mm)
        product(bank[2][0:P, 0:NE], [(ones[:], earlier[:, NT, :])], rank_mm)
        pe.wait_ge(halves_lo, SPLIT["ws1"])
        shared_up_products(0)
        pe.wait_ge(combine_done, 1)
        for g, (lo, hi) in enumerate(GROUPS):
            for t in range(lo, hi):
                pe.transpose(bank[g][0:NE, 128 * (t - lo):128 * (t - lo) + P], work[:, t, :], ident[0:P, 0:P]).then_inc(combine_turned, 1)
        pe.wait_ge(halves_lo, SPLIT["ws2"])
        pe.wait_ge(ws2_loaded, 64)
        pe.wait_ge(combineT_done, len(GROUPS))
        shared_down_products(0)
        for g in range(1, len(GROUPS)):
            shared_up_products(g)
            shared_down_products(g)
        pe.wait_ge(ffw_loaded, 96)
        for half in range(2):
            product(bank[3][:, half:half + 1],
                    [(wf1_raw[:, k, 128 * half:128 * (half + 1)], b_col[:, k:k + 1]) for k in range(KD)], bf1_mm)
        pe.wait_ge(shared_done, NT)
        pe.wait_ge(bf1_done, 1)

        def turn_pair(q, v, turn):
            pe.wait_ge(pair_fetched[v], 16 * (turn + 1))
            pe.wait_ge(pairT_done, tile_freed(q, 1 if v == 0 else 2))
            for k in range(KD):
                last = pe.transpose(bank[v % 2][:, 128 * k:128 * (k + 1)], pair_rows[v][:, 128 * k:128 * (k + 1)], ident[:])
            last.then_inc(pair_turned, 1)

        def up_products(it, n):
            j = BODY * it + n
            par = n % 2
            if n % 2 == 0:
                pe.wait_ge(pairT_done, tile_done(BODY // 2 * it + n // 2))
            pe.wait_ge(w_copied, copied(j))
            pe.wait_ge(up_copied, tile_freed(j, 2))
            for k in range(KD):
                for half in range(2):
                    last = pe.matmul(bank[2 + par][SLOTS * half:SLOTS * (half + 1), 0:128],
                                     pair_rowsT[n // 2][:, k, SLOTS * par:SLOTS * (par + 1)],
                                     w_tile[n][:, k * DFF + 128 * half:k * DFF + 128 * (half + 1)],
                                     start=(k == 0), stop=(k == KD - 1), skip_group_check=True)
            last.then_inc(up_mm, 1)

        def up_transpose(j, par):
            pe.wait_ge(up_copied, tile_done(j))
            pe.wait_ge(up_act, tile_freed(j, 2))
            pe.transpose(bank[4 + par][:, 0:128], up[par][:], ident[:]).then_inc(up_turned, 1)

        def down_products(j, n, turn):
            par = n % 2
            pe.wait_ge(up_act, tile_done(j))
            pe.wait_ge(down_copied, turn)
            for k in range(2):
                for half in range(2):
                    last = pe.matmul(bank[6 + par][SLOTS * half:SLOTS * (half + 1), 0:D // 2], upT[par][:, k, :],
                                     w_tile[n][:, W1_COLS + k * D + half * (D // 2):W1_COLS + k * D + (half + 1) * (D // 2)],
                                     start=(k == 0), stop=(k == 1), skip_group_check=True)
            last.then_inc(down_mm, 1)

        def pe_step(it, first=False, last=False):
            for n in range(BODY):
                j = BODY * it + n
                up_products(it, n)
                if n % 2 and not (last and n == BODY - 1):
                    v = (n + 1) // 2
                    turn_pair(3 * it + v, v % 3, it + v // 3)
                if not (first and n < 1):
                    up_transpose(j - 1, (n - 1) % 2)
                if not (first and n < 2):
                    down_products(j - 2, (n - 2) % BODY, j - 3 if not (first and n < 4) else 0)

        def pe_skip(it):
            pe.wait_ge(up_turned, tile_done(BODY * it - 2))
            pe.sem_inc(up_turned, BODY)
            pe.wait_ge(down_mm, tile_done(BODY * it - 3))
            pe.sem_inc(down_mm, BODY)

        turn_pair(0, 0, 0)
        pe.wait_ge(tables_done, TABLE_BODIES)
        run = pe.value_load(bodies[0:1, 0:1], min_val=STEPS_MIN, max_val=STEPS)
        pe_step(0, first=True)
        with pe.Fori(1, STEPS - 1) as it:
            with pe.If(it < run):
                pe_step(it)
            with pe.If(it >= run):
                pe_skip(it)
        with pe.If(run >= STEPS):
            pe_step(STEPS - 1, last=True)
            up_transpose(TILES - 1, 1)
            for j in (TILES - 2, TILES - 1):
                down_products(j, j % BODY, j - 1)
        with pe.If(run < STEPS):
            pe_skip(STEPS - 1)
        pe.wait_ge(halves_lo, SPLIT["wf1"])
        pe.wait_ge(halves_lo, SPLIT["wf2"])
        pe.wait_ge(zeroed, ZEROED_FFT)
        pe.wait_ge(pairT_done, tile_done(TILES // 2 - 1))
        pe.wait_ge(down_copied, TILES)
        pe.wait_ge(up_copied, tile_done(TILES - 1))
        pe.wait_ge(up_act, tile_done(TILES - 1))
        for g, (lo, hi) in enumerate(GROUPS):
            width = (hi - lo) * PW
            for t in range(lo, hi):
                pe.wait_ge(ff_in_done, t + 1)
                if t >= 2:
                    pe.wait_ge(ffT_lo_done, t - 1)
                turn(ff_in[t % 2], t % 2, ff_turned)
            pe.wait_ge(ffT_lo_done, hi)
            for half in range(2):
                if g:
                    pe.wait_ge(ff_act, 2 * (g - 1) + half + 1)
                cols = slice(128 * half, 128 * (half + 1))
                product(bank[2 + half][:, 0:width],
                        split_terms(lambda k: wf1_hi[:, k, cols], lambda k: wf1_lo[:, k, cols],
                                    lambda k: ffT_hi[:, k, 0:hi - lo, :].rearrange("p t c -> p (t c)"),
                                    lambda k: ffT_lo[:, k, 0:hi - lo, :].rearrange("p t c -> p (t c)"), KD), ff_up)
            pe.wait_ge(ff_h_lo_done, 2 * (g + 1))
            for t in range(lo, hi):
                if t >= 2:
                    pe.wait_ge(result_done, t - 1)
                cols = slice((t - lo) * PW, (t - lo) * PW + P)
                product(bank[4 + t % 2][0:P, :],
                        split_terms(lambda k: ff_hT_hi[:, k, cols], lambda k: ff_hT_lo[:, k, cols],
                                    lambda k: wf2_hi[:, k, :], lambda k: wf2_lo[:, k, :], 2), ff_down)

    block.__exit__(None, None, None)


_ORDER = ["x", "src", "dst", "edge_weight", "u", "s", "vt", "gnn_bias", "wqkv_t", "wout_t", "bout", "ln1_g", "ln1_b",
          "wr", "codebook_t", "experts", "b2", "ws1", "bs1_cols", "ws2", "bs2", "ffln_g_cols", "ffln_b_cols", "wf1",
          "bf1_cols", "wf2", "bf2"]


def laid_out(i):
    import numpy as np

    def col(v):
        return v.reshape(-1, 128).T

    w1, w2, b1 = i["L0_ffn_W1"], i["L0_ffn_W2"], i["L0_ffn_b1"]
    experts = np.concatenate([
        w1.reshape(NE, KD, 128, DFF).transpose(0, 2, 1, 3).reshape(NE, 128, KD * DFF),
        w2.reshape(NE, 2, 128, D).transpose(0, 2, 1, 3).reshape(NE, 128, 2 * D),
        b1.reshape(NE, 2, 128).transpose(0, 2, 1)], axis=2)
    row = lambda v: v.reshape(1, -1)
    return {
        "x": i["x"], "src": i["src"].reshape(P, EC), "dst": i["dst"].reshape(P, EC),
        "edge_weight": i["edge_weight"].reshape(P, EC), "u": i["L0_gnn_U"], "s": row(i["L0_gnn_s"]),
        "vt": i["L0_gnn_Vt"], "gnn_bias": row(i["L0_gnn_bias"]), "wqkv_t": i["L0_mix_Wqkv"].T,
        "wout_t": i["L0_mix_Wout"].T, "bout": row(i["L0_mix_bout"]), "ln1_g": row(i["L0_ffn_ln1_g"]),
        "ln1_b": row(i["L0_ffn_ln1_b"]), "wr": i["L0_ffn_Wr"], "codebook_t": i["L0_ffn_codebook"].T,
        "experts": experts, "b2": i["L0_ffn_b2"], "ws1": i["L0_ffn_Ws1"], "bs1_cols": col(i["L0_ffn_bs1"]),
        "ws2": i["L0_ffn_Ws2"], "bs2": row(i["L0_ffn_bs2"]), "ffln_g_cols": col(i["L0_ffn_ffln_g"]),
        "ffln_b_cols": col(i["L0_ffn_ffln_b"]), "wf1": i["L0_ffn_Wf1"], "bf1_cols": col(i["L0_ffn_bf1"]),
        "wf2": i["L0_ffn_Wf2"], "bf2": row(i["L0_ffn_bf2"]),
    }


def kernel(**inputs):
    import numpy as np
    import concourse.bacc as bacc
    from concourse.bass_utils import run_bass_kernel_spmd

    nc = bacc.Bacc("TRN2", target_bir_lowering=False, num_devices=1)
    arrays, args = {}, []
    laid = laid_out({k: np.asarray(v) for k, v in inputs.items()})
    for name in _ORDER:
        a = np.ascontiguousarray(laid[name])
        arrays[f"in_{name}"] = a
        args.append(nc.dram_tensor(f"in_{name}", a.shape, mybir.dt.from_np(a.dtype), kind="ExternalInput").ap())
    args.append(nc.dram_tensor("result", (N, D), F32, kind="ExternalOutput").ap())
    gps_layer(nc, *args)
    r = run_bass_kernel_spmd(nc, [arrays], core_ids=[0])
    return r.results[0]["result"]
```

```python
from contextlib import contextmanager

import concourse.bass as bass
from concourse import mybir

F32 = mybir.dt.float32
F16 = mybir.dt.float16
BF16 = mybir.dt.bfloat16
F32R = mybir.dt.float32r
I32 = mybir.dt.int32
U32 = mybir.dt.uint32
ALU = mybir.AluOpType
ACT = mybir.ActivationFunctionType
AX = mybir.AxisListType

N = 1250
D = 512
E_EDGES = 20000
P = 125
NT = N // P
PW = P + 1
KD = D // 128
RANK = 64
HEADS = 8
PAIRS = HEADS // 2
EC = E_EDGES // P
BC = 8
OH_RING = 4
BANK = 512
EPS = 1e-5

NE = 64
DR = 64
DFF = 256
DSH = 1024
SB = DSH // 128
TEMP = 0.7
SHARED_SCALE = 0.25
SLOTS = 64
TILES = (2 * N + (SLOTS - 1) * NE) // SLOTS
GROUPS = [(0, 4), (4, 7), (7, 10)]

PAIR_TILES = TILES // 2
BODY = 6
STEPS = TILES // BODY
UNSURE = -(-(TILES * SLOTS - 2 * N // SLOTS * SLOTS) // N)
STEPS_MIN = 2 * N // (SLOTS * BODY)
W_RING = 8
W_AHEAD = 2
STORE_LAG = 4
EARLY_LOADS = W_RING // 2
EO_RING, HM_RING = 4, 3
SH_RING = 4
RELAY_LAG = 2
W1_COLS = KD * DFF
B1_AT = W1_COLS + 2 * D
W_COLS = B1_AT + 2

SPLIT = {"u": 1, "wqkv": 1 + KD, "wout": 2 + KD, "vt": 3 + KD, "wr": 4 + KD, "bias": 5 + KD, "ws1": 5 + 2 * KD, "ws2": 6 + 2 * KD,
         "wf1": 7 + 2 * KD, "wf2": 8 + 2 * KD}
MADE_NODES, MADE_FILLS, MADE_IDENT, MADE_BEFORE, MADE_IDS, MADE_ZEROS = 1, 7, 8, 9, 13, 14
MADE_NODE_COLS, MADE_EXPERT_IDS, MADE_EDGES = 1, 3, 6

ZEROED_HT, ZEROED_CTX, ZEROED_FFT = 2, 3, 5
TABLE_ENDS, TABLE_BODIES, TABLE_TILES, TABLE_SLOTS = 1, 2, 3, 4

AHEAD = 2
CHUNK_AHEAD = 32


def done(n):
    return n + 1 + AHEAD


def freed(n, ring=2):
    return n + 1 + AHEAD - ring


def tile_done(j):
    return j + 1 + BODY


def tile_freed(j, ring):
    return j + 1 + BODY - ring


def copied(j):
    return j + 2


def slot_of(expert):
    return expert & (W_RING - 1)


def update_steps(engine, step):
    for it in range(2):
        step(it, 0)
        step(it, 1)
    with engine.Fori(2, NT // 2) as it:
        step(it, 0)
        step(it, 1)
    for it in range(NT // 2, NT // 2 + 2):
        step(it, 0)
        step(it, 1)


def tiles_of(it, n):
    def tile(k):
        t = 2 * it + n - k
        if isinstance(it, int) and not 0 <= t < NT:
            return None, 0, 0
        return t, (n - k) % 2, it + (n - k) // 2
    return tile


class Steps:

    def __init__(self):
        self.n, self.turns = 0, 0

    def one(self):
        self.n += 1
        return 1

    def now(self):
        return self.n + self.turns

    @contextmanager
    def loop(self, it, count, each):
        start, self.turns = self.n, it * each
        yield
        assert self.n == start + each, self.n - start
        self.n, self.turns = start + each * count, 0


class Region:

    def __init__(self, nc, start, end):
        self.nc, self.at, self.end = nc, start, end

    def place(self, name, shape, dtype=F32):
        size = mybir.dt.size(dtype)
        for n in shape[1:]:
            size *= n
        tensor = self.nc.alloc_sbuf_tensor_at(name, shape, dtype, offset=self.at)
        self.at += (size + 31) // 32 * 32
        assert self.at <= self.end, (name, self.at, self.end)
        return tensor


def gps_layer(nc, x, src, dst, edge_weight, u, s, vt, gnn_bias, wqkv_t, wout_t, bout, ln1_g, ln1_b, wr, codebook_t,
              experts, b2, ws1, bs1_cols, ws2, bs2, ffln_g_cols, ffln_b_cols, wf1, bf1_cols, wf2, bf2, out):
    base = (nc.sbuf_base + 31) // 32 * 32
    top = nc.sbuf_usable_end // 32 * 32

    keep = Region(nc, base, top)
    x_sb = keep.place("x_sb", [P, NT, D])
    ident = keep.place("ident", [128, 128])
    before = keep.place("before", [P, P], BF16)
    ones = keep.place("ones", [P, P], BF16)
    zero_w = keep.place("zero_w", [P, 128], F32R)
    one_row = keep.place("one_row", [1, 128], F32R)
    eps_col = keep.place("eps_col", [P, 1])
    stats = keep.place("stats", [P, NT, 6])
    moments = keep.place("moments", [P, NT, 2])
    std = keep.place("std", [P, NT])
    rstd = keep.place("rstd", [P, NT])
    logits = keep.place("logits", [P, NT, NE])
    top_logit = keep.place("top_logit", [P, NT, 8])
    top_expert = keep.place("top_expert", [P, NT, 8], U32)
    expert_id = keep.place("expert_id", [P, NE])
    expert_i32 = keep.place("expert_i32", [P, NE], I32)
    tile_start_i32 = keep.place("tile_start_i32", [P, 1], I32)
    tile_start = keep.place("tile_start", [P, 1])
    token_id = keep.place("token_id", [P, NT], I32)
    picks = keep.place("picks", [P, NT, 2])
    gap = keep.place("gap", [P, NT])
    gate1 = keep.place("gate1", [P, NT])
    gate2 = keep.place("gate2", [P, NT])
    gates_up = keep.place("gates_up", [P, 2, NT])
    slots_f = keep.place("slots_f", [P, 2, NT])
    slots = keep.place("slots", [P, 2, NT], I32)
    slot_low = keep.place("slot_low", [P, 2, NT], I32)
    slot_high = keep.place("slot_high", [P, 2, NT], I32)
    table_at = keep.place("table_at", [P, 2, NT], I32)
    padded_i32 = keep.place("padded_i32", [P, NE], I32)
    padded = keep.place("padded", [P, NE])
    scan = [keep.place(f"scan{i}", [P, NE]) for i in range(2)]
    starts = keep.place("starts", [P, NE])
    tile_expert_f = keep.place("tile_expert_f", [P, 1])
    tile_expert = keep.place("tile_expert", [P, 1], I32)
    tile_expert_row = keep.place("tile_expert_row", [1, P], I32)
    bodies = keep.place("bodies", [P, 2], I32)
    expert_end = keep.place("expert_end", [P, NE], I32)
    slot_token = keep.place("slot_token", [128, PAIR_TILES], I32)
    no_token = keep.place("no_token", [128, PAIR_TILES], I32)
    bs1_sb = keep.place("bs1_sb", [128, SB])
    mid = Region(nc, keep.at, top)
    q_sb = mid.place("q_sb", [P, NT, D])
    agg_sb = mid.place("agg_sb", [128, NT, PW])
    kv = Region(nc, mid.at, top)
    k_sb = kv.place("k_sb", [P, NT, D])
    v_sb = kv.place("v_sb", [P, NT, PAIRS, 130])
    kv_start, kv_end = mid.at, kv.at
    wqkv_raw = Region(nc, kv_start, kv_end).place("wqkv_raw", [128, KD, 3 * D])
    pe_ = Region(nc, kv_end, top)
    wqkv_hi = pe_.place("wqkv_hi", [128, KD, 3 * D], F32R)
    wqkv_lo = pe_.place("wqkv_lo", [128, KD, 3 * D], F32R)
    u_raw = pe_.place("u_raw", [128, KD, RANK])
    u_hl = pe_.place("u_hl", [128, KD, 2 * RANK], F32R)
    s_row = pe_.place("s_row", [P, RANK])
    t_sb = pe_.place("t_sb", [P, NT, RANK])
    xn = [pe_.place(f"xn{i}", [P, D]) for i in range(2)]
    xnt_hi = [pe_.place(f"xnt_hi{i}", [128, KD, PW], F32R) for i in range(2)]
    xnt_lo = [pe_.place(f"xnt_lo{i}", [128, KD, PW], F32R) for i in range(2)]
    node_of_col = pe_.place("node_of_col", [P, NT, PW], F16)
    node_i32 = nc.alloc_sbuf_tensor_at("node_i32", [P, NT, PW], I32, offset=pe_.at)
    onehot = [pe_.place(f"onehot{i}", [P, NT * PW], F32R) for i in range(OH_RING)]
    rows = [pe_.place(f"rows{i}", [P, BC, RANK]) for i in range(2)]
    rows_hl = [pe_.place(f"rows_hl{i}", [P, BC, 2 * RANK], F32R) for i in range(2)]
    q_exp = [pe_.place(f"q_exp{i}", [P, D]) for i in range(2)]
    q_top = pe_.place("q_top", [P, HEADS])
    q_sum = pe_.place("q_sum", [P, HEADS])
    q_inv = pe_.place("q_inv", [P, HEADS])
    k_top = pe_.place("k_top", [P, D])
    dst_sb = pe_.place("dst_sb", [P, EC], I32)
    src_sb = pe_.place("src_sb", [P, EC], I32)
    src_f = pe_.place("src_f", [P, EC])
    weight_sb = pe_.place("weight_sb", [P, EC])
    batch_dst = [pe_.place(f"batch_dst{i}", [P, BC], I32) for i in range(2)]
    late = Region(nc, kv_end, top)
    hT_hi = late.place("hT_hi", [128, KD, NT, PW], F32R)
    hT_lo = late.place("hT_lo", [128, KD, NT, PW], F32R)
    after_hT = late.at
    wout_raw = late.place("wout_raw", [128, PAIRS, D])
    wout_hi = late.place("wout_hi", [128, PAIRS, D], F32R)
    wout_lo = late.place("wout_lo", [128, PAIRS, D], F32R)
    ctx = late.place("ctx", [128, PAIRS, 128])
    ctxT_hi = late.place("ctxT_hi", [128, PAIRS, 128], F32R)
    ctxT_lo = late.place("ctxT_lo", [128, PAIRS, 128], F32R)
    k_inv = late.place("k_inv", [128, PAIRS])
    k_top_col = late.place("k_top_col", [128, PAIRS])
    k_top_wide = late.place("k_top_wide", [128, PAIRS, P])
    late.at = max(late.at, after_hT + 8 * KD * DSH)
    vt2_raw = late.place("vt2_raw", [128, D])
    vt2_hi = late.place("vt2_hi", [128, D], F32R)
    vt2_lo = late.place("vt2_lo", [128, D], F32R)
    bias_row = late.place("bias_row", [1, D])
    bias_hi = late.place("bias_hi", [1, D], F32R)
    bias_lo = late.place("bias_lo", [1, D], F32R)
    bout_row = late.place("bout_row", [P, D])
    g_row = late.place("g_row", [P, D])
    b_row = late.place("b_row", [P, D])
    wr_raw = late.place("wr_raw", [128, KD, DR])
    wr_hl = late.place("wr_hl", [128, KD, 2 * DR], F32R)
    codebook2 = late.place("codebook2", [128, NE])
    m_hi = late.place("m_hi", [128, PAIRS, D], F32R)
    m_lo = late.place("m_lo", [128, PAIRS, D], F32R)
    upd = Region(nc, kv_start, kv_end)
    q_tile = [upd.place(f"q_tile{i}", [P, D]) for i in range(2)]
    qT_hi = [upd.place(f"qT_hi{i}", [128, PAIRS, PW], F32R) for i in range(2)]
    qT_lo = [upd.place(f"qT_lo{i}", [128, PAIRS, PW], F32R) for i in range(2)]
    agg_hi = [upd.place(f"agg_hi{i}", [128, PW], F32R) for i in range(2)]
    agg_lo = [upd.place(f"agg_lo{i}", [128, PW], F32R) for i in range(2)]
    mixed = [upd.place(f"mixed{i}", [P, D]) for i in range(2)]
    x1 = [upd.place(f"x1_{i}", [P, D]) for i in range(2)]
    z = [upd.place(f"z{i}", [P, D]) for i in range(2)]
    h_tile = [upd.place(f"h_tile{i}", [P, D]) for i in range(2)]
    rT = [upd.place(f"rT{i}", [128, PW]) for i in range(2)]
    x1_parts = [upd.place(f"x1_parts{i}", [P, 6]) for i in range(2)]
    x1_moments = [upd.place(f"x1_moments{i}", [P, 2]) for i in range(2)]
    x1_std = [upd.place(f"x1_std{i}", [P, 1]) for i in range(2)]
    x1_rstd = [upd.place(f"x1_rstd{i}", [P, 1]) for i in range(2)]
    z_var = [upd.place(f"z_var{i}", [P, 1]) for i in range(2)]
    z_std = [upd.place(f"z_std{i}", [P, 1]) for i in range(2)]
    z_rstd = [upd.place(f"z_rstd{i}", [P, 1]) for i in range(2)]

    zone1 = Region(nc, keep.at, kv_end)
    shared = zone1.place("shared", [P, NT, D])
    after_shared = zone1.at
    ws2_hi = zone1.place("ws2_hi", [128, SB, D], F32R)
    ws2_raw = nc.alloc_sbuf_tensor_at("ws2_raw", [128, SB, D], F32, offset=zone1.at)
    ws2_lo = zone1.place("ws2_lo", [128, SB, D], F32R)
    shared_h = [zone1.place(f"shared_h{i}", [128, 4 * PW]) for i in range(SH_RING)]
    bs2_row = zone1.place("bs2_row", [P, D])
    work = zone1.place("work", [P, NT, NE])
    zone2 = Region(nc, after_hT, top)
    ws1_hi = zone2.place("ws1_hi", [128, KD, DSH], F32R)
    ws1_raw = nc.alloc_sbuf_tensor_at("ws1_raw", [128, KD, DSH], F32, offset=zone2.at)
    ws1_lo = zone2.place("ws1_lo", [128, KD, DSH], F32R)
    after_ws1 = zone2.at
    shared_hT_hi = zone2.place("shared_hT_hi", [128, SB, 4 * PW], F32R)
    shared_hT_lo = zone2.place("shared_hT_lo", [128, SB, 4 * PW], F32R)
    combineT = nc.alloc_sbuf_tensor_at("combineT", [NE, NT, P], F32, offset=zone2.at)
    first_pick = zone2.place("first_pick", [P, NT, NE], BF16)
    second_pick = zone2.place("second_pick", [P, NT, NE], BF16)
    picked_any = zone2.place("picked_any", [P, NT, NE], BF16)
    earlier = zone2.place("earlier", [P, NT + 1, NE], BF16)
    b2_sb = zone2.place("b2_sb", [NE, D])
    slot_all = zone2.place("slot_all", [P, NT, NE])
    moe = Region(nc, after_shared, top)
    w_tile = [moe.place(f"w_tile{i}", [128, W_COLS]) for i in range(BODY - 1)]
    up = [moe.place(f"up{i}", [128, 128]) for i in range(2)]
    upT = [moe.place(f"upT{i}", [128, 2, SLOTS]) for i in range(2)]
    moe.at = max(moe.at, kv_end)
    wf1_hi = moe.place("wf1_hi", [128, KD, DFF], F32R)
    wf1_lo = moe.place("wf1_lo", [128, KD, DFF], F32R)
    wf2_hi = moe.place("wf2_hi", [128, 2, D], F32R)
    wf2_lo = moe.place("wf2_lo", [128, 2, D], F32R)
    g_col = moe.place("g_col", [128, KD])
    b_col = moe.place("b_col", [128, KD])
    bf1_raw = moe.place("bf1_raw", [128, 2])
    bf1_sb = moe.place("bf1_sb", [128, 2])
    bf2_row = moe.place("bf2_row", [P, D])
    pair_idx = [moe.place(f"pair_idx{i}", [128, 1], I32) for i in range(3)]
    pair_rows = [moe.place(f"pair_rows{i}", [128, D]) for i in range(3)]
    ring_start = moe.at
    w_ring = moe.place("w_ring", [128, W_RING, W_COLS])
    before_loop = Region(nc, ring_start + EARLY_LOADS * W_COLS * 4, after_ws1)
    wf1_raw = before_loop.place("wf1_raw", [128, KD, DFF])
    wf1_g = before_loop.place("wf1_g", [128, KD, DFF])
    wf2_raw = before_loop.place("wf2_raw", [128, 2, D])
    w_tile.append(moe.place(f"w_tile{BODY - 1}", [128, W_COLS]))
    pair_rowsT = [moe.place(f"pair_rowsT{i}", [128, KD, 128]) for i in range(3)]
    down = [moe.place(f"down{i}", [128, 2, D // 2]) for i in range(3)]
    last_ = Region(nc, ring_start, ring_start + W_RING * W_COLS * 4)
    eo_first = [last_.place(f"eo_first{i}", [P, D]) for i in range(EO_RING)]
    eo_second = [last_.place(f"eo_second{i}", [P, D]) for i in range(EO_RING)]
    hmoe = [last_.place(f"hmoe{i}", [P, D]) for i in range(HM_RING)]
    ff_in = [last_.place(f"ff_in{i}", [P, D]) for i in range(2)]
    hm_parts = [last_.place(f"hm_parts{i}", [P, 6]) for i in range(2)]
    hm_moments = [last_.place(f"hm_moments{i}", [P, 2]) for i in range(2)]
    hm_std = [last_.place(f"hm_std{i}", [P, 1]) for i in range(2)]
    hm_rstd = [last_.place(f"hm_rstd{i}", [P, 1]) for i in range(2)]
    ffT_hi = last_.place("ffT_hi", [128, KD, 4, PW], F32R)
    ffT_lo = last_.place("ffT_lo", [128, KD, 4, PW], F32R)
    ff_h = [last_.place(f"ff_h{i}", [128, 2 * PW]) for i in range(2)]
    ff_hT_hi = last_.place("ff_hT_hi", [128, 2, 4, PW], F32R)
    ff_hT_lo = last_.place("ff_hT_lo", [128, 2, 4, PW], F32R)
    result = [last_.place(f"result{i}", [P, D]) for i in range(2)]

    bank = [nc.alloc_psum_tensor(f"bank{i}", [128, BANK], F32) for i in range(8)]

    t_rows = nc.dram_tensor("t_rows", (N, RANK), F32, kind="Internal").ap()
    h_rows = nc.dram_tensor("h_rows", (N, D), F32, kind="Internal").ap()

    slot_table = nc.dram_tensor("slot_table", (128 * PAIR_TILES, 1), I32, kind="Internal").ap()
    tile_expert_d = nc.dram_tensor("tile_expert_d", (P, 1), I32, kind="Internal").ap()
    expert_rows = nc.dram_tensor("expert_rows", (TILES * SLOTS, D), F32, kind="Internal").ap()

    def sem(name):
        return nc.alloc_semaphore(name)

    def sems(names):
        return [sem(n) for n in names.split()]

    x_loaded = [sem(f"x_loaded{i}") for i in range(NT // 2)]
    wqkv_loaded, edges_loaded = sems(
        "wqkv_loaded edges_loaded")
    moments_done, std_done = sems(
        "moments_done std_done")
    xn_done, xn_turned, xnt_hi_done, xnt_lo_done, t_mm, t_done = sems(
        "xn_done xn_turned xnt_hi_done xnt_lo_done t_mm t_done")
    t_stored, agg_opened, indices_done, chunk_mm, onehot_done = sems(
        "t_stored agg_opened indices_done chunk_mm onehot_done")
    gathered = [sem(f"gathered{i}") for i in range(2)]
    rows_scaled, rows_hi_done, rows_lo_done = sems("rows_scaled rows_hi_done rows_lo_done")
    q_mm, k_mm, v_mm, q_sub_done, q_exp_done = sems(
        "q_mm k_mm v_mm q_sub_done q_exp_done")
    k_top_done, k_copied, v_copied, agg_closed, agg_copied = sems("k_top_done k_copied v_copied agg_closed agg_copied")
    wout_loaded, = sems(
        "wout_loaded")
    k_top_turned, k_top_wide_done, k_top_back, k_sub_done, k_exp_done = sems(
        "k_top_turned k_top_wide_done k_top_back k_sub_done k_exp_done")
    ctx_mm, ctx_done, ctx_turned, ctxT_hi_done, ctxT_lo_done = sems(
        "ctx_mm ctx_done ctx_turned ctxT_hi_done ctxT_lo_done")
    m_mm, m_hi_done, m_lo_done = sems(
        "m_mm m_hi_done m_lo_done")
    xb_done, q_tile_done, q_turned, qT_hi_done, qT_lo_done, agg_hi_done, agg_lo_done, g_mm, y_mm = sems(
        "xb_done q_tile_done q_turned qT_hi_done qT_lo_done agg_hi_done agg_lo_done g_mm y_mm")
    g_relu_done, y_sum_done, x1_done, x1_moments_done, x1_std_done, x1_rstd_done, z_var_done = sems(
        "g_relu_done y_sum_done x1_done x1_moments_done x1_std_done x1_rstd_done z_var_done")
    z_done, z_std_done, z_rstd_done = sems("z_done z_std_done z_rstd_done")
    res_done, h_done, h_turned, hT_hi_done, hT_lo_done, r_mm, rT_done, l_mm, logits_done, picked = sems(
        "res_done h_done h_turned hT_hi_done hT_lo_done r_mm rT_done l_mm logits_done picked")
    zeroed = sem("zeroed")
    gnn_loaded, update_loaded = sems("gnn_loaded update_loaded")
    pair_index_done, x1_parts_done = sems("pair_index_done x1_parts_done")
    made, made_dve, dve_step, halves_hi, halves_lo = sems("made made_dve dve_step halves_hi halves_lo")
    h_stored = [sem(f"h_stored{i}") for i in range(2)]
    ws1_loaded, ws2_loaded = sems("ws1_loaded ws2_loaded")
    earlier_done, gap_done = sems(
        "earlier_done gap_done")
    gap_exp, rank_mm = sems("gap_exp rank_mm")
    tables_done, tile_expert_moved, table_written, table_moved = sems(
        "tables_done tile_expert_moved table_written table_moved")
    shared_up, shared_act, shared_lo_done, shared_down, shared_done = sems(
        "shared_up shared_act shared_lo_done shared_down shared_done")
    combine_done, combine_turned, combineT_done = sems(
        "combine_done combine_turned combineT_done")
    ffw_loaded, wf1_g_done, bf1_mm, bf1_done = sems(
        "ffw_loaded wf1_g_done bf1_mm bf1_done")
    experts_here, w_copied = sems("experts_here w_copied")
    w_loaded = [sem(f"w_loaded{i}") for i in range(W_RING)]
    pair_fetched = [sem(f"pair_fetched{i}") for i in range(3)]
    pair_turned, pairT_done, up_mm, up_copied, up_turned, up_act, down_mm, down_copied = sems(
        "pair_turned pairT_done up_mm up_copied up_turned up_act down_mm down_copied")
    down_stored = [sem(f"down_stored{i}") for i in range(3)]
    eo_fetched = [sem(f"eo_fetched{i}") for i in range(EO_RING)]
    hm_done, hm_moments_done, hm_std_done, hm_rstd_done, ff_in_done, hm_kept, bf2_added = sems(
        "hm_done hm_moments_done hm_std_done hm_rstd_done ff_in_done hm_kept bf2_added")
    ff_turned, ffT_hi_done, ffT_lo_done, ff_up, ff_act, ff_h_lo_done, ff_down, result_done = sems(
        "ff_turned ffT_hi_done ffT_lo_done ff_up ff_act ff_h_lo_done ff_down result_done")
    result_stored = [sem(f"result_stored{i}") for i in range(2)]

    x_v = x.rearrange("(p t) d -> p t d", t=NT)
    out_v = out.rearrange("(p t) d -> p t d", t=NT)
    h_rows_v = h_rows.rearrange("(p t) d -> p t d", t=NT)
    WIDE = 112

    def load_tokens(eng, to, of, signal):
        eng.dma_start(to[0:WIDE], of[0:WIDE]).then_inc(signal, 16)
        eng.dma_start(to[WIDE:P], of[WIDE:P]).then_inc(signal, 16)

    def turned(b):
        return bank[b][:, 0:KD * PW].rearrange("p (k c) -> p k c", k=KD)

    block = nc.Block()
    block.__enter__()

    @block.sync
    def _(sp):
        for i in range(NT // 2):
            load_tokens(sp, x_sb[:, 2 * i:2 * i + 2, :], x_v[:, 2 * i:2 * i + 2, :], x_loaded[i])
        sp.dma_start(u_raw[:], u.rearrange("(k p) r -> p k r", p=128)).then_inc(gnn_loaded, 16)
        sp.dma_start(s_row[:], s.partition_broadcast(P)).then_inc(gnn_loaded, 16)
        sp.dma_start(wqkv_raw[:], wqkv_t.rearrange("(k p) c -> p k c", p=128)).then_inc(wqkv_loaded, 16)
        sp.dma_start(src_sb[:], src).then_inc(edges_loaded, 16)
        sp.dma_start(dst_sb[:], dst).then_inc(edges_loaded, 16)
        sp.dma_start(weight_sb[:], edge_weight).then_inc(edges_loaded, 16)
        sp.wait_ge(made, MADE_IDS)
        sp.dma_start(slot_table.rearrange("(p j) a -> p (j a)", p=128), no_token[:]).then_inc(table_moved, 16)
        sp.wait_ge(t_done, done(NT - 1))
        sp.dma_start(t_rows.rearrange("(p t) r -> p t r", t=NT), t_sb[:]).then_inc(t_stored, 16)
        sp.wait_ge(agg_closed, 1)
        sp.dma_start(wout_raw[:], wout_t.rearrange("(k p) c -> p k c", p=128)).then_inc(wout_loaded, 16)
        for i in range(2):
            sp.dma_start(vt2_raw[RANK * i:RANK * (i + 1)], vt).then_inc(update_loaded, 16)
        sp.dma_start(bias_row[:], gnn_bias).then_inc(update_loaded, 16)
        for to, of in ((bout_row, bout), (g_row, ln1_g), (b_row, ln1_b)):
            sp.dma_start(to[:], of.partition_broadcast(P)).then_inc(update_loaded, 16)
        sp.dma_start(wr_raw[:], wr.rearrange("(k p) r -> p k r", p=128)).then_inc(update_loaded, 16)
        for i in range(2):
            sp.dma_start(codebook2[DR * i:DR * (i + 1)], codebook_t).then_inc(update_loaded, 16)
        sp.wait_ge(m_lo_done, PAIRS)
        sp.dma_start(ws1_raw[:], ws1.rearrange("(k p) f -> p k f", p=128)).then_inc(ws1_loaded, 16)
        sp.dma_start(bs1_sb[:], bs1_cols).then_inc(ws1_loaded, 16)
        with sp.Fori(0, NT // 2) as it:
            for par in range(2):
                t = 2 * it + par
                sp.wait_ge(h_done, done(t))
                sp.dma_start(h_rows_v[:, t, :], h_tile[par][:]).then_inc(h_stored[par], 16)
        for par in range(2):
            sp.wait_ge(h_stored[par], 16 * (NT // 2))
        sp.wait_ge(picked, NT)
        sp.wait_ge(l_mm, done(NT - 1))
        sp.wait_ge(res_done, done(NT - 1))
        sp.dma_start(ws2_raw[:], ws2.rearrange("(k p) f -> p k f", p=128)).then_inc(ws2_loaded, 16)
        sp.dma_start(bs2_row[:], bs2.partition_broadcast(P)).then_inc(ws2_loaded, 16)
        sp.dma_start(b2_sb[:], b2).then_inc(ws2_loaded, 16)
        sp.wait_ge(tables_done, TABLE_TILES)
        sp.dma_start(tile_expert_d, tile_expert[:]).then_inc(tile_expert_moved, 16)
        sp.wait_ge(tile_expert_moved, 16)
        sp.dma_start(tile_expert_row[:], tile_expert_d.rearrange("p a -> a p")).then_inc(tile_expert_moved, 16)
        sp.wait_ge(table_written, 16 * 2 * NT)
        sp.dma_start(slot_token[:], slot_table.rearrange("(p j) a -> p (j a)", p=128)).then_inc(table_moved, 16)
        sp.wait_ge(shared_up, len(GROUPS) * SB)
        for to, of in ((wf1_raw, wf1.rearrange("(k p) f -> p k f", p=128)), (wf2_raw, wf2.rearrange("(k p) f -> p k f", p=128)),
                       (g_col, ffln_g_cols), (b_col, ffln_b_cols), (bf1_raw, bf1_cols), (bf2_row, bf2.partition_broadcast(P))):
            sp.dma_start(to[:], of).then_inc(ffw_loaded, 16)
        for e in range(EARLY_LOADS):
            sp.dma_start(w_ring[:, slot_of(e), :], experts[e]).then_inc(w_loaded[e], 16)
        sp.wait_ge(shared_done, NT)
        sp.wait_ge(halves_lo, SPLIT["wf2"])
        sp.wait_ge(bf1_done, 1)
        sp.wait_ge(tables_done, TABLE_ENDS)

        def relay(e, turn):
            sp.wait_ge(w_loaded[e], 16 * turn)
            sp.sem_inc(experts_here, 1)

        for e in range(EARLY_LOADS, W_RING):
            sp.dma_start(w_ring[:, slot_of(e), :], experts[e]).then_inc(w_loaded[e], 16)
        for e in range(W_RING - RELAY_LAG):
            relay(e, 1)
        with sp.Fori(1, NE // W_RING) as it:
            for e in range(W_RING):
                end = sp.value_load(expert_end[0:1, bass.ds(W_RING * it + (e - W_RING), 1)], min_val=0, max_val=TILES)
                sp.wait_ge(w_copied, end + 1)
                sp.dma_start(w_ring[:, slot_of(e), :], experts[bass.ds(W_RING * it + e, 1), :, :].rearrange("a p c -> p (a c)")
                             ).then_inc(w_loaded[e], 16)
                if e < RELAY_LAG:
                    relay(e - RELAY_LAG + W_RING, it)
                else:
                    relay(e - RELAY_LAG, it + 1)
        for e in range(W_RING - RELAY_LAG, W_RING):
            relay(e, NE // W_RING)
        for t in range(NT):
            sp.wait_ge(result_done, t + 1)
            load_tokens(sp, out_v[:, t, :], result[t % 2], result_stored[t % 2])
        for par in range(2):
            sp.wait_ge(result_stored[par], 32 * (NT // 2))

    @block.gpsimd
    def _(pool):
        pool.sem_inc(res_done, AHEAD)
        pool.sem_inc(pair_index_done, 3)

        def keep_hm(t):
            pool.wait_ge(hm_done, t + 1)
            pool.wait_ge(bf2_added, t + 1)
            pool.tensor_tensor(x_sb[:, t, :], x_sb[:, t, :], hmoe[t % HM_RING][:], ALU.add).then_inc(hm_kept, 1)

        pool.iota(node_i32[:], [[1, NT], [NT, PW]], base=0, channel_multiplier=0).then_inc(made, 1)
        pool.memset(ident[:], 0.0).then_inc(made, 1)
        pool.memset(before[:], 0.0).then_inc(made, 1)
        pool.memset(ones[:], 1.0).then_inc(made, 1)
        pool.memset(eps_col[:], EPS).then_inc(made, 1)
        pool.memset(zero_w[:].bitcast(F32), 0.0).then_inc(made, 1)
        pool.memset(one_row[:].bitcast(F32), 1.0).then_inc(made, 1)
        pool.wait_ge(made, MADE_FILLS)
        pool.affine_select(out=ident[:], in_=ident[:], compare_op=ALU.not_equal, fill=1.0, base=0,
                           pattern=[[-1, 128]], channel_multiplier=1).then_inc(made, 1)
        pool.affine_select(out=before[:], in_=before[:], compare_op=ALU.is_ge, fill=1.0, base=0,
                           pattern=[[-1, P]], channel_multiplier=1).then_inc(made, 1)
        pool.iota(expert_i32[:], [[1, NE]], base=0, channel_multiplier=0).then_inc(made, 1)
        pool.iota(tile_start_i32[:], [[0, 1]], base=0, channel_multiplier=SLOTS).then_inc(made, 1)
        pool.iota(token_id[:], [[1, NT]], base=0, channel_multiplier=NT).then_inc(made, 1)
        pool.memset(no_token[:], 0).then_inc(made, 1)
        pool.wait_ge(made_dve, MADE_NODE_COLS)
        pool.memset(onehot[0][:].bitcast(F32), 0.0).then_inc(made, 1)
        pool.wait_ge(edges_loaded, 48)
        with pool.Fori(0, NT // 2) as it:
            for step in range(4):
                half = step % 2
                batch = 4 * it + step
                pool.wait_ge(rows_lo_done, freed(batch))
                pool.tensor_copy(batch_dst[half][:], dst_sb[:, bass.ds(batch * BC, BC)]).then_inc(indices_done, 1)
                pool.wait_ge(t_stored, 16)
                pool.wait_ge(indices_done, batch + 1)
                for c in range(BC):
                    pool.indirect_dma_start(rows[half][:, c, :], None, t_rows,
                                            bass.IndirectOffsetOnAxis(ap=batch_dst[half][:, c:c + 1], axis=0)
                                            ).then_inc(gathered[half], 16)
        pool.wait_ge(halves_lo, SPLIT["wqkv"])
        pool.wait_ge(update_loaded, 144)
        pool.wait_ge(agg_closed, 1)
        pool.memset(hT_hi[:, :, :, P:PW].bitcast(F32), 0.0).then_inc(zeroed, 1)
        pool.memset(hT_lo[:, :, :, P:PW].bitcast(F32), 0.0).then_inc(zeroed, 1)
        pool.memset(ctx[:], 0.0).then_inc(zeroed, 1)
        with pool.Fori(0, NT) as t:
            pool.tensor_tensor(x_sb[:, t, :], x_sb[:, t, :], bout_row[:], ALU.add).then_inc(xb_done, 1)
        with pool.Fori(0, NT // 2) as it:
            for par in range(2):
                t = 2 * it + par
                pool.wait_ge(z_done, done(t))
                pool.wait_ge(x1_done, done(t))
                pool.tensor_tensor(x_sb[:, t, :], x1[par][:], z[par][:], ALU.add).then_inc(res_done, 1)
        pool.wait_ge(table_moved, 16 * (1 + UNSURE))
        pool.wait_ge(tables_done, TABLE_SLOTS)
        for which in range(2):
            for t in range(NT):
                pool.indirect_dma_start(slot_table, bass.IndirectOffsetOnAxis(ap=table_at[:, which, t:t + 1], axis=0),
                                        token_id[:, t:t + 1], None).then_inc(table_written, 16)
        pool.wait_ge(shared_up, len(GROUPS) * SB)
        pool.wait_ge(table_moved, 16 * (2 + UNSURE))

        def fetch_pair(q, v):
            pool.wait_ge(pair_turned, tile_freed(q, 3))
            pool.tensor_copy(pair_idx[v][:], slot_token[:, bass.ds(q, 1)]).then_inc(pair_index_done, 1)
            pool.wait_ge(table_moved, 16 * (2 + UNSURE))
            pool.wait_ge(pair_index_done, q + 4)
            pool.indirect_dma_start(pair_rows[v][:], None, h_rows,
                                    bass.IndirectOffsetOnAxis(ap=pair_idx[v][:], axis=0)).then_inc(pair_fetched[v], 16)

        def store_pair(q, v):
            for par in range(2):
                j = 2 * q + par
                pool.wait_ge(down_copied, j + 1)
                pool.dma_start(expert_rows[bass.ds(j * SLOTS, SLOTS), :].rearrange("s (h c) -> h s c", h=2),
                               down[v][:, par, :]).then_inc(down_stored[v], 16)

        pool.wait_ge(tables_done, TABLE_BODIES)
        run = pool.value_load(bodies[0:1, 0:1], min_val=STEPS_MIN, max_val=STEPS)
        run_less_one = pool.value_load(bodies[0:1, 1:2], min_val=STEPS_MIN - 1, max_val=STEPS - 1)
        fetch_pair(0, 0)
        pool.wait_ge(ffw_loaded, 96)
        pool.wait_ge(res_done, done(NT - 1))
        for t in range(NT):
            pool.tensor_tensor(x_sb[:, t, :], x_sb[:, t, :], bf2_row[:], ALU.add).then_inc(bf2_added, 1)
        pool.wait_ge(shared_done, NT)
        for q in range(1, 6):
            fetch_pair(q, q % 3)
            if q >= STORE_LAG:
                store_pair(q - STORE_LAG, (q - STORE_LAG) % 3)
        with pool.Fori(2, STEPS) as it:
            with pool.If(it <= run):
                for v in range(3):
                    fetch_pair(3 * it + v, v)
                    store_pair(3 * it + v - STORE_LAG, (v - STORE_LAG) % 3)
        with pool.If(run >= STEPS):
            for q in range(TILES // 2 - STORE_LAG, TILES // 2):
                store_pair(q, q % 3)
            for v in range(3):
                pool.wait_ge(down_stored[v], 32 * STEPS)
        with pool.If(run < STEPS):
            for v, stored in enumerate((run, run, run_less_one)):
                pool.wait_ge(down_stored[v], 32 * stored)
        pool.wait_ge(w_copied, copied(TILES - 1))
        pool.memset(ffT_hi[:, :, :, P:PW].bitcast(F32), 0.0).then_inc(zeroed, 1)
        pool.memset(ffT_lo[:, :, :, P:PW].bitcast(F32), 0.0).then_inc(zeroed, 1)
        for t in range(NT):
            if t >= EO_RING:
                keep_hm(t - EO_RING)
            for to, which in ((eo_first, 0), (eo_second, 1)):
                pool.indirect_dma_start(to[t % EO_RING][:], None, expert_rows,
                                        bass.IndirectOffsetOnAxis(ap=slots[:, which, t:t + 1], axis=0)
                                        ).then_inc(eo_fetched[t % EO_RING], 16)
        for t in range(NT - EO_RING, NT):
            keep_hm(t)

    @block.scalar
    def _(act):
        for signal in (g_relu_done, xnt_hi_done, rows_scaled, rows_hi_done, q_exp_done, k_copied, v_copied,
                       q_tile_done, qT_hi_done, agg_hi_done, hT_hi_done, rT_done, x1_std_done, z_std_done):
            act.sem_inc(signal, AHEAD)
        for signal in (up_act, pairT_done):
            act.sem_inc(signal, BODY)
        act.wait_ge(gnn_loaded, 32)
        act.activation(u_hl[:, :, 0:RANK], u_raw[:], ACT.Copy).then_inc(halves_hi, 1)
        act.wait_ge(moments_done, NT)
        act.wait_ge(made, MADE_FILLS)
        act.activation(std[:], moments[:, :, 1], ACT.Sqrt, bias=eps_col[:]).then_inc(std_done, 1)


        def high_step(it, n):
            t, par, _ = tiles_of(it, n)(0)
            act.wait_ge(xn_turned, done(t))
            act.wait_ge(t_mm, freed(t))
            act.activation(xnt_hi[par][:, :, 0:P], turned(6 + par)[:, :, 0:P], ACT.Copy).then_inc(xnt_hi_done, 1)

        high_step(0, 0)
        high_step(0, 1)
        act.wait_ge(wqkv_loaded, 16)
        with act.Fori(1, NT // 2) as it:
            act.activation(wqkv_hi[:, bass.ds(it - 1, 1), :], wqkv_raw[:, bass.ds(it - 1, 1), :], ACT.Copy).then_inc(halves_hi, 1)
            high_step(it, 0)
            high_step(it, 1)
        act.wait_ge(halves_lo, SPLIT["wqkv"])

        def scale_rows(batch, half, turn):
            act.wait_ge(gathered[half], 16 * BC * (turn + 1))
            for c in range(BC):
                last = act.activation(rows[half][:, c, :], rows[half][:, c, :], ACT.Copy,
                                      scale=weight_sb[:, bass.ds(batch * BC + c, 1)])
            last.then_inc(rows_scaled, 1)
            act.wait_ge(rows_scaled, done(batch))
            act.wait_ge(chunk_mm, BC * (batch - 1) + CHUNK_AHEAD)
            act.activation(rows_hl[half][:, :, 0:RANK], rows[half][:], ACT.Copy).then_inc(rows_hi_done, 1)

        act.wait_ge(t_mm, done(NT - 1))
        act.wait_ge(edges_loaded, 48)
        act.wait_ge(made_dve, MADE_EDGES)

        def xnt_high(t, par):
            act.wait_ge(xn_turned, done(NT + t))
            act.wait_ge(v_mm, freed(t))
            act.activation(xnt_hi[par][:, :, 0:P], turned(6 + par)[:, :, 0:P], ACT.Copy).then_inc(xnt_hi_done, 1)

        def act_tiles(it, final=False):
            for par in range(2):
                t = 2 * it + par
                more = not (final and par)
                scale_rows(2 * t + 1, 1, t)
                act.wait_ge(q_sub_done, done(t))
                act.activation(q_exp[par][:], q_exp[par][:], ACT.Exp).then_inc(q_exp_done, 1)
                if more:
                    xnt_high(t + 1, 1 - par)
                act.wait_ge(k_mm, done(t))
                act.activation(k_sb[:, t, :], bank[4][0:P, :], ACT.Copy).then_inc(k_copied, 1)
                if more:
                    scale_rows(2 * t + 2, 0, t + 1)
                act.wait_ge(v_mm, done(t))
                act.activation(v_sb[:, t, :, 0:128], bank[5][0:P, :].rearrange("p (a c) -> p a c", a=PAIRS),
                               ACT.Copy).then_inc(v_copied, 1)

        xnt_high(0, 0)
        scale_rows(0, 0, 0)
        with act.Fori(0, NT // 2 - 1) as it:
            act_tiles(it)
        act_tiles(NT // 2 - 1, final=True)
        act.wait_ge(agg_closed, 1)
        for b, (lo, hi) in enumerate(GROUPS):
            act.activation(agg_sb[:, lo:hi, :], bank[b][:, 0:(hi - lo) * PW].rearrange("p (t c) -> p t c", c=PW),
                           ACT.Copy).then_inc(agg_copied, 1)
        with act.Fori(0, NT) as t:
            act.wait_ge(k_sub_done, t + 1)
            act.activation(k_sb[:, t, :], k_sb[:, t, :], ACT.Exp).then_inc(k_exp_done, 1)
        act.wait_ge(wout_loaded, 16)
        act.activation(wout_hi[:], wout_raw[:], ACT.Copy).then_inc(halves_hi, 1)
        act.wait_ge(update_loaded, 144)
        act.activation(vt2_hi[:], vt2_raw[:], ACT.Copy).then_inc(halves_hi, 1)
        act.wait_ge(update_loaded, 144)
        act.activation(wr_hl[:, :, 0:DR], wr_raw[:], ACT.Copy).then_inc(halves_hi, 1)
        act.activation(bias_hi[:], bias_row[:], ACT.Copy).then_inc(halves_hi, 1)
        act.wait_ge(k_top_wide_done, 1)
        for n in range(UNSURE):
            act.dma_start(expert_rows[TILES * SLOTS - (n + 1) * N:TILES * SLOTS - n * N, :].rearrange("(p t) d -> p t d", t=NT),
                         q_sb[:]).then_inc(table_moved, 16)
        act.wait_ge(ctx_turned, 1)
        act.activation(ctxT_hi[:], bank[5][:, :].rearrange("p (a c) -> p a c", a=PAIRS), ACT.Copy).then_inc(ctxT_hi_done, 1)
        for pair in range(PAIRS):
            act.wait_ge(m_mm, pair + 1)
            act.activation(m_hi[:, pair, :], bank[(3, 4, 6, 7)[pair]][:, :], ACT.Copy).then_inc(m_hi_done, 1)
        def fetch_q(t, par):
            act.wait_ge(q_turned, freed(t))
            act.activation(q_tile[par][:], q_sb[:, t, :], ACT.Copy).then_inc(q_tile_done, 1)
            act.wait_ge(g_mm, freed(t))
            act.activation(agg_hi[par][:], agg_sb[:, t, :], ACT.Copy).then_inc(agg_hi_done, 1)

        def act_update(it, n):
            tile = tiles_of(it, n)
            if isinstance(it, int) and it >= NT // 2:
                k = 2 * it + n - NT
                act.wait_ge(ws1_loaded, 32)
                act.activation(ws1_hi[:, k, :], ws1_raw[:, k, :], ACT.Copy).then_inc(halves_hi, 1)
            t, par, _ = tile(0)
            if t is not None:
                fetch_q(t, par)
            t, par, _ = tile(3)
            if t is not None:
                act.wait_ge(h_turned, done(t))
                act.activation(hT_hi[:, :, t, 0:P], turned(7 * par)[:, :, 0:P], ACT.Copy).then_inc(hT_hi_done, 1)
            t, par, _ = tile(0)
            if t is not None:
                act.wait_ge(q_turned, done(t))
                act.wait_ge(y_mm, freed(t))
                act.activation(qT_hi[par][:, :, 0:P], turned(7 * par)[:, :, 0:P], ACT.Copy).then_inc(qT_hi_done, 1)
            t, par, _ = tile(2)
            if t is not None:
                act.wait_ge(x1_moments_done, done(t))
                act.wait_ge(x1_rstd_done, freed(t))
                act.activation(x1_std[par][:], x1_moments[par][:, 1:2], ACT.Sqrt, bias=eps_col[:]).then_inc(x1_std_done, 1)
                act.wait_ge(z_var_done, done(t))
                act.wait_ge(z_rstd_done, freed(t))
                act.activation(z_std[par][:], z_var[par][:], ACT.Sqrt, bias=eps_col[:]).then_inc(z_std_done, 1)
            t, par, _ = tile(1)
            if t is not None:
                act.wait_ge(g_mm, done(t))
                act.wait_ge(x1_done, freed(t))
                act.activation(mixed[par][:], bank[3 + par][0:P, :], ACT.Relu).then_inc(g_relu_done, 1)
            t, par, _ = tile(3)
            if t is not None:
                act.wait_ge(r_mm, done(t))
                act.wait_ge(l_mm, freed(t))
                act.activation(rT[par][:], bank[5 + par][:, 0:PW], ACT.Copy).then_inc(rT_done, 1)

        update_steps(act, act_update)

        act.wait_ge(gap_done, 1)
        act.activation(gap[:], gap[:], ACT.Exp).then_inc(gap_exp, 1)
        act.wait_ge(res_done, done(NT - 1))
        for par in range(2):
            act.wait_ge(h_stored[par], 16 * (NT // 2))
        for g, (lo, hi) in enumerate(GROUPS):
            for fb in range(SB):
                n = g * SB + fb
                act.wait_ge(shared_up, n + 1)
                if n >= SH_RING:
                    act.wait_ge(shared_lo_done, n - SH_RING + 1)
                act.activation(shared_h[fb % SH_RING][:, 0:(hi - lo) * PW], bank[3 + fb % 2][:, 0:(hi - lo) * PW], ACT.Silu,
                               bias=bs1_sb[:, fb:fb + 1]).then_inc(shared_act, 1)
                if n == 2:
                    act.wait_ge(ws2_loaded, 48)
                    act.activation(ws2_hi[:], ws2_raw[:], ACT.Copy).then_inc(halves_hi, 1)
            if g == 0:
                act.wait_ge(combine_turned, NT)
                for n, (first, end) in enumerate(GROUPS):
                    act.activation(combineT[:, first:end, :], bank[n][0:NE, 0:128 * (end - first)].rearrange("p (t c) -> p t c", c=128)[:, :, 0:P],
                                   ACT.Copy).then_inc(combineT_done, 1)
        act.wait_ge(wf1_g_done, KD)
        act.activation(wf1_hi[:], wf1_g[:], ACT.Copy).then_inc(halves_hi, 1)
        act.activation(wf2_hi[:], wf2_raw[:], ACT.Copy).then_inc(halves_hi, 1)

        def take_down(j, n, turn):
            v, par = n // 2, n % 2
            act.wait_ge(down_mm, tile_done(j))
            if par == 0:
                act.wait_ge(down_stored[v], 32 * turn)
            act.activation(down[v][:, par, :], bank[6 + par][:, 0:D // 2], ACT.Copy).then_inc(down_copied, 1)

        def turn_pair(q, v):
            act.wait_ge(pair_turned, tile_done(q))
            act.wait_ge(up_mm, tile_freed(2 * q, BODY))
            act.activation(pair_rowsT[v][:], bank[v % 2][:, :].rearrange("p (k c) -> p k c", k=KD), ACT.Copy).then_inc(pairT_done, 1)

        def act_step(it, first=False, final=False):
            for n in range(BODY):
                j = BODY * it + n
                par = n % 2
                if n % 2 == 0 and not (final and n + 2 == BODY):
                    v = n // 2 + 1
                    turn_pair(BODY // 2 * it + v, v % 3)
                act.wait_ge(up_turned, tile_done(j))
                act.wait_ge(down_mm, tile_freed(j, 2))
                act.wait_ge(w_copied, copied(j))
                for half in range(2):
                    last = act.activation(upT[par][:, half, :], bank[4 + par][:, SLOTS * half:SLOTS * (half + 1)], ACT.Silu,
                                          bias=w_tile[n][:, B1_AT + half:B1_AT + half + 1])
                last.then_inc(up_act, 1)
                if not (first and n == 0):
                    take_down(j - 1, (n - 1) % BODY, it)

        def act_skip(it, final=False):
            act.wait_ge(pairT_done, tile_done(BODY // 2 * it))
            act.sem_inc(pairT_done, BODY // 2 - final)
            act.wait_ge(up_act, tile_done(BODY * it - 1))
            act.sem_inc(up_act, BODY)
            act.wait_ge(down_copied, BODY * it - 1)
            act.sem_inc(down_copied, BODY + final)

        turn_pair(0, 0)
        act.wait_ge(tables_done, TABLE_BODIES)
        run = act.value_load(bodies[0:1, 0:1], min_val=STEPS_MIN, max_val=STEPS)
        act_step(0, first=True)
        with act.Fori(1, STEPS - 1) as it:
            with act.If(it < run):
                act_step(it)
            with act.If(it >= run):
                act_skip(it)
        with act.If(run >= STEPS):
            act_step(STEPS - 1, final=True)
            take_down(TILES - 1, BODY - 1, STEPS - 1)
        with act.If(run < STEPS):
            act_skip(STEPS - 1, final=True)
        def spread(t):
            act.wait_ge(hm_moments_done, t + 1)
            if t >= 2:
                act.wait_ge(hm_rstd_done, t - 1)
            act.activation(hm_std[t % 2][:], hm_moments[t % 2][:, 1:2], ACT.Sqrt, bias=eps_col[:]).then_inc(hm_std_done, 1)

        spread(0)
        for step in range(NT + 2):
            if step < NT:
                t = step
                act.wait_ge(ff_turned, t + 1)
                if t >= 4:
                    act.wait_ge(ff_up, 2 * (t // 2 - 1))
                act.activation(ffT_hi[:, :, t % 4, 0:P], turned(t % 2)[:, :, 0:P], ACT.Copy).then_inc(ffT_hi_done, 1)
            if step >= 2:
                item, half = step - 2, step % 2
                act.wait_ge(ff_up, item + 1)
                if item >= 2:
                    act.wait_ge(ff_h_lo_done, item - 1)
                act.activation(ff_h[half][:], bank[2 + half][:, 0:2 * PW], ACT.Silu, bias=bf1_sb[:, half:half + 1]).then_inc(ff_act, 1)
            if step + 1 < NT:
                spread(step + 1)

    @block.vector
    def _(dve):
        for signal in (xn_done, xnt_lo_done, t_done, rows_lo_done, q_sub_done, k_top_done, qT_lo_done,
                       agg_lo_done, y_sum_done, x1_done, x1_parts_done, x1_moments_done, z_var_done, x1_rstd_done, z_done, z_rstd_done,
                       h_done, hT_lo_done, logits_done):
            dve.sem_inc(signal, AHEAD)
        dve.sem_inc(up_copied, BODY)
        dve.sem_inc(w_copied, 1)
        own = Steps()
        dve.wait_ge(made, MADE_NODES)
        dve.tensor_copy(node_of_col[:], node_i32[:]).then_inc(made_dve, 1)
        dve.wait_ge(made, MADE_IDS)
        dve.tensor_copy(expert_id[:], expert_i32[:]).then_inc(made_dve, 1)
        dve.tensor_copy(tile_start[:], tile_start_i32[:]).then_inc(made_dve, 1)
        for t in range(NT):
            if t % 2 == 0:
                dve.wait_ge(x_loaded[t // 2], 32)
            dve.bn_stats(stats[:, t, :], x_sb[:, t, :]).then_inc(dve_step, own.one())
        for t in range(NT):
            dve.wait_ge(dve_step, own.now())
            dve.bn_aggr(moments[:, t, :], stats[:, t, :]).then_inc(moments_done, 1)
        dve.wait_ge(std_done, 1)
        dve.reciprocal(rstd[:], std[:]).then_inc(dve_step, own.one())
        dve.wait_ge(halves_hi, SPLIT["u"])
        dve.tensor_tensor(u_hl[:, :, RANK:2 * RANK], u_raw[:], u_hl[:, :, 0:RANK].bitcast(F32),
                          ALU.subtract).then_inc(halves_lo, 1)
        dve.wait_ge(dve_step, own.now())
        dve.wait_ge(gnn_loaded, 32)

        def normed(t, par, item):
            dve.wait_ge(xn_turned, freed(item))
            dve.tensor_scalar(xn[par][:], x_sb[:, t, :], moments[:, t, 0:1], rstd[:, bass.ds(t, 1)],
                              ALU.subtract, ALU.mult).then_inc(xn_done, 1)

        def xnt_low(par, item):
            dve.wait_ge(xnt_hi_done, done(item))
            dve.tensor_tensor(xnt_lo[par][:, :, 0:P], turned(6 + par)[:, :, 0:P],
                              xnt_hi[par][:, :, 0:P].bitcast(F32), ALU.subtract).then_inc(xnt_lo_done, 1)

        def rank_step(it, n):
            tile = tiles_of(it, n)
            t, par, _ = tile(0)
            if t is not None:
                normed(t, par, t)
            t, par, _ = tile(1)
            if t is not None:
                xnt_low(par, t)
            t, par, _ = tile(2)
            if t is not None:
                dve.wait_ge(t_mm, done(t))
                dve.tensor_copy(t_sb[:, t, :], bank[4 + par][0:P, 0:RANK]).then_inc(dve_step, own.one())
                dve.wait_ge(dve_step, own.now())
                dve.tensor_tensor(t_sb[:, t, :], t_sb[:, t, :], bank[4 + par][0:P, RANK:2 * RANK], ALU.add).then_inc(dve_step, own.one())
                dve.wait_ge(dve_step, own.now())
                dve.tensor_tensor(t_sb[:, t, :], t_sb[:, t, :], s_row[:], ALU.mult).then_inc(t_done, 1)

        rank_step(0, 0)
        rank_step(0, 1)
        with dve.Fori(1, NT // 2) as it, own.loop(it - 1, NT // 2 - 1, 4):
            rank_step(it, 0)
            block_k = bass.ds(it - 1, 1)
            dve.wait_ge(halves_hi, SPLIT["wqkv"] - KD + it)
            dve.tensor_tensor(wqkv_lo[:, block_k, :], wqkv_raw[:, block_k, :], wqkv_hi[:, block_k, :].bitcast(F32),
                              ALU.subtract).then_inc(halves_lo, 1)
            rank_step(it, 1)
        rank_step(NT // 2, 0)
        rank_step(NT // 2, 1)
        dve.wait_ge(edges_loaded, 48)
        dve.tensor_copy(src_f[:], src_sb[:]).then_inc(made_dve, 1)
        dve.wait_ge(halves_lo, SPLIT["wqkv"])
        dve.memset(v_sb[:, :, :, 128:130], 1.0).then_inc(made_dve, 1)
        dve.memset(k_top[:], -3.0e38).then_inc(made_dve, 1)
        dve.wait_ge(made_dve, MADE_EDGES)
        dve.wait_ge(agg_opened, 1)

        def onehots(batch, half, first, last):
            for c in range(first, last):
                chunk = batch * BC + c
                dve.wait_ge(chunk_mm, chunk + 1 - OH_RING + CHUNK_AHEAD)
                dve.tensor_scalar(onehot[(half * BC + c) % OH_RING][:], node_of_col[:].rearrange("p t c -> p (t c)"),
                                  src_f[:, bass.ds(chunk, 1)], None, ALU.is_equal).then_inc(onehot_done, 1)

        def rows_low(batch, half):
            dve.wait_ge(rows_hi_done, done(batch))
            dve.tensor_tensor(rows_hl[half][:, :, RANK:2 * RANK], rows[half][:],
                              rows_hl[half][:, :, 0:RANK].bitcast(F32), ALU.subtract).then_inc(rows_lo_done, 1)

        def softmax_q_start(t, par):
            psq = bank[3][0:P, :].rearrange("p (h c) -> p h c", h=HEADS)
            dve.wait_ge(q_mm, done(t))
            dve.reduce_max(q_top[:], psq, AX.X).then_inc(dve_step, own.one())
            dve.wait_ge(dve_step, own.now())
            dve.tensor_tensor(q_exp[par][:].rearrange("p (h c) -> p h c", h=HEADS), psq,
                              q_top[:].unsqueeze(2).broadcast_to([P, HEADS, RANK]), ALU.subtract).then_inc(q_sub_done, 1)

        def softmax_q_end(t, par):
            qe = q_exp[par][:].rearrange("p (h c) -> p h c", h=HEADS)
            dve.wait_ge(q_exp_done, done(t))
            dve.reduce_sum(q_sum[:], qe, AX.X).then_inc(dve_step, own.one())
            dve.wait_ge(dve_step, own.now())
            dve.reciprocal(q_inv[:], q_sum[:]).then_inc(dve_step, own.one())
            dve.wait_ge(dve_step, own.now())
            dve.tensor_tensor(q_sb[:, t, :].rearrange("p (h c) -> p h c", h=HEADS), qe,
                              q_inv[:].unsqueeze(2).broadcast_to([P, HEADS, RANK]), ALU.mult).then_inc(dve_step, own.one())

        def dve_edge_tiles(it, final=False):
            for par in range(2):
                t = 2 * it + par
                more = not (final and par)
                for c in range(2 * BC):
                    onehots(2 * t + c // BC, c // BC, c % BC, c % BC + 1)
                    if c == 1 and more:
                        normed(t + 1, 1 - par, NT + t + 1)
                    if c == 5:
                        rows_low(2 * t + 1, 1)
                    if c == 8:
                        softmax_q_start(t, par)
                    if c == 11 and more:
                        xnt_low(1 - par, NT + t + 1)
                    if c == 12:
                        softmax_q_end(t, par)
                    if c == 13:
                        dve.wait_ge(k_top_done, freed(t, 1))
                        dve.wait_ge(k_copied, done(t))
                        dve.tensor_tensor(k_top[:], k_top[:], k_sb[:, t, :], ALU.max).then_inc(k_top_done, 1)
                    if c == 14 and more:
                        rows_low(2 * t + 2, 0)

        normed(0, 0, NT)
        xnt_low(0, NT)
        rows_low(0, 0)
        with dve.Fori(0, NT // 2 - 1) as it, own.loop(it, NT // 2 - 1, 8):
            dve_edge_tiles(it)
        dve_edge_tiles(NT // 2 - 1, final=True)
        dve.wait_ge(agg_closed, 1)
        dve.wait_ge(k_top_turned, 1)
        dve.reduce_max(k_top_col[:], turned(6)[:, :, 0:P], AX.X).then_inc(dve_step, own.one())
        dve.wait_ge(dve_step, own.now())
        dve.tensor_copy(k_top_wide[:], k_top_col[:].unsqueeze(2).broadcast_to([128, PAIRS, P])).then_inc(k_top_wide_done, 1)
        dve.wait_ge(k_copied, done(NT - 1))
        dve.wait_ge(k_top_back, 1)
        with dve.Fori(0, NT) as t:
            dve.tensor_tensor(k_sb[:, t, :], k_sb[:, t, :], bank[7][0:P, :], ALU.subtract).then_inc(k_sub_done, 1)
        dve.wait_ge(halves_hi, SPLIT["wout"])
        dve.tensor_tensor(wout_lo[:], wout_raw[:], wout_hi[:].bitcast(F32), ALU.subtract).then_inc(halves_lo, 1)
        dve.wait_ge(halves_hi, SPLIT["vt"])
        dve.tensor_tensor(vt2_lo[:], vt2_raw[:], vt2_hi[:].bitcast(F32), ALU.subtract).then_inc(halves_lo, 1)
        dve.wait_ge(halves_hi, SPLIT["wr"])
        dve.tensor_tensor(wr_hl[:, :, DR:2 * DR], wr_raw[:], wr_hl[:, :, 0:DR].bitcast(F32),
                          ALU.subtract).then_inc(halves_lo, 1)
        dve.wait_ge(halves_hi, SPLIT["bias"])
        dve.tensor_tensor(bias_lo[:], bias_row[:], bias_hi[:].bitcast(F32), ALU.subtract).then_inc(halves_lo, 1)
        dve.wait_ge(ctx_mm, PAIRS)
        dve.wait_ge(zeroed, ZEROED_CTX)
        for pair in range(PAIRS):
            at = 132 * (pair % 2)
            dve.reciprocal(k_inv[:, pair:pair + 1], bank[3 + pair // 2][:, at + 128:at + 129]).then_inc(dve_step, own.one())
        dve.wait_ge(dve_step, own.now())
        for pair in range(PAIRS):
            at = 132 * (pair % 2)
            for h in range(2):
                part = slice(64 * h, 64 * (h + 1))
                dve.tensor_scalar(ctx[part, pair, part], bank[3 + pair // 2][part, at + 64 * h:at + 64 * (h + 1)],
                                  k_inv[part, pair:pair + 1], None, ALU.mult).then_inc(ctx_done, 1)
        dve.wait_ge(ctxT_hi_done, 1)
        dve.tensor_tensor(ctxT_lo[:], bank[5][:, :].rearrange("p (a c) -> p a c", a=PAIRS), ctxT_hi[:].bitcast(F32),
                          ALU.subtract).then_inc(ctxT_lo_done, 1)
        for pair in range(PAIRS):
            dve.wait_ge(m_hi_done, pair + 1)
            dve.tensor_tensor(m_lo[:, pair, :], bank[(3, 4, 6, 7)[pair]][:, :], m_hi[:, pair, :].bitcast(F32),
                              ALU.subtract).then_inc(m_lo_done, 1)
        dve.wait_ge(update_loaded, 144)
        dve.wait_ge(xb_done, NT)
        def dve_update(it, n):
            tile = tiles_of(it, n)
            t, par, _ = tile(2)
            if t is not None:
                dve.wait_ge(y_mm, done(t))
                dve.wait_ge(g_relu_done, done(t))
                dve.tensor_tensor(mixed[par][:], mixed[par][:], bank[1 + par][0:P, :], ALU.add).then_inc(y_sum_done, 1)
                dve.wait_ge(y_sum_done, done(t))
                dve.wait_ge(res_done, freed(t))
                dve.tensor_tensor(x1[par][:], mixed[par][:], x_sb[:, t, :], ALU.add).then_inc(x1_done, 1)
                dve.wait_ge(x1_done, done(t))
                dve.bn_stats(x1_parts[par][:], x1[par][:]).then_inc(x1_parts_done, 1)
                dve.wait_ge(moments_done, NT)
                dve.wait_ge(x1_parts_done, done(t))
                dve.bn_aggr(x1_moments[par][:], x1_parts[par][:]).then_inc(x1_moments_done, 1)
            t, par, _ = tile(3)
            if t is not None:
                dve.wait_ge(hT_hi_done, done(t))
                dve.tensor_tensor(hT_lo[:, :, t, 0:P], turned(7 * par)[:, :, 0:P],
                                  hT_hi[:, :, t, 0:P].bitcast(F32), ALU.subtract).then_inc(hT_lo_done, 1)
            t, par, _ = tile(0)
            if t is not None:
                dve.wait_ge(agg_hi_done, done(t))
                dve.tensor_tensor(agg_lo[par][:], agg_sb[:, t, :], agg_hi[par][:].bitcast(F32),
                                  ALU.subtract).then_inc(agg_lo_done, 1)
            t, par, _ = tile(2)
            if t is not None:
                dve.wait_ge(x1_std_done, done(t))
                dve.reciprocal(x1_rstd[par][:], x1_std[par][:]).then_inc(x1_rstd_done, 1)
                dve.wait_ge(x1_rstd_done, done(t))
                dve.tensor_scalar(z_var[par][:], x1_moments[par][:, 1:2], x1_rstd[par][:], x1_rstd[par][:],
                                  ALU.mult, ALU.mult).then_inc(z_var_done, 1)
                dve.tensor_scalar(z[par][:], x1[par][:], x1_moments[par][:, 0:1], x1_rstd[par][:],
                                  ALU.subtract, ALU.mult).then_inc(z_done, 1)
            t, par, _ = tile(0)
            if t is not None:
                dve.wait_ge(qT_hi_done, done(t))
                dve.tensor_tensor(qT_lo[par][:, :, 0:P], turned(7 * par)[:, :, 0:P],
                                  qT_hi[par][:, :, 0:P].bitcast(F32), ALU.subtract).then_inc(qT_lo_done, 1)
            t, par, turn = tile(2)
            if t is not None:
                dve.wait_ge(z_std_done, done(t))
                dve.reciprocal(z_rstd[par][:], z_std[par][:]).then_inc(z_rstd_done, 1)
                dve.wait_ge(z_rstd_done, done(t))
                dve.wait_ge(h_turned, freed(t))
                if not (isinstance(turn, int) and turn == 0):
                    dve.wait_ge(h_stored[par], 16 * turn)
                dve.scalar_tensor_tensor(h_tile[par][:], z[par][:], z_rstd[par][:], g_row[:],
                                         ALU.mult, ALU.mult).then_inc(dve_step, own.one())
            if t is not None:
                dve.wait_ge(dve_step, own.now())
                dve.tensor_tensor(h_tile[par][:], h_tile[par][:], b_row[:], ALU.add).then_inc(h_done, 1)
            if isinstance(it, int) and it >= NT // 2:
                k = 2 * it + n - NT
                dve.wait_ge(halves_hi, SPLIT["ws1"] - KD + k + 1)
                dve.tensor_tensor(ws1_lo[:, k, :], ws1_raw[:, k, :], ws1_hi[:, k, :].bitcast(F32), ALU.subtract).then_inc(halves_lo, 1)
            t, par, _ = tile(4)
            if t is not None:
                dve.wait_ge(l_mm, done(t))
                dve.tensor_scalar(logits[:, t, :], bank[5 + par][0:P, 128:128 + NE], 1.0 / TEMP, None,
                                  ALU.mult).then_inc(logits_done, 1)

        for n in range(4):
            dve_update(n // 2, n % 2)
        with dve.Fori(2, NT // 2) as it, own.loop(it - 2, NT // 2 - 2, 2):
            dve_update(it, 0)
            dve_update(it, 1)
        for n in range(NT, NT + 4):
            dve_update(n // 2, n % 2)
        for t in range(NT):
            dve.wait_ge(logits_done, done(t))
            dve.max(top_logit[:, t, :], logits[:, t, :]).then_inc(dve_step, own.one())
        for t in range(NT):
            dve.wait_ge(dve_step, own.now())
            dve.max_index(top_expert[:, t, :], top_logit[:, t, :], logits[:, t, :]).then_inc(picked, 1)

        dve.wait_ge(picked, NT)
        dve.tensor_copy(picks[:], top_expert[:, :, 0:2]).then_inc(dve_step, own.one())
        dve.tensor_tensor(gap[:], top_logit[:, :, 1], top_logit[:, :, 0], ALU.subtract).then_inc(gap_done, 1)
        dve.wait_ge(dve_step, own.now())
        dve.wait_ge(made_dve, MADE_EXPERT_IDS)
        every = expert_id[:].unsqueeze(1).broadcast_to([P, NT, NE])
        for which, to in enumerate((first_pick, second_pick)):
            dve.tensor_tensor(to[:], every, picks[:, :, which:which + 1].broadcast_to([P, NT, NE]),
                              ALU.is_equal).then_inc(dve_step, own.one())
        dve.memset(earlier[:, 0, :], 0.0).then_inc(earlier_done, 1)
        dve.wait_ge(dve_step, own.now())
        dve.wait_ge(dve_step, own.now())
        dve.tensor_tensor(picked_any[:], first_pick[:], second_pick[:], ALU.add).then_inc(dve_step, own.one())
        dve.wait_ge(dve_step, own.now())
        for t in range(NT):
            dve.wait_ge(earlier_done, t + 1)
            dve.tensor_tensor(earlier[:, t + 1, :], earlier[:, t, :], picked_any[:, t, :], ALU.add).then_inc(earlier_done, 1)
        dve.wait_ge(gap_exp, 1)
        dve.tensor_scalar(gate2[:], gap[:], 1.0, None, ALU.add).then_inc(dve_step, own.one())
        dve.wait_ge(dve_step, own.now())
        dve.reciprocal(gate1[:], gate2[:]).then_inc(dve_step, own.one())
        dve.wait_ge(dve_step, own.now())
        dve.tensor_tensor(gate2[:], gate1[:], gap[:], ALU.mult).then_inc(dve_step, own.one())
        dve.wait_ge(rank_mm, 3)
        dve.tensor_scalar(padded_i32[:], bank[2][0:P, 0:NE], float(SLOTS - 1), None, ALU.add).then_inc(dve_step, own.one())
        dve.wait_ge(dve_step, own.now())
        dve.tensor_scalar(padded_i32[:], padded_i32[:], 6, 6, ALU.arith_shift_right, ALU.arith_shift_left).then_inc(dve_step, own.one())
        dve.wait_ge(dve_step, own.now())
        dve.tensor_copy(padded[:], padded_i32[:]).then_inc(dve_step, own.one())
        dve.wait_ge(dve_step, own.now())
        src_scan = padded
        shifts = (1, 2, 4, 8, 16, 32)
        for n, shift in enumerate(shifts):
            to = scan[n % 2]
            dve.wait_ge(dve_step, own.now())
            dve.tensor_copy(to[:, 0:shift], src_scan[:, 0:shift]).then_inc(dve_step, own.one())
            dve.tensor_tensor(to[:, shift:NE], src_scan[:, shift:NE], src_scan[:, 0:NE - shift], ALU.add).then_inc(dve_step, own.one())
            src_scan = to
        ends = src_scan
        dve.wait_ge(dve_step, own.now())
        dve.tensor_tensor(starts[:], ends[:], padded[:], ALU.subtract).then_inc(dve_step, own.one())
        dve.tensor_copy(expert_end[:], ends[:]).then_inc(dve_step, own.one())
        dve.wait_ge(dve_step, own.now())
        dve.tensor_scalar(expert_end[:], expert_end[:], 6, None, ALU.arith_shift_right).then_inc(tables_done, 1)
        dve.tensor_scalar(tile_expert_f[:], ends[:, NE - 1:NE], 1.0 / (SLOTS * BODY), (BODY + 1 - (BODY - 1) / 2) / BODY,
                          ALU.mult, ALU.add).then_inc(dve_step, own.one())
        dve.wait_ge(dve_step, own.now())
        dve.tensor_scalar(bodies[:, 0:1], tile_expert_f[:], float(STEPS), None, ALU.min).then_inc(dve_step, own.one())
        dve.wait_ge(dve_step, own.now())
        dve.tensor_scalar(bodies[:, 1:2], bodies[:, 0:1], 1.0, None, ALU.subtract).then_inc(tables_done, 1)
        dve.tensor_scalar(scan[0][:], ends[:], tile_start[:], None, ALU.is_le).then_inc(dve_step, own.one())
        dve.wait_ge(dve_step, own.now())
        dve.reduce_sum(tile_expert_f[:], scan[0][:], AX.X).then_inc(dve_step, own.one())
        dve.wait_ge(dve_step, own.now())
        dve.tensor_scalar(tile_expert[:], tile_expert_f[:], float(NE - 1), None, ALU.min).then_inc(tables_done, 1)
        dve.wait_ge(rank_mm, 2)
        for n in range(2):
            dve.tensor_tensor(slot_all[:, 5 * n:5 * (n + 1), :],
                              bank[n][0:P, 0:5 * NE].rearrange("p (t e) -> p t e", e=NE),
                              starts[:].unsqueeze(1).broadcast_to([P, 5, NE]), ALU.add).then_inc(dve_step, own.one())
        dve.wait_ge(dve_step, own.now())
        for which, pick in enumerate((first_pick, second_pick)):
            if which:
                dve.wait_ge(dve_step, own.now())
            dve.tensor_tensor(work[:], slot_all[:], pick[:], ALU.mult).then_inc(dve_step, own.one())
            dve.wait_ge(dve_step, own.now())
            dve.reduce_sum(slots_f[:, which, :], work[:], AX.X).then_inc(dve_step, own.one())
        dve.wait_ge(dve_step, own.now())
        dve.tensor_copy(slots[:], slots_f[:]).then_inc(dve_step, own.one())
        dve.wait_ge(dve_step, own.now())
        dve.tensor_scalar(slot_low[:], slots[:], 127, None, ALU.bitwise_and).then_inc(dve_step, own.one())
        dve.tensor_scalar(slot_high[:], slots[:], 7, None, ALU.arith_shift_right).then_inc(dve_step, own.one())
        dve.wait_ge(dve_step, own.now())
        dve.scalar_tensor_tensor(table_at[:], slot_low[:], float(PAIR_TILES), slot_high[:], ALU.mult, ALU.add).then_inc(tables_done, 1)
        dve.tensor_scalar(gates_up[:, 0, :], gate1[:], 1.0 / SHARED_SCALE, None, ALU.mult).then_inc(dve_step, own.one())
        dve.tensor_scalar(gates_up[:, 1, :], gate2[:], 1.0 / SHARED_SCALE, None, ALU.mult).then_inc(dve_step, own.one())
        dve.wait_ge(dve_step, own.now())
        dve.tensor_tensor(slot_all[:], first_pick[:], gates_up[:, 0, :].unsqueeze(2).broadcast_to([P, NT, NE]), ALU.mult).then_inc(dve_step, own.one())
        dve.tensor_tensor(work[:], second_pick[:], gates_up[:, 1, :].unsqueeze(2).broadcast_to([P, NT, NE]), ALU.mult).then_inc(dve_step, own.one())
        dve.wait_ge(dve_step, own.now())
        dve.tensor_tensor(work[:], work[:], slot_all[:], ALU.add).then_inc(combine_done, 1)
        dve.wait_ge(table_moved, 16 * (1 + UNSURE))
        dve.wait_ge(ws2_loaded, 48)
        dve.tensor_scalar(bs2_row[:], bs2_row[:], SHARED_SCALE, None, ALU.mult).then_inc(dve_step, own.one())
        dve.wait_ge(dve_step, own.now())
        for g, (lo, hi) in enumerate(GROUPS):
            width = (hi - lo) * PW
            for fb in range(SB):
                n = g * SB + fb
                dve.wait_ge(shared_act, n + 1)
                if g:
                    dve.wait_ge(shared_down, lo)
                dve.tensor_copy(shared_hT_hi[:, fb, 0:width], shared_h[fb % SH_RING][:, 0:width]).then_inc(dve_step, own.one())
                dve.wait_ge(dve_step, own.now())
                dve.tensor_tensor(shared_hT_lo[:, fb, 0:width], shared_h[fb % SH_RING][:, 0:width],
                                  shared_hT_hi[:, fb, 0:width].bitcast(F32), ALU.subtract).then_inc(shared_lo_done, 1)
                if n == SH_RING - 1:
                    dve.wait_ge(halves_hi, SPLIT["ws2"])
                    dve.tensor_tensor(ws2_lo[:], ws2_raw[:], ws2_hi[:].bitcast(F32), ALU.subtract).then_inc(halves_lo, 1)
            if hi == NT:
                dve.wait_ge(ffw_loaded, 96)
                for k in range(KD):
                    dve.tensor_scalar(wf1_g[:, k, :], wf1_raw[:, k, :], g_col[:, k:k + 1], None, ALU.mult).then_inc(wf1_g_done, 1)
                dve.wait_ge(halves_hi, SPLIT["wf1"])
                dve.tensor_tensor(wf1_lo[:], wf1_g[:], wf1_hi[:].bitcast(F32), ALU.subtract).then_inc(halves_lo, 1)
                dve.wait_ge(halves_hi, SPLIT["wf2"])
                dve.tensor_tensor(wf2_lo[:], wf2_raw[:], wf2_hi[:].bitcast(F32), ALU.subtract).then_inc(halves_lo, 1)
            for t in range(lo, hi):
                dve.wait_ge(shared_down, t + 1)
                dve.scalar_tensor_tensor(shared[:, t, :], bank[5 + t % 2][0:P, :], SHARED_SCALE, bs2_row[:],
                                         ALU.mult, ALU.add).then_inc(shared_done, 1)

        dve.wait_ge(bf1_mm, 2)
        dve.tensor_tensor(bf1_sb[:], bank[3][:, 0:2], bf1_raw[:], ALU.add).then_inc(bf1_done, 1)

        def expert_of(j):
            return dve.value_load(tile_expert_row[0:1, bass.ds(j, 1)], min_val=0, max_val=NE - 1)

        def copy_weights(j, n, expert):
            dve.wait_ge(experts_here, expert + 1)
            dve.wait_ge(down_mm, tile_freed(j, BODY))
            dve.tensor_copy(w_tile[n][:], w_ring[:, bass.ds(slot_of(expert), 1), :].rearrange("p a c -> p (a c)")).then_inc(w_copied, 1)

        def dve_tiles(it, last):
            for n in range(BODY):
                j = BODY * it + n
                par = n % 2
                more = not (last and n + W_AHEAD >= BODY)
                if more:
                    expert = expert_of(j + W_AHEAD)
                dve.wait_ge(up_mm, tile_done(j))
                dve.wait_ge(up_turned, tile_freed(j, 2))
                dve.tensor_copy(up[par][:], bank[2 + par][:, 0:128]).then_inc(up_copied, 1)
                if more:
                    copy_weights(j + W_AHEAD, (n + W_AHEAD) % BODY, expert)

        def dve_skip(it, copies):
            dve.wait_ge(up_copied, tile_done(BODY * it - 1))
            dve.sem_inc(up_copied, BODY)
            dve.wait_ge(w_copied, copied(BODY * it + W_AHEAD - 1))
            dve.sem_inc(w_copied, copies)

        dve.wait_ge(tile_expert_moved, 32)
        for j in range(W_AHEAD):
            copy_weights(j, j, expert_of(j))
        run = dve.value_load(bodies[0:1, 0:1], min_val=STEPS_MIN, max_val=STEPS)
        with dve.Fori(0, STEPS - 1) as it:
            with dve.If(it < run):
                dve_tiles(it, False)
            with dve.If(it >= run):
                dve_skip(it, BODY)
        with dve.If(run >= STEPS):
            dve_tiles(STEPS - 1, True)
        with dve.If(run < STEPS):
            dve_skip(STEPS - 1, BODY - W_AHEAD)
        def combine(t):
            par, hm = t % 2, hmoe[t % HM_RING]
            dve.wait_ge(eo_fetched[t % EO_RING], 32 * (t // EO_RING + 1))
            if t >= HM_RING:
                dve.wait_ge(hm_kept, t - HM_RING + 1)
            dve.scalar_tensor_tensor(hm[:], eo_first[t % EO_RING][:], gate1[:, t:t + 1], shared[:, t, :], ALU.mult,
                                     ALU.add).then_inc(dve_step, own.one())
            dve.wait_ge(dve_step, own.now())
            dve.scalar_tensor_tensor(hm[:], eo_second[t % EO_RING][:], gate2[:, t:t + 1], hm[:], ALU.mult,
                                     ALU.add).then_inc(hm_done, 1)
            dve.wait_ge(hm_done, t + 1)
            dve.bn_stats(hm_parts[par][:], hm[:]).then_inc(dve_step, own.one())
            dve.wait_ge(dve_step, own.now())
            dve.bn_aggr(hm_moments[par][:], hm_parts[par][:]).then_inc(hm_moments_done, 1)

        combine(0)
        for step in range(NT + 5):
            t, par = step, step % 2
            if t < NT:
                dve.wait_ge(hm_std_done, t + 1)
                dve.reciprocal(hm_rstd[par][:], hm_std[par][:]).then_inc(hm_rstd_done, 1)
                dve.wait_ge(hm_rstd_done, t + 1)
                if t >= 2:
                    dve.wait_ge(ff_turned, t - 1)
                dve.tensor_scalar(ff_in[par][:], hmoe[t % HM_RING][:], hm_moments[par][:, 0:1], hm_rstd[par][:],
                                  ALU.subtract, ALU.mult).then_inc(ff_in_done, 1)
            if 3 <= t < NT + 3:
                item = t - 3
                pair, half = item // 2, item % 2
                where = slice(2 * (pair % 2), 2 * (pair % 2) + 2)
                act_rows = ff_h[half][:].rearrange("p (t c) -> p t c", t=2)
                dve.wait_ge(ff_act, item + 1)
                if pair >= 2:
                    dve.wait_ge(ff_down, 2 * (pair - 1))
                dve.tensor_copy(ff_hT_hi[:, half, where, :], act_rows).then_inc(dve_step, own.one())
                dve.wait_ge(dve_step, own.now())
                dve.tensor_tensor(ff_hT_lo[:, half, where, :], act_rows, ff_hT_hi[:, half, where, :].bitcast(F32),
                                  ALU.subtract).then_inc(ff_h_lo_done, 1)
            if t >= 5:
                u = t - 5
                dve.wait_ge(ff_down, u + 1)
                dve.wait_ge(hm_kept, u + 1)
                if u >= 2:
                    dve.wait_ge(result_stored[u % 2], 32 * (u // 2))
                dve.tensor_tensor(result[u % 2][:], bank[4 + u % 2][0:P, :], x_sb[:, u, :], ALU.add).then_inc(result_done, 1)
            if t + 1 < NT:
                combine(t + 1)
            if t < NT:
                dve.wait_ge(ffT_hi_done, t + 1)
                dve.tensor_tensor(ffT_lo[:, :, t % 4, 0:P], turned(par)[:, :, 0:P],
                                  ffT_hi[:, :, t % 4, 0:P].bitcast(F32), ALU.subtract).then_inc(ffT_lo_done, 1)

    @block.tensor
    def _(pe):
        for signal in (xn_turned, t_mm, q_mm, k_mm, v_mm, q_turned, g_mm, y_mm, h_turned, r_mm, l_mm):
            pe.sem_inc(signal, AHEAD)
        for signal in (pair_turned, up_mm, up_turned, down_mm):
            pe.sem_inc(signal, BODY)
        pe.sem_inc(chunk_mm, CHUNK_AHEAD)

        def turn(tile, to, signal):
            for k in range(KD):
                last = pe.transpose(turned(to)[:, k, 0:P], tile[:, 128 * k:128 * (k + 1)], ident[0:P, 0:P])
            last.then_inc(signal, 1)

        def turn_x(par, item):
            pe.wait_ge(xn_done, done(item))
            pe.wait_ge(xnt_lo_done, freed(item))
            turn(xn[par], 6 + par, xn_turned)

        def product(to, terms, signal):
            for i, (a, b) in enumerate(terms):
                last = pe.matmul(to, a, b, start=(i == 0), stop=(i == len(terms) - 1))
            last.then_inc(signal, 1)

        def split_terms(a_hi, a_lo, b_hi, b_lo, blocks):
            terms = []
            for k in range(blocks):
                terms += [(a_hi(k), b_hi(k)), (a_hi(k), b_lo(k)), (a_lo(k), b_hi(k))]
            return terms

        pe.wait_ge(made, MADE_IDENT)
        pe.wait_ge(halves_lo, SPLIT["u"])

        def rank_products(it, n):
            tile = tiles_of(it, n)
            t, par, _ = tile(0)
            if t is not None:
                turn_x(par, t)
            t, par, _ = tile(1)
            if t is not None:
                pe.wait_ge(xnt_lo_done, done(t))
                pe.wait_ge(t_done, freed(t))
                product(bank[4 + par][0:P, 0:2 * RANK],
                        [(half[par][:, k, 0:P], u_hl[:, k, :]) for k in range(KD) for half in (xnt_hi, xnt_lo)], t_mm)

        rank_products(0, 0)
        rank_products(0, 1)
        with pe.Fori(1, NT // 2) as it:
            rank_products(it, 0)
            rank_products(it, 1)
        rank_products(NT // 2, 0)
        pe.wait_ge(made, MADE_ZEROS)
        agg = [bank[b][:, 0:(hi - lo) * PW] for b, (lo, hi) in enumerate(GROUPS)]
        for b, (lo, hi) in enumerate(GROUPS):
            last = pe.matmul(agg[b], zero_w[:], onehot[0][:, lo * PW:hi * PW], start=True, stop=False,
                             skip_group_check=True)
        last.then_inc(agg_opened, 1)

        def sum_edges(batch, half, first, last_c):
            pe.wait_ge(rows_lo_done, done(batch))
            for c in range(first, last_c):
                pe.wait_ge(onehot_done, batch * BC + c + 1)
                for b, (lo, hi) in enumerate(GROUPS):
                    last = pe.matmul(agg[b], rows_hl[half][:, c, :],
                                     onehot[(half * BC + c) % OH_RING][:, lo * PW:hi * PW],
                                     start=False, stop=False, skip_group_check=True)
                last.then_inc(chunk_mm, 1)

        pe.wait_ge(halves_lo, SPLIT["wqkv"])
        pe.wait_ge(t_done, done(NT - 1))

        def project(t, par, part, first, end):
            signal, readers = ((q_mm, (q_sub_done,)), (k_mm, (k_copied,)), (v_mm, (v_copied,)))[part]
            if first == 0 and end > 0:
                for reader in readers:
                    pe.wait_ge(reader, freed(t, 1))
            cols = slice(D * part, D * (part + 1))
            terms = split_terms(lambda k: xnt_hi[par][:, k, 0:P], lambda k: xnt_lo[par][:, k, 0:P],
                                lambda k: wqkv_hi[:, k, cols], lambda k: wqkv_lo[:, k, cols], KD)
            for i in range(first, end):
                last = pe.matmul(bank[3 + part][0:P, :], terms[i][0], terms[i][1], start=(i == 0), stop=(i == len(terms) - 1),
                                 skip_group_check=True)
                if i == len(terms) - 1:
                    last.then_inc(signal, 1)

        def pe_edge_tiles(it, final=False):
            for par in range(2):
                t = 2 * it + par
                pe.wait_ge(xnt_lo_done, done(NT + t))
                for c in range(2 * BC):
                    sum_edges(2 * t + c // BC, c // BC, c % BC, c % BC + 1)
                    begin, end = 3 * 3 * KD * c // (2 * BC), 3 * 3 * KD * (c + 1) // (2 * BC)
                    for part in range(3):
                        at = 3 * KD * part
                        lo, hi = max(begin - at, 0), min(end - at, 3 * KD)
                        if lo < hi:
                            project(t, par, part, lo, hi)
                    if c == BC - 1 and not (final and par):
                        turn_x(1 - par, NT + t + 1)

        turn_x(0, NT)
        with pe.Fori(0, NT // 2 - 1) as it:
            pe_edge_tiles(it)
        pe_edge_tiles(NT // 2 - 1, final=True)
        for b, (lo, hi) in enumerate(GROUPS):
            last = pe.matmul(agg[b], zero_w[:], onehot[0][:, lo * PW:hi * PW], start=False, stop=True,
                             skip_group_check=True)
        last.then_inc(agg_closed, 1)
        pe.wait_ge(k_top_done, done(NT - 1))
        pe.wait_ge(xnt_lo_done, done(2 * NT - 1))
        turn(k_top, 6, k_top_turned)
        pe.wait_ge(k_top_wide_done, 1)
        for k in range(PAIRS):
            last = pe.transpose(bank[7][0:P, 128 * k:128 * (k + 1)], k_top_wide[:, k, :], ident[:])
        last.then_inc(k_top_back, 1)
        pe.wait_ge(v_copied, done(NT - 1))
        pe.wait_ge(q_sub_done, done(NT - 1))
        for pair in range(PAIRS):
            at = 132 * (pair % 2)
            for t in range(NT):
                pe.wait_ge(k_exp_done, t + 1)
                last = pe.matmul(bank[3 + pair // 2][:, at:at + 130], k_sb[:, t, 128 * pair:128 * (pair + 1)],
                                 v_sb[:, t, pair, :], start=(t == 0), stop=(t == NT - 1))
            last.then_inc(ctx_mm, 1)
        pe.wait_ge(ctx_done, 2 * PAIRS)
        for pair in range(PAIRS):
            last = pe.transpose(bank[5][:, 128 * pair:128 * (pair + 1)], ctx[:, pair, :], ident[:])
        last.then_inc(ctx_turned, 1)
        pe.wait_ge(ctxT_lo_done, 1)
        pe.wait_ge(halves_lo, SPLIT["wout"])
        for pair in range(PAIRS):
            product(bank[(3, 4, 6, 7)[pair]][:, :],
                    [(ctxT_hi[:, pair, :], wout_hi[:, pair, :]), (ctxT_hi[:, pair, :], wout_lo[:, pair, :]),
                     (ctxT_lo[:, pair, :], wout_hi[:, pair, :])], m_mm)
        pe.wait_ge(m_lo_done, PAIRS)
        pe.wait_ge(zeroed, ZEROED_HT)
        pe.wait_ge(halves_lo, SPLIT["vt"])
        pe.wait_ge(halves_lo, SPLIT["bias"])
        pe.wait_ge(agg_copied, 3)
        def pe_update(it, n):
            tile = tiles_of(it, n)
            t, par, _ = tile(3)
            if t is not None:
                pe.wait_ge(h_done, done(t))
                if tile(1)[0] is not None:
                    pe.wait_ge(qT_lo_done, done(tile(1)[0]))
                turn(h_tile[par], 7 * par, h_turned)
            t, par, _ = tile(1)
            if t is not None:
                pe.wait_ge(agg_lo_done, done(t))
                pe.wait_ge(g_relu_done, freed(t))
                product(bank[3 + par][0:P, :], [(one_row[:, 0:P], bias_hi[:]), (one_row[:, 0:P], bias_lo[:]),
                                                (agg_hi[par][:, 0:P], vt2_hi[:]), (agg_hi[par][:, 0:P], vt2_lo[:]),
                                                (agg_lo[par][:, 0:P], vt2_hi[:])], g_mm)
            t, par, _ = tile(4)
            if t is not None:
                pe.wait_ge(rT_done, done(t))
                product(bank[5 + par][0:P, 128:128 + NE], [(rT[par][:, 0:P], codebook2[:])], l_mm)
            t, par, _ = tile(0)
            if t is not None:
                pe.wait_ge(q_tile_done, done(t))
                if tile(4)[0] is not None:
                    pe.wait_ge(hT_lo_done, done(tile(4)[0]))
                turn(q_tile[par], 7 * par, q_turned)
            t, par, _ = tile(1)
            if t is not None:
                pe.wait_ge(qT_lo_done, done(t))
                pe.wait_ge(y_sum_done, freed(t))
                product(bank[1 + par][0:P, :],
                        split_terms(lambda k: qT_hi[par][:, k, 0:P], lambda k: qT_lo[par][:, k, 0:P],
                                    lambda k: m_hi[:, k, :], lambda k: m_lo[:, k, :], PAIRS), y_mm)
            t, par, _ = tile(3)
            if t is not None:
                pe.wait_ge(logits_done, freed(t))
                pe.wait_ge(hT_lo_done, done(t))
                product(bank[5 + par][:, 0:PW],
                        [(wr_hl[:, k, :], half[:, k, t, :]) for k in range(KD) for half in (hT_hi, hT_lo)], r_mm)

        update_steps(pe, pe_update)

        def shared_up_products(g, first=0, end=SB):
            lo, hi = GROUPS[g]
            for fb in range(first, end):
                n = g * SB + fb
                if n >= 2:
                    pe.wait_ge(shared_act, n - 1)
                cols = slice(128 * fb, 128 * (fb + 1))
                product(bank[3 + fb % 2][:, 0:(hi - lo) * PW],
                        split_terms(lambda k: ws1_hi[:, k, cols], lambda k: ws1_lo[:, k, cols],
                                    lambda k: hT_hi[:, k, lo:hi, :].rearrange("p t c -> p (t c)"),
                                    lambda k: hT_lo[:, k, lo:hi, :].rearrange("p t c -> p (t c)"), KD), shared_up)

        def shared_down_products(g):
            lo, hi = GROUPS[g]
            pe.wait_ge(shared_lo_done, (g + 1) * SB)
            for t in range(lo, hi):
                if t >= 2:
                    pe.wait_ge(shared_done, t - 1)
                cols = slice((t - lo) * PW, (t - lo) * PW + P)
                product(bank[5 + t % 2][0:P, :],
                        split_terms(lambda k: shared_hT_hi[:, k, cols], lambda k: shared_hT_lo[:, k, cols],
                                    lambda k: ws2_hi[:, k, :], lambda k: ws2_lo[:, k, :], SB)
                        + [(combineT[:, t, :], b2_sb[:])], shared_down)

        pe.wait_ge(halves_lo, SPLIT["ws1"])
        shared_up_products(0, 0, 2)
        pe.wait_ge(made, MADE_BEFORE)
        pe.wait_ge(earlier_done, NT + 1)
        for n in range(2):
            tiles_ = slice(5 * n, 5 * (n + 1))
            product(bank[n][0:P, 0:5 * NE], [(before[:], picked_any[:, tiles_, :].rearrange("p t e -> p (t e)")),
                                             (ones[:], earlier[:, tiles_, :].rearrange("p t e -> p (t e)"))], rank_mm)
        product(bank[2][0:P, 0:NE], [(ones[:], earlier[:, NT, :])], rank_mm)
        shared_up_products(0, 2)
        pe.wait_ge(combine_done, 1)
        for g, (lo, hi) in enumerate(GROUPS):
            for t in range(lo, hi):
                pe.transpose(bank[g][0:NE, 128 * (t - lo):128 * (t - lo) + P], work[:, t, :], ident[0:P, 0:P]).then_inc(combine_turned, 1)
        pe.wait_ge(halves_lo, SPLIT["ws2"])
        pe.wait_ge(ws2_loaded, 48)
        pe.wait_ge(combineT_done, len(GROUPS))
        shared_down_products(0)
        for g in range(1, len(GROUPS)):
            shared_up_products(g)
            shared_down_products(g)
        pe.wait_ge(ffw_loaded, 96)
        for half in range(2):
            product(bank[3][:, half:half + 1],
                    [(wf1_raw[:, k, 128 * half:128 * (half + 1)], b_col[:, k:k + 1]) for k in range(KD)], bf1_mm)
        pe.wait_ge(shared_done, NT)
        pe.wait_ge(bf1_done, 1)

        def turn_pair(q, v, turn):
            pe.wait_ge(pair_fetched[v], 16 * (turn + 1))
            pe.wait_ge(pairT_done, tile_freed(q, 1 if v == 0 else 2))
            for k in range(KD):
                last = pe.transpose(bank[v % 2][:, 128 * k:128 * (k + 1)], pair_rows[v][:, 128 * k:128 * (k + 1)], ident[:])
            last.then_inc(pair_turned, 1)

        def up_products(it, n):
            j = BODY * it + n
            par = n % 2
            if n % 2 == 0:
                pe.wait_ge(pairT_done, tile_done(BODY // 2 * it + n // 2))
            pe.wait_ge(w_copied, copied(j))
            pe.wait_ge(up_copied, tile_freed(j, 2))
            for k in range(KD):
                for half in range(2):
                    last = pe.matmul(bank[2 + par][SLOTS * half:SLOTS * (half + 1), 0:128],
                                     pair_rowsT[n // 2][:, k, SLOTS * par:SLOTS * (par + 1)],
                                     w_tile[n][:, k * DFF + 128 * half:k * DFF + 128 * (half + 1)],
                                     start=(k == 0), stop=(k == KD - 1), skip_group_check=True)
            last.then_inc(up_mm, 1)

        def up_transpose(j, par):
            pe.wait_ge(up_copied, tile_done(j))
            pe.wait_ge(up_act, tile_freed(j, 2))
            pe.transpose(bank[4 + par][:, 0:128], up[par][:], ident[:]).then_inc(up_turned, 1)

        def down_products(j, n, turn):
            par = n % 2
            pe.wait_ge(up_act, tile_done(j))
            pe.wait_ge(down_copied, turn)
            for k in range(2):
                for half in range(2):
                    last = pe.matmul(bank[6 + par][SLOTS * half:SLOTS * (half + 1), 0:D // 2], upT[par][:, k, :],
                                     w_tile[n][:, W1_COLS + k * D + half * (D // 2):W1_COLS + k * D + (half + 1) * (D // 2)],
                                     start=(k == 0), stop=(k == 1), skip_group_check=True)
            last.then_inc(down_mm, 1)

        def pe_step(it, first=False, last=False):
            for n in range(BODY):
                j = BODY * it + n
                up_products(it, n)
                if n % 2 and not (last and n == BODY - 1):
                    v = (n + 1) // 2
                    turn_pair(3 * it + v, v % 3, it + v // 3)
                if not (first and n < 1):
                    up_transpose(j - 1, (n - 1) % 2)
                if not (first and n < 2):
                    down_products(j - 2, (n - 2) % BODY, j - 3 if not (first and n < 4) else 0)

        def pe_skip(it):
            pe.wait_ge(up_turned, tile_done(BODY * it - 2))
            pe.sem_inc(up_turned, BODY)
            pe.wait_ge(down_mm, tile_done(BODY * it - 3))
            pe.sem_inc(down_mm, BODY)

        turn_pair(0, 0, 0)
        pe.wait_ge(tables_done, TABLE_BODIES)
        run = pe.value_load(bodies[0:1, 0:1], min_val=STEPS_MIN, max_val=STEPS)
        pe_step(0, first=True)
        with pe.Fori(1, STEPS - 1) as it:
            with pe.If(it < run):
                pe_step(it)
            with pe.If(it >= run):
                pe_skip(it)
        with pe.If(run >= STEPS):
            pe_step(STEPS - 1, last=True)
            up_transpose(TILES - 1, 1)
            for j in (TILES - 2, TILES - 1):
                down_products(j, j % BODY, j - 1)
        with pe.If(run < STEPS):
            pe_skip(STEPS - 1)
        pe.wait_ge(halves_lo, SPLIT["wf1"])
        pe.wait_ge(halves_lo, SPLIT["wf2"])
        pe.wait_ge(zeroed, ZEROED_FFT)
        pe.wait_ge(pairT_done, tile_done(TILES // 2 - 1))
        pe.wait_ge(down_copied, TILES)
        pe.wait_ge(up_copied, tile_done(TILES - 1))
        pe.wait_ge(up_act, tile_done(TILES - 1))
        for step in range(NT + 4):
            t = step
            if t < NT:
                pe.wait_ge(ff_in_done, t + 1)
                if t >= 2:
                    pe.wait_ge(ffT_lo_done, t - 1)
                turn(ff_in[t % 2], t % 2, ff_turned)
            if 2 <= t < NT + 2:
                item = t - 2
                pair, half = item // 2, item % 2
                pe.wait_ge(ffT_lo_done, 2 * (pair + 1))
                if pair >= 1:
                    pe.wait_ge(ff_act, item - 1)
                cols = slice(128 * half, 128 * (half + 1))
                where = slice(2 * (pair % 2), 2 * (pair % 2) + 2)
                product(bank[2 + half][:, 0:2 * PW],
                        split_terms(lambda k: wf1_hi[:, k, cols], lambda k: wf1_lo[:, k, cols],
                                    lambda k: ffT_hi[:, k, where, :].rearrange("p t c -> p (t c)"),
                                    lambda k: ffT_lo[:, k, where, :].rearrange("p t c -> p (t c)"), KD), ff_up)
            if t >= 4:
                u = t - 4
                pe.wait_ge(ff_h_lo_done, 2 * (u // 2 + 1))
                if u >= 2:
                    pe.wait_ge(result_done, u - 1)
                product(bank[4 + u % 2][0:P, :],
                        split_terms(lambda k: ff_hT_hi[:, k, u % 4, 0:P], lambda k: ff_hT_lo[:, k, u % 4, 0:P],
                                    lambda k: wf2_hi[:, k, :], lambda k: wf2_lo[:, k, :], 2), ff_down)

    block.__exit__(None, None, None)


_ORDER = ["x", "src", "dst", "edge_weight", "u", "s", "vt", "gnn_bias", "wqkv_t", "wout_t", "bout", "ln1_g", "ln1_b",
          "wr", "codebook_t", "experts", "b2", "ws1", "bs1_cols", "ws2", "bs2", "ffln_g_cols", "ffln_b_cols", "wf1",
          "bf1_cols", "wf2", "bf2"]


def laid_out(i):
    import numpy as np

    def col(v):
        return v.reshape(-1, 128).T

    w1, w2, b1 = i["L0_ffn_W1"], i["L0_ffn_W2"], i["L0_ffn_b1"]
    experts = np.concatenate([
        w1.reshape(NE, KD, 128, DFF).transpose(0, 2, 1, 3).reshape(NE, 128, KD * DFF),
        w2.reshape(NE, 2, 128, D).transpose(0, 2, 1, 3).reshape(NE, 128, 2 * D),
        b1.reshape(NE, 2, 128).transpose(0, 2, 1)], axis=2)
    row = lambda v: v.reshape(1, -1)
    return {
        "x": i["x"], "src": i["src"].reshape(P, EC), "dst": i["dst"].reshape(P, EC),
        "edge_weight": i["edge_weight"].reshape(P, EC), "u": i["L0_gnn_U"], "s": row(i["L0_gnn_s"]),
        "vt": i["L0_gnn_Vt"], "gnn_bias": row(i["L0_gnn_bias"]), "wqkv_t": i["L0_mix_Wqkv"].T,
        "wout_t": i["L0_mix_Wout"].T, "bout": row(i["L0_mix_bout"]), "ln1_g": row(i["L0_ffn_ln1_g"]),
        "ln1_b": row(i["L0_ffn_ln1_b"]), "wr": i["L0_ffn_Wr"], "codebook_t": i["L0_ffn_codebook"].T,
        "experts": experts, "b2": i["L0_ffn_b2"], "ws1": i["L0_ffn_Ws1"], "bs1_cols": col(i["L0_ffn_bs1"]),
        "ws2": i["L0_ffn_Ws2"], "bs2": row(i["L0_ffn_bs2"]), "ffln_g_cols": col(i["L0_ffn_ffln_g"]),
        "ffln_b_cols": col(i["L0_ffn_ffln_b"]), "wf1": i["L0_ffn_Wf1"], "bf1_cols": col(i["L0_ffn_bf1"]),
        "wf2": i["L0_ffn_Wf2"], "bf2": row(i["L0_ffn_bf2"]),
    }


def kernel(**inputs):
    import numpy as np
    import concourse.bacc as bacc
    from concourse.bass_utils import run_bass_kernel_spmd

    nc = bacc.Bacc("TRN2", target_bir_lowering=False, num_devices=1)
    arrays, args = {}, []
    laid = laid_out({k: np.asarray(v) for k, v in inputs.items()})
    for name in _ORDER:
        a = np.ascontiguousarray(laid[name])
        arrays[f"in_{name}"] = a
        args.append(nc.dram_tensor(f"in_{name}", a.shape, mybir.dt.from_np(a.dtype), kind="ExternalInput").ap())
    args.append(nc.dram_tensor("result", (N, D), F32, kind="ExternalOutput").ap())
    gps_layer(nc, *args)
    r = run_bass_kernel_spmd(nc, [arrays], core_ids=[0])
    return r.results[0]["result"]
```
